# Optimizing a Trainium2 kernel written in Bass

```python
import numpy as np
import jax
import jax.numpy as jnp

def _softmax(x, axis=-1):
    return jax.nn.softmax(x, axis=axis)

def _gelu(x):
    return jax.nn.gelu(x, approximate=True)

def _silu(x):
    return jax.nn.silu(x)

def _sigmoid(x):
    return jax.nn.sigmoid(x)

def _layernorm(x, axis=-1, eps=1e-05):
    m = jnp.mean(x, axis=axis, keepdims=True)
    v = jnp.var(x, axis=axis, keepdims=True)
    return (x - m) / jnp.sqrt(v + eps)

def _scatter_add(tgt, idx, src, axis=0):
    return tgt.at[idx].add(src)

def _segment_sum(src, seg, n):
    return jax.ops.segment_sum(src, seg, n)
kernel_name = 'mk_xattn_ffn_d2_seqx_r2_0f67f0'

def setup_inputs(seed: int=0):
    np.random.seed(seed)
    _w = jnp.asarray

    def _rec_inputs():
        import jax
        import jax.numpy as jnp
        _rk = jax.random.key(seed)
        x = -0.000125 + 0.9999 * jax.random.normal(jax.random.fold_in(_rk, 1), (16, 256, 512), jnp.float32)
        _lenS = 256 - jax.random.randint(jax.random.fold_in(_rk, 7), (16,), 0, max(1, 256 // 4) + 1, jnp.int32)
        _lenS2 = 256 - jax.random.randint(jax.random.fold_in(_rk, 8), (16,), 0, max(1, 256 // 4) + 1, jnp.int32)
        _ctx_1024P = jax.random.normal(jax.random.fold_in(_rk, 11), (16, 16, 512), jnp.float32)
        _ctx_1024c = jax.random.dirichlet(jax.random.fold_in(_rk, 511), 0.3 * jnp.ones((16,), jnp.float32), (16, 256))
        _ctx_1024t = jnp.einsum('bsk,bkd->bsd', _ctx_1024c, _ctx_1024P)
        _ctx_1024t = _ctx_1024t * jax.lax.rsqrt(jnp.mean(jnp.square(_ctx_1024t)) + 1e-12) * 0.953939
        ctx_1024 = -0.000188977 + 0.999793 * (_ctx_1024t + 0.3 * jax.random.normal(jax.random.fold_in(_rk, 611), (16, 256, 512), jnp.float32))
        fside_1xSxS2_0 = 0.000675642 + 1.00031 * jax.random.normal(jax.random.fold_in(_rk, 12), (1, 256, 256), jnp.float32)
        return (x, ctx_1024, fside_1xSxS2_0)
    x, ctx_1024, fside_1xSxS2_0 = _rec_inputs()

    def _L0_xattn_setup():
        import jax, jax.numpy as jnp
        import numpy as np
        HEADS = 16
        DIM_HEAD = 64
        INNER = HEADS * DIM_HEAD
        QUERY_DIM = 512
        CONTEXT_DIM = 512
        TEXT_LEN = 77
        IMG_SCALE = 1.0
        SCALE = DIM_HEAD ** (-0.5)

        def _attend(q, k, v):
            sim = jnp.einsum('bihd,bjhd->bhij', q, k) * SCALE
            attn = jax.nn.softmax(sim, axis=-1)
            out = jnp.einsum('bhij,bjhd->bihd', attn, v)
            B, N, H, D = out.shape
            return out.reshape(B, N, H * D)
        key = jax.random.key(seed)
        ks = jax.random.split(key, 10)
        B, N, Lc = (16, 1024, 333)
        x = jax.random.normal(ks[0], (B, N, QUERY_DIM), dtype=jnp.float32)
        context = jax.random.normal(ks[1], (B, Lc, CONTEXT_DIM), dtype=jnp.float32)

        def w(k, din, dout):
            return jax.random.normal(k, (din, dout), dtype=jnp.float32) * din ** (-0.5)
        Wq = w(ks[2], QUERY_DIM, INNER)
        Wk = w(ks[3], CONTEXT_DIM, INNER)
        Wv = w(ks[4], CONTEXT_DIM, INNER)
        Wk_ip = w(ks[5], CONTEXT_DIM, INNER)
        Wv_ip = w(ks[6], CONTEXT_DIM, INNER)
        Wo = w(ks[7], INNER, QUERY_DIM)
        bo = jnp.zeros((QUERY_DIM,), dtype=jnp.float32)
        return {'x': x, 'context': context, 'Wq': Wq, 'Wk': Wk, 'Wv': Wv, 'Wk_ip': Wk_ip, 'Wv_ip': Wv_ip, 'Wo': Wo, 'bo': bo}
    _L0_xattn_all = _L0_xattn_setup()
    _L0_xattn_in = {k: v for k, v in _L0_xattn_all.items() if k in ('Wq', 'Wk', 'Wv', 'Wk_ip', 'Wv_ip', 'Wo', 'bo')}
    del _L0_xattn_all

    def _L0_ffn_setup():
        import jax, jax.numpy as jnp
        import numpy as np
        BLOCK = 32
        W_BITS = 4
        ACT_BITS = 16

        def act_qdq(x):
            qmax = 2.0 ** (ACT_BITS - 1) - 1.0
            scale = jnp.maximum(jnp.max(jnp.abs(x)) / qmax, 1e-12)
            return jnp.clip(jnp.round(x / scale), -qmax - 1.0, qmax) * scale

        def fixed_qdq_u16(x):
            scale = 1.0 / 65536.0
            return jnp.clip(jnp.round(x / scale), 0.0, 65535.0) * scale

        def lpbq_dequant(w):
            O, I = w.shape
            qmax = 2.0 ** (W_BITS - 1) - 1.0
            wb = w.reshape(O, I // BLOCK, BLOCK)
            s = jnp.maximum(jnp.max(jnp.abs(wb), axis=-1, keepdims=True) / qmax, 1e-12)
            wq = jnp.clip(jnp.round(wb / s), -qmax - 1.0, qmax) * s
            return wq.reshape(O, I)
        key = jax.random.key(seed)
        k1, k2, k3, k4 = jax.random.split(key, 4)
        B, S, H, I = (2, 2048, 512, 1536)
        x = jax.random.normal(k1, (B, S, H), jnp.float32)
        w_gate = jax.random.normal(k2, (I, H), jnp.float32) * 0.02
        w_up = jax.random.normal(k3, (I, H), jnp.float32) * 0.02
        w_down = jax.random.normal(k4, (H, I), jnp.float32) * 0.02
        return {'x': x, 'w_gate': w_gate, 'w_up': w_up, 'w_down': w_down}
    _L0_ffn_all = _L0_ffn_setup()
    _L0_ffn_in = {k: v for k, v in _L0_ffn_all.items() if k in ('w_gate', 'w_up', 'w_down')}
    del _L0_ffn_all

    def _L1_xattn_setup():
        import jax, jax.numpy as jnp
        import numpy as np
        import math
        D = 512
        B, S = (8, 1024)

        def _proj(x, W1, b1, W2, b2):
            h = jnp.einsum('bsd,od->bso', x, W1) + b1
            return jnp.einsum('bsd,od->bso', h, W2) + b2
        key = jax.random.key(seed)
        ks = jax.random.split(key, 8)
        q = jax.random.normal(ks[0], (B, S, D), dtype=jnp.float32)
        k = jax.random.normal(ks[1], (B, S, D), dtype=jnp.float32)
        v1 = jax.random.normal(ks[2], (B, S, D), dtype=jnp.float32)
        mask = jax.random.normal(ks[3], (1, S, S), dtype=jnp.float32)
        lim = 1.0 / math.sqrt(D)
        W1 = jax.random.uniform(ks[4], (D, D), jnp.float32, -lim, lim)
        b1 = jax.random.uniform(ks[5], (D,), jnp.float32, -lim, lim)
        W2 = jax.random.uniform(ks[6], (D, D), jnp.float32, -lim, lim)
        b2 = jax.random.uniform(ks[7], (D,), jnp.float32, -lim, lim)
        return {'q': q, 'k': k, 'v1': v1, 'mask': mask, 'W1': W1, 'b1': b1, 'W2': W2, 'b2': b2}
    _L1_xattn_all = _L1_xattn_setup()
    _L1_xattn_in = {k: v for k, v in _L1_xattn_all.items() if k in ('W1', 'b1', 'W2', 'b2')}
    del _L1_xattn_all

    def _L1_ffn_setup():
        import jax, jax.numpy as jnp
        import numpy as np
        B, S, D, H = (8, 512, 512, 2048)
        E, R = (3, 8)
        SCALING = 1.0 / R

        def _mole(x, W, b, A, Bm, Rw):
            gates = jax.nn.softmax(jnp.einsum('bsd,de->bse', x, Rw), axis=-1)
            base = jnp.einsum('bsd,dh->bsh', x, W) + b
            z = jnp.einsum('bsd,edr->ebsr', x, A)
            zg = z * jnp.transpose(gates, (2, 0, 1))[..., None]
            lora = jnp.einsum('ebsr,erh->bsh', zg, Bm)
            return base + SCALING * lora
        key = jax.random.key(seed)
        ks = jax.random.split(key, 12)
        s = lambda k, shape, scale: jax.random.normal(k, shape, dtype=jnp.float32) * scale
        return {'x': s(ks[0], (B, S, D), 1.0), 'W1': s(ks[1], (D, H), D ** (-0.5)), 'b1': jnp.zeros((H,), jnp.float32), 'A1': s(ks[2], (E, D, R), D ** (-0.5)), 'B1': s(ks[3], (E, R, H), 0.0) + s(ks[4], (E, R, H), R ** (-0.5)), 'R1': s(ks[5], (D, E), D ** (-0.5)), 'W2': s(ks[6], (H, D), H ** (-0.5)), 'b2': jnp.zeros((D,), jnp.float32), 'A2': s(ks[7], (E, H, R), H ** (-0.5)), 'B2': s(ks[8], (E, R, D), R ** (-0.5)), 'R2': s(ks[9], (H, E), H ** (-0.5))}
    _L1_ffn_all = _L1_ffn_setup()
    _L1_ffn_in = {k: v for k, v in _L1_ffn_all.items() if k in ('W1', 'b1', 'A1', 'B1', 'R1', 'W2', 'b2', 'A2', 'B2', 'R2')}
    del _L1_ffn_all
    return {'x': x, 'ctx_1024': ctx_1024, 'fside_1xSxS2_0': fside_1xSxS2_0, 'L0_xattn_Wq': _L0_xattn_in['Wq'], 'L0_xattn_Wk': _L0_xattn_in['Wk'], 'L0_xattn_Wv': _L0_xattn_in['Wv'], 'L0_xattn_Wk_ip': _L0_xattn_in['Wk_ip'], 'L0_xattn_Wv_ip': _L0_xattn_in['Wv_ip'], 'L0_xattn_Wo': _L0_xattn_in['Wo'], 'L0_xattn_bo': _L0_xattn_in['bo'], 'L0_ffn_w_gate': _L0_ffn_in['w_gate'], 'L0_ffn_w_up': _L0_ffn_in['w_up'], 'L0_ffn_w_down': _L0_ffn_in['w_down'], 'L1_xattn_W1': _L1_xattn_in['W1'], 'L1_xattn_b1': _L1_xattn_in['b1'], 'L1_xattn_W2': _L1_xattn_in['W2'], 'L1_xattn_b2': _L1_xattn_in['b2'], 'L1_ffn_W1': _L1_ffn_in['W1'], 'L1_ffn_b1': _L1_ffn_in['b1'], 'L1_ffn_A1': _L1_ffn_in['A1'], 'L1_ffn_B1': _L1_ffn_in['B1'], 'L1_ffn_R1': _L1_ffn_in['R1'], 'L1_ffn_W2': _L1_ffn_in['W2'], 'L1_ffn_b2': _L1_ffn_in['b2'], 'L1_ffn_A2': _L1_ffn_in['A2'], 'L1_ffn_B2': _L1_ffn_in['B2'], 'L1_ffn_R2': _L1_ffn_in['R2']}

def reference(x, ctx_1024, fside_1xSxS2_0, L0_xattn_Wq, L0_xattn_Wk, L0_xattn_Wv, L0_xattn_Wk_ip, L0_xattn_Wv_ip, L0_xattn_Wo, L0_xattn_bo, L0_ffn_w_gate, L0_ffn_w_up, L0_ffn_w_down, L1_xattn_W1, L1_xattn_b1, L1_xattn_W2, L1_xattn_b2, L1_ffn_W1, L1_ffn_b1, L1_ffn_A1, L1_ffn_B1, L1_ffn_R1, L1_ffn_W2, L1_ffn_b2, L1_ffn_A2, L1_ffn_B2, L1_ffn_R2):
    import jax
    import jax.numpy as jnp

    def _L0_xattn_ref(x, context, Wq, Wk, Wv, Wk_ip, Wv_ip, Wo, bo):
        import jax, jax.numpy as jnp
        import numpy as np
        HEADS = 16
        DIM_HEAD = 64
        INNER = HEADS * DIM_HEAD
        QUERY_DIM = 512
        CONTEXT_DIM = 512
        TEXT_LEN = 77
        IMG_SCALE = 1.0
        SCALE = DIM_HEAD ** (-0.5)

        def _attend(q, k, v):
            sim = jnp.einsum('bihd,bjhd->bhij', q, k) * SCALE
            attn = jax.nn.softmax(sim, axis=-1)
            out = jnp.einsum('bhij,bjhd->bihd', attn, v)
            B, N, H, D = out.shape
            return out.reshape(B, N, H * D)
        B, N, _ = x.shape
        ctx_txt = context[:, :TEXT_LEN, :]
        ctx_img = context[:, TEXT_LEN:, :]
        q = (x @ Wq).reshape(B, N, HEADS, DIM_HEAD)
        k = (ctx_txt @ Wk).reshape(B, TEXT_LEN, HEADS, DIM_HEAD)
        v = (ctx_txt @ Wv).reshape(B, TEXT_LEN, HEADS, DIM_HEAD)
        out = _attend(q, k, v)
        Li = ctx_img.shape[1]
        k_ip = (ctx_img @ Wk_ip).reshape(B, Li, HEADS, DIM_HEAD)
        v_ip = (ctx_img @ Wv_ip).reshape(B, Li, HEADS, DIM_HEAD)
        out_ip = _attend(q, k_ip, v_ip)
        out = out + IMG_SCALE * out_ip
        return out @ Wo + bo

    def _L0_ffn_ref(x, w_gate, w_up, w_down):
        import jax, jax.numpy as jnp
        import numpy as np
        BLOCK = 32
        W_BITS = 4
        ACT_BITS = 16

        def act_qdq(x):
            qmax = 2.0 ** (ACT_BITS - 1) - 1.0
            scale = jnp.maximum(jnp.max(jnp.abs(x)) / qmax, 1e-12)
            return jnp.clip(jnp.round(x / scale), -qmax - 1.0, qmax) * scale

        def fixed_qdq_u16(x):
            scale = 1.0 / 65536.0
            return jnp.clip(jnp.round(x / scale), 0.0, 65535.0) * scale

        def lpbq_dequant(w):
            O, I = w.shape
            qmax = 2.0 ** (W_BITS - 1) - 1.0
            wb = w.reshape(O, I // BLOCK, BLOCK)
            s = jnp.maximum(jnp.max(jnp.abs(wb), axis=-1, keepdims=True) / qmax, 1e-12)
            wq = jnp.clip(jnp.round(wb / s), -qmax - 1.0, qmax) * s
            return wq.reshape(O, I)
        x = act_qdq(x)
        up = act_qdq(x @ lpbq_dequant(w_up).T)
        gate = act_qdq(x @ lpbq_dequant(w_gate).T)
        sig = fixed_qdq_u16(jax.nn.sigmoid(gate))
        gate = act_qdq(gate * sig)
        o = act_qdq(gate * up)
        return o @ lpbq_dequant(w_down).T

    def _L1_xattn_ref(q, k, v1, mask, W1, b1, W2, b2):
        import jax, jax.numpy as jnp
        import numpy as np
        import math
        D = 512
        B, S = (8, 1024)

        def _proj(x, W1, b1, W2, b2):
            h = jnp.einsum('bsd,od->bso', x, W1) + b1
            return jnp.einsum('bsd,od->bso', h, W2) + b2
        qp = _proj(q, W1, b1, W2, b2)
        kp = _proj(k, W1, b1, W2, b2)
        scale = 1.0 / math.sqrt(qp.shape[-1])
        qk = jnp.einsum('bqd,bkd->bqk', qp, kp) * scale
        qk = qk + mask
        attn = jax.nn.softmax(qk, axis=-1)
        return jnp.einsum('bqk,bkd->bqd', attn, v1)

    def _L1_ffn_ref(x, W1, b1, A1, B1, R1, W2, b2, A2, B2, R2):
        import jax, jax.numpy as jnp
        import numpy as np
        B, S, D, H = (8, 512, 512, 2048)
        E, R = (3, 8)
        SCALING = 1.0 / R

        def _mole(x, W, b, A, Bm, Rw):
            gates = jax.nn.softmax(jnp.einsum('bsd,de->bse', x, Rw), axis=-1)
            base = jnp.einsum('bsd,dh->bsh', x, W) + b
            z = jnp.einsum('bsd,edr->ebsr', x, A)
            zg = z * jnp.transpose(gates, (2, 0, 1))[..., None]
            lora = jnp.einsum('ebsr,erh->bsh', zg, Bm)
            return base + SCALING * lora
        h = _mole(x, W1, b1, A1, B1, R1)
        h = jax.nn.relu(h)
        return _mole(h, W2, b2, A2, B2, R2)
    x = x + _L0_xattn_ref(_layernorm(x, axis=-1), ctx_1024, L0_xattn_Wq, L0_xattn_Wk, L0_xattn_Wv, L0_xattn_Wk_ip, L0_xattn_Wv_ip, L0_xattn_Wo, L0_xattn_bo)
    x = x + _L0_ffn_ref(_layernorm(x, axis=-1), L0_ffn_w_gate, L0_ffn_w_up, L0_ffn_w_down)
    x = x + _L1_xattn_ref(_layernorm(x, axis=-1), ctx_1024, ctx_1024, fside_1xSxS2_0, L1_xattn_W1, L1_xattn_b1, L1_xattn_W2, L1_xattn_b2)
    x = x + _L1_ffn_ref(_layernorm(x, axis=-1), L1_ffn_W1, L1_ffn_b1, L1_ffn_A1, L1_ffn_B1, L1_ffn_R1, L1_ffn_W2, L1_ffn_b2, L1_ffn_A2, L1_ffn_B2, L1_ffn_R2)
    return x

_drawn_inputs = setup_inputs


def setup_inputs(seed=0):
    import zlib

    import numpy as np

    out = dict(_drawn_inputs(seed))
    spreads = {'L0_xattn_bo': (0.0, 0.1), 'L1_ffn_b1': (0.0, 0.1), 'L1_ffn_b2': (0.0, 0.1)}
    factors = {'L1_xattn_b1': 8.0,
     'L1_xattn_W2': 3.811,
     'L1_xattn_b2': 8.0,
     'L1_ffn_R2': 3.46,
     'L1_ffn_R1': 2.698}
    for name, (base, spread) in spreads.items():
        noise = np.random.default_rng([zlib.crc32(name.encode()), seed]).standard_normal(out[name].shape)
        drawn = base * np.exp(spread * noise) if base else spread * noise
        out[name] = jnp.asarray(drawn.astype(out[name].dtype))
    for name, factor in factors.items():
        out[name] = (out[name] * factor).astype(out[name].dtype)
    return out
```

```python
from contextlib import ExitStack

import concourse.bass as bass
from concourse import mybir

ALU = mybir.AluOpType
ACT = mybir.ActivationFunctionType
F32 = mybir.dt.float32
I16 = mybir.dt.int16
U16 = mybir.dt.uint16
AX_X = mybir.AxisListType.X
RMAX = bass.bass_isa.ReduceOp.max

P = 128
B, S, D = 16, 256, 512
TOK = B * S
CT = 512
NCH = TOK // CT
NT = CT // P
KD = D // P
NB = CT // S
EPS = 1e-5

HEADS, DH = 16, 64
INNER = HEADS * DH
TEXT = 77
NPAIR = HEADS // 2

FF = 1536
KF = FF // P
QB = 32
WMAX = 7.0
AMAX = 32767.0
TINY = 1e-12
SIGQ = 65536.0
MAGIC = 12582912.0

H2 = 2048
KH = H2 // P
E, R = 3, 8
ER = E * R
LZ = E + ER


class Count:

    def __init__(self, eng, sem, base=0):
        self.eng, self.sem, self.base, self.n = eng, sem, base, 0

    def done(self, ins):
        ins.then_inc(self.sem, 1)
        self.n += 1
        return self.n

    def wait(self, n=None):
        self.eng.wait_ge(self.sem, self.base + (self.n if n is None else n))


class Phase:

    def __init__(self, nc, name):
        self.nc, self.name, self.ctx = nc, name, ExitStack()
        self.sems, self.blocks = [], ExitStack()

    def __enter__(self):
        self.ctx.__enter__()
        return self

    def __exit__(self, *a):
        self.blocks.close()
        if self.sems:
            with self.nc.Block() as block:
                @block.sync
                def _(sp):
                    for s in self.sems:
                        sp.sem_clear(s)
        return self.ctx.__exit__(*a)

    def block(self):
        return self.blocks.enter_context(self.nc.Block())

    def sb(self, name, shape, dt=F32):
        return self.ctx.enter_context(self.nc.sbuf_tensor(f"{self.name}_{name}", shape, dt))

    def ps(self, name, shape):
        return self.ctx.enter_context(self.nc.psum_tensor(f"{self.name}_{name}", shape, F32))

    def sem(self, name):
        self.sems.append(self.ctx.enter_context(self.nc.semaphore(f"{self.name}_{name}")))
        return self.sems[-1]


def wait_alone(eng, sem, value, spacer):
    eng.wait_ge(sem, value)
    eng.sem_inc(spacer, 1)


def tokens(ap, c):
    return ap[bass.ds(c * CT, CT), :].rearrange("(t p) d -> p t d", p=P)


def flat3(ap):
    return ap.rearrange("b s d -> (b s) d")


def kernel_program(nc, a, out):
    x_in, ctx_in, out_f = flat3(a["x"]), flat3(a["ctx_1024"]), flat3(out)
    x1 = nc.dram_tensor("x1", (TOK, D), F32).ap()
    x2 = nc.dram_tensor("x2", (TOK, D), F32).ap()
    x3 = nc.dram_tensor("x3", (TOK, D), F32).ap()
    raw_up = nc.dram_tensor("raw_up", (NCH, P, KF * CT), F32).ap()
    raw_gate = nc.dram_tensor("raw_gate", (NCH, P, KF * CT), F32).ap()
    with ExitStack() as top:
        ident = top.enter_context(nc.sbuf_tensor("ident", [P, P], F32))
        neghalf = top.enter_context(nc.sbuf_tensor("neghalf", [P, NT], F32))
        consts(nc, ident, neghalf)
        cross_attention(nc, a, x_in, ctx_in, x1, ident, neghalf)
        quantized_ffn(nc, a, x1, x2, raw_up, raw_gate, ident, neghalf)
        masked_attention(nc, a, x2, ctx_in, x3, ident, neghalf)
        lora_ffn(nc, a, x3, out_f, ident, neghalf)


def consts(nc, ident, neghalf):
    with Phase(nc, "c0") as ph:
        cleared = ph.sem("cleared")
        made = ph.sem("made")
        with nc.Block() as block:
            @block.gpsimd
            def _(pool):
                pool.memset(neghalf[:], -0.5).then_inc(made, 1)
                pool.memset(ident[:], 0.0).then_inc(cleared, 1)
                pool.wait_ge(cleared, 1)
                pool.affine_select(out=ident[:], in_=ident[:], compare_op=ALU.not_equal, fill=1.0, base=0,
                                   pattern=[[-1, P]], channel_multiplier=1).then_inc(made, 1)
                pool.wait_ge(made, 2)



def norm_stats(dve, st, mv, steps, mv_ready, spacer, x):
    for t in range(NT):
        n = steps.done(dve.bn_stats(st[:, t, :], x[:, t, :]))
    steps.eng.wait_ge(steps.sem, steps.base + n)
    dve.sem_inc(spacer, 1)
    for t in range(NT):
        ins = dve.bn_aggr(mv[:, t, :], st[:, t, :])
    ins.then_inc(mv_ready, 1)


def norm_rstd(pool, mv, var, rstd, neghalf, mv_ready, rstd_ready, var_done, it, spacer):
    wait_alone(pool, mv_ready, it + 1, spacer)
    pool.tensor_scalar(var[:], mv[:, :, 1], EPS, None, ALU.add).then_inc(var_done, 1)
    pool.wait_ge(var_done, it + 1)
    pool.tensor_tensor(rstd[:], var[:], neghalf[:], ALU.pow).then_inc(rstd_ready, 1)


def norm_rows(dve, xn, x, mv, rstd):
    for t in range(NT):
        ins = dve.tensor_scalar(xn[:, t, :], x[:, t, :], mv[:, t, 0:1], rstd[:, t:t + 1], ALU.subtract, ALU.mult)
    return ins


def transpose_job(pe, bank, src, k, ident):
    for t in range(NT):
        ins = pe.transpose(bank[:, t * P:(t + 1) * P], src[:, t, k * P:(k + 1) * P], ident[:])
    return ins


def cross_attention(nc, a, x_in, ctx_in, x1, ident, neghalf):
    JOBS = 2 * KD + 3 * NPAIR + NT
    JB = JOBS // 2
    U = NB * HEADS
    SEG = [(0, TEXT), (TEXT, S)]
    XT0, CT0, PR0, OU0 = 0, KD, 2 * KD, 2 * KD + 3 * NPAIR
    with Phase(nc, "xa") as ph:
        w = {n: ph.sb(n, [P, KD, INNER]) for n in ("Wq", "Wk", "Wv", "Wk_ip", "Wv_ip")}
        wo = ph.sb("Wo", [P, NPAIR, D])
        bo = ph.sb("bo", [P, D])
        xin = ph.sb("xin", [P, NT, D])
        cin = ph.sb("cin", [P, NT, D])
        xres = ph.sb("xres", [P, NT, D])
        xn = ph.sb("xn", [P, NT, D])
        st = ph.sb("st", [P, NT, 6])
        mv = ph.sb("mv", [P, NT, 2])
        var = ph.sb("var", [P, NT])
        rstd = ph.sb("rstd", [P, NT])
        xT = ph.sb("xT", [P, KD, CT])
        cT = ph.sb("cT", [P, KD, CT])
        cimg = ph.sb("cimg", [P, KD, NB, P])
        qT = ph.sb("qT", [P, 2, CT])
        kT = ph.sb("kT", [P, 2, CT])
        v = ph.sb("v", [P, 2, 2 * NB, P])
        nm = ph.sb("nm", [P, 2, 2, 2])
        sums = ph.sb("sums", [P, 2, 2, 2])
        rec = ph.sb("rec", [P, 2, 2, 2])
        prob = ph.sb("prob", [P, 2, 2, S])
        pT = ph.sb("pT", [P, 2, 2, S])
        oT = ph.sb("oT", [P, NPAIR, CT])
        yout = ph.sb("yout", [P, NT, D])
        pj = [ph.ps(f"pj{i}", [P, CT]) for i in range(2)]
        sc = [ph.ps(f"sc{i}", [P, 2, S]) for i in range(2)]
        tp = [ph.ps(f"tp{i}", [P, 2, S]) for i in range(2)]
        po = [ph.ps(f"po{i}", [P, 512]) for i in range(2)]
        loaded = ph.sem("weights")
        x_ready, c_ready, stored = ph.sem("x_ready"), ph.sem("c_ready"), ph.sem("stored")
        c_used, res_ready = ph.sem("c_used"), ph.sem("res_ready")
        cimg_clear, var_done = ph.sem("cimg_clear"), ph.sem("var_done")
        steps_done, mv_ready, rstd_ready, xn_ready = (ph.sem(n) for n in ("steps", "mv_ready", "rstd_ready", "xn_ready"))
        spacer_d, spacer_p = ph.sem("spacer_d"), ph.sem("spacer_p")
        job_full = ph.sem("job_full")
        job_done = [ph.sem(f"job_done{i}") for i in range(2)]
        s_full, max_done, exp_done, norm_done = (ph.sem(n) for n in ("s_full", "max_done", "exp_done", "norm_done"))
        t_full, pt_done, pv_full, o_done = (ph.sem(n) for n in ("t_full", "pt_done", "pv_full", "o_done"))
        rec_done = ph.sem("rec_done")
        block = ph.block()

        def slot_job(t):
            p = t // 4 + 1
            return (p, t % 4, PR0 + 3 * p + t % 4) if p < NPAIR and t % 4 < 3 and t < U else None

        @block.sync
        def _(sp):
            for n, t in w.items():
                sp.dma_start(t[:], a["L0_xattn_" + n].rearrange("(k p) n -> p k n", p=P)).then_inc(loaded, 16)
            sp.dma_start(bo[:], a["L0_xattn_bo"].rearrange("(o n) -> o n", o=1).broadcast_to([P, D])).then_inc(loaded, 16)
            sp.dma_start(wo[:], a["L0_xattn_Wo"].rearrange("(k p) n -> p k n", p=P)).then_inc(loaded, 16)
            sp.sem_inc(xn_ready, 1)
            sp.sem_inc(res_ready, 1)
            sp.sem_inc(c_used, 1)
            with sp.Fori(0, NCH) as it:
                sp.wait_ge(xn_ready, it + 1)
                sp.wait_ge(res_ready, it + 1)
                sp.dma_start(xin[:], tokens(x_in, it)).then_inc(x_ready, 16)
                sp.wait_ge(c_used, it + 1)
                sp.dma_start(cin[:], tokens(ctx_in, it)).then_inc(c_ready, 16)

        @block.gpsimd
        def _(pool):
            pool.memset(cimg[:, :, :, 0:TEXT], 0.0).then_inc(cimg_clear, 1)
            pool.wait_ge(loaded, 16 * 7)
            with pool.Fori(0, NCH) as it:
                norm_rstd(pool, mv, var, rstd, neghalf, mv_ready, rstd_ready, var_done, it, spacer_p)
                for s in job_done:
                    wait_alone(pool, s, JB * it + 1, spacer_p)
                wait_alone(pool, x_ready, 16 * it + 16, spacer_p)
                for t in range(NT):
                    ins = pool.tensor_tensor(xres[:, t, :], xin[:, t, :], bo[:], ALU.add)
                ins.then_inc(res_ready, 1)

        @block.vector
        def _(dve):
            dve.wait_ge(cimg_clear, 1)
            with dve.Fori(0, NCH) as it:
                steps = Count(dve, steps_done, NT * it)
                dve.wait_ge(x_ready, 16 * it + 16)
                norm_stats(dve, st, mv, steps, mv_ready, spacer_d, xin)
                dve.wait_ge(rstd_ready, it + 1)
                norm_rows(dve, xn, xin, mv, rstd).then_inc(xn_ready, 1)

                def evacuate(p, what, g):
                    dve.wait_ge(job_full, JOBS * it + g + 1)
                    to = kT[:, p % 2, :] if what == 1 else v[:, p % 2].rearrange("p j n -> p (j n)")
                    dve.tensor_copy(to, pj[g % 2][:]).then_inc(job_done[g % 2], 1)

                evacuate(0, 1, PR0 + 1)
                evacuate(0, 2, PR0 + 2)
                for t in range(U + 1):
                    i = t % 2
                    if t < U:
                        dve.wait_ge(s_full, U * it + t + 1)
                        for g, (lo, hi) in enumerate(SEG):
                            ins = dve.tensor_reduce(nm[:, i, g, :], sc[i][:, :, lo:hi], AX_X, ALU.max, negate=True)
                        ins.then_inc(max_done, 1)
                        job = slot_job(t)
                        if job and job[1] > 0:
                            evacuate(*job)
                        dve.wait_ge(exp_done, U * it + t + 3)
                        dve.reciprocal(rec[:, i].rearrange("p a b -> p (a b)"),
                                       sums[:, i].rearrange("p a b -> p (a b)")).then_inc(rec_done, 1)
                        dve.wait_ge(rec_done, U * it + t + 1)
                        for g, (lo, hi) in enumerate(SEG):
                            for m in range(2):
                                ins = dve.tensor_scalar(prob[:, i, m, lo:hi], prob[:, i, m, lo:hi], rec[:, i, g, m:m + 1],
                                                        None, ALU.mult)
                        ins.then_inc(norm_done, 1)
                    if t > 0:
                        j = (t - 1) % 2
                        dve.wait_ge(t_full, U * it + t + 2)
                        dve.wait_ge(pv_full, U * it + t)
                        dve.tensor_copy(pT[:, j], tp[j][:]).then_inc(pt_done, 1)
                for t in range(NT):
                    g = OU0 + t
                    dve.wait_ge(job_full, JOBS * it + g + 1)
                    if t == 0:
                        dve.wait_ge(res_ready, it + 2)
                        dve.wait_ge(stored, 16 * it + 16)
                    dve.tensor_tensor(yout[:, t, :], pj[g % 2][:], xres[:, t, :], ALU.add).then_inc(job_done[g % 2], 1)

        @block.scalar
        def _(act):
            act.sem_inc(t_full, 2)
            act.sem_inc(stored, 16)
            act.wait_ge(cimg_clear, 1)
            with act.Fori(0, NCH) as it:
                for g in range(2 * KD):
                    k = g % KD
                    act.wait_ge(job_full, JOBS * it + g + 1)
                    if g < KD:
                        ins = act.activation(xT[:, k, :], pj[g % 2][:], ACT.Copy)
                    else:
                        act.activation(cT[:, k, :], pj[g % 2][:], ACT.Copy)
                        ins = act.activation(cimg[:, k, :, TEXT:P], pj[g % 2][:].rearrange("p (b s) -> p b s", b=NB)[:, :, TEXT:P], ACT.Copy)
                    ins.then_inc(job_done[g % 2], 1)

                def query(p, what, g):
                    act.wait_ge(job_full, JOBS * it + g + 1)
                    act.activation(qT[:, p % 2, :], pj[g % 2][:], ACT.Copy, scale=DH ** -0.5).then_inc(job_done[g % 2], 1)

                query(0, 0, PR0)
                for t in range(U + 2):
                    i = t % 2
                    if t < U:
                        act.wait_ge(max_done, U * it + t + 1)
                        act.wait_ge(t_full, U * it + t + 1)
                        for g, (lo, hi) in enumerate(SEG):
                            for m in range(2):
                                ins = act.activation(prob[:, i, m, lo:hi], sc[i][:, m, lo:hi], ACT.Exp,
                                                     bias=nm[:, i, g, m:m + 1], accum_out=sums[:, i, g, m:m + 1])
                        ins.then_inc(exp_done, 1)
                        job = slot_job(t)
                        if job and job[1] == 0:
                            query(*job)
                    if t > 1:
                        u = t - 2
                        p, b, h = u // 4, u // 2 % 2, u % 2
                        act.wait_ge(pv_full, U * it + u + 3)
                        act.activation(oT[64 * h:64 * h + 64, p, b * S:(b + 1) * S], po[u % 2][0:DH, 0:S], ACT.Copy).then_inc(o_done, 1)
                for s in job_done:
                    act.wait_ge(s, JB * it + JB + 1)
                act.dma_start(tokens(x1, it), yout[:]).then_inc(stored, 16)
            act.wait_ge(stored, 16 * NCH + 16)

        @block.tensor
        def _(pe):
            for s in job_done:
                pe.sem_inc(s, 1)
            pe.sem_inc(exp_done, 2)
            pe.sem_inc(pt_done, 2)
            pe.sem_inc(pv_full, 2)
            pe.sem_inc(o_done, 2)
            pe.wait_ge(loaded, 16 * 7)
            with pe.Fori(0, NCH) as it:
                def free(g):
                    pe.wait_ge(job_done[g % 2], JB * it + g // 2 + 1)

                def taken(g):
                    pe.wait_ge(job_done[g % 2], JB * it + g // 2 + 2)

                pe.wait_ge(xn_ready, it + 2)
                for g in range(KD):
                    free(g)
                    transpose_job(pe, pj[g % 2], xn, g, ident).then_inc(job_full, 1)
                pe.wait_ge(c_ready, 16 * it + 16)
                for g in range(KD, 2 * KD):
                    free(g)
                    ins = transpose_job(pe, pj[g % 2], cin, g - KD, ident)
                    ins.then_inc(job_full, 1)

                def project(p, what, g):
                    free(g)
                    out = pj[g % 2]
                    cols = slice(p * P, (p + 1) * P)
                    if what == 0:
                        for k in range(KD):
                            ins = pe.matmul(out[:], w["Wq"][:, k, cols], xT[:, k, :], start=k == 0, stop=k == KD - 1)
                    elif what == 1:
                        for name, (lo, hi) in zip(("Wk", "Wk_ip"), SEG):
                            for k in range(KD):
                                ins = pe.matmul(out[:].rearrange("p (b s) -> p b s", b=NB)[:, :, lo:hi], w[name][:, k, cols],
                                                cT[:, k, :].rearrange("p (b s) -> p b s", b=NB)[:, :, lo:hi],
                                                start=k == 0, stop=k == KD - 1)
                    else:
                        for j in range(2 * NB):
                            b, c = j // 2, j % 2
                            o = out[:, j * P:(j + 1) * P]
                            for k in range(KD):
                                keys = cT[:, k, b * S + P:(b + 1) * S] if c else cimg[:, k, b, :]
                                ins = pe.matmul(o, keys, w["Wv_ip"][:, k, cols], start=k == 0, stop=k == KD - 1)
                            if c == 0:
                                for k in range(KD):
                                    ins = pe.matmul(out[0:TEXT, j * P:(j + 1) * P], cT[:, k, b * S:b * S + TEXT],
                                                    w["Wv"][:, k, cols], start=False, stop=False, skip_group_check=True)
                    ins.then_inc(job_full, 1)

                taken(KD - 1)
                taken(KD - 2)
                project(0, 0, PR0)
                taken(2 * KD - 1)
                taken(2 * KD - 2)
                pe.sem_inc(c_used, 1)
                project(0, 1, PR0 + 1)
                project(0, 2, PR0 + 2)
                for t in range(U + 2):
                    if t < U:
                        p, b, h = t // 4, t // 2 % 2, t % 2
                        if t % 4 == 0:
                            taken(PR0 + 3 * p)
                            taken(PR0 + 3 * p + 1)
                            taken(PR0 + 3 * p + 2)
                        pe.wait_ge(exp_done, U * it + t + 1)
                        rows = slice(64 * h, 64 * h + 64)
                        for m in range(2):
                            q0 = b * S + m * P
                            ins = pe.matmul(sc[t % 2][:, m, :], qT[rows, p % 2, q0:q0 + P], kT[rows, p % 2, b * S:(b + 1) * S],
                                            start=True, stop=True)
                        ins.then_inc(s_full, 1)
                        job = slot_job(t)
                        if job:
                            project(*job)
                    if 0 < t <= U:
                        u = t - 1
                        pe.wait_ge(norm_done, U * it + u + 1)
                        pe.wait_ge(pt_done, U * it + u + 1)
                        for c in range(2):
                            for m in range(2):
                                ins = pe.transpose(tp[u % 2][:, c, m * P:(m + 1) * P], prob[:, u % 2, m, c * P:(c + 1) * P], ident[:])
                        ins.then_inc(t_full, 1)
                    if t > 1:
                        u = t - 2
                        p, b, h = u // 4, u // 2 % 2, u % 2
                        pe.wait_ge(pt_done, U * it + u + 3)
                        pe.wait_ge(o_done, U * it + u + 1)
                        for c in range(2):
                            ins = pe.matmul(po[u % 2][0:DH, 0:S], v[:, p % 2, 2 * b + c, DH * h:DH * h + DH], pT[:, u % 2, c, :],
                                            start=c == 0, stop=c == 1)
                        ins.then_inc(pv_full, 1)
                pe.wait_ge(o_done, U * it + U + 2)
                for t in range(NT):
                    g = OU0 + t
                    free(g)
                    for k in range(NPAIR):
                        ins = pe.matmul(pj[g % 2][:], oT[:, k, t * P:(t + 1) * P], wo[:, k, :], start=k == 0, stop=k == NPAIR - 1)
                    ins.then_inc(job_full, 1)



SUB = 3
SC = KF * CT // SUB
MS = KF // SUB
S_X, I_X, S_G, I_G, S_U, I_U, S_A, I_A, S_O, I_O, S_AU = range(11)


def dequantize(nc, name, loops, pieces, ident):
    n = len(pieces)
    NQ = D // QB
    with Phase(nc, name) as ph:
        raw = ph.sb("raw", [P, n, NQ, QB])
        amax = ph.sb("amax", [P, n, NQ])
        scale = ph.sb("scale", [P, n, NQ])
        inv = ph.sb("inv", [P, n, NQ])
        deq = ph.sb("deq", [P, n, NQ, QB])
        turned = [ph.ps(f"turned{i}", [P, KD, P]) for i in range(n)]
        raw_ready = [ph.sem(f"raw_ready{i}") for i in range(n)]
        steps_done, deq_ready, turned_full = ph.sem("steps"), ph.sem("deq_ready"), ph.sem("turned_full")
        placed = ph.sem("placed")
        spacer = ph.sem("spacer")
        STEPS = 5
        with nc.Block() as block:
            @block.sync
            def _(sp):
                sp.sem_inc(deq_ready, n)
                with sp.Fori(0, loops) as it:
                    for i, (src, _) in enumerate(pieces):
                        sp.wait_ge(deq_ready, n * it + i + 1)
                        sp.dma_start(raw[:, i], src(it).rearrange("p (a b) -> p a b", b=QB)).then_inc(raw_ready[i], 16)

            @block.vector
            def _(dve):
                dve.sem_inc(turned_full, n)
                with dve.Fori(0, loops) as it:
                    for i in range(n):
                        c = Count(dve, steps_done, (n * STEPS) * it + i * STEPS)
                        dve.wait_ge(raw_ready[i], 16 * it + 16)
                        c.done(dve.tensor_reduce(amax[:, i], raw[:, i], AX_X, ALU.max, apply_absolute_value=True))
                        c.wait()
                        c.done(dve.tensor_scalar(scale[:, i], amax[:, i], 1.0 / WMAX, TINY, ALU.mult, ALU.max))
                        c.wait()
                        c.done(dve.reciprocal(inv[:, i], scale[:, i]))
                        c.wait()
                        dve.wait_ge(turned_full, n * it + i + 1)
                        c.done(dve.tensor_tensor(deq[:, i], raw[:, i], inv[:, i].unsqueeze(2).broadcast_to([P, NQ, QB]), ALU.mult))
                        c.wait()
                        c.done(dve.tensor_scalar(deq[:, i], deq[:, i], MAGIC, MAGIC, ALU.add, ALU.subtract))
                        c.wait()
                        dve.tensor_tensor(deq[:, i], deq[:, i], scale[:, i].unsqueeze(2).broadcast_to([P, NQ, QB]), ALU.mult).then_inc(deq_ready, 1)
                        assert c.n == STEPS

            @block.tensor
            def _(pe):
                pe.sem_inc(placed, n)
                with pe.Fori(0, loops) as it:
                    for i in range(n):
                        pe.wait_ge(deq_ready, n * it + i + 1 + n)
                        pe.wait_ge(placed, n * it + i + 1)
                        rows = deq[:, i].rearrange("p a b -> p (a b)")
                        for k in range(KD):
                            ins = pe.transpose(turned[i][:, k, :], rows[:, k * P:(k + 1) * P], ident[:])
                        ins.then_inc(turned_full, 1)

            @block.scalar
            def _(act):
                with act.Fori(0, loops) as it:
                    for i, (_, dst) in enumerate(pieces):
                        wait_alone(act, turned_full, n * it + i + 1 + n, spacer)
                        act.activation(dst(it), turned[i][:], ACT.Copy).then_inc(placed, 1)


def quantized_ffn(nc, a, x1, x2, raw_up, raw_gate, ident, neghalf):
    with Phase(nc, "qf") as top:
        wd = top.sb("wd", [P, KF, D])
        scal = top.sb("scal", [P, 16])
        big = top.sb("big", [P, 4])
        with Phase(nc, "qw") as mid:
            wu = mid.sb("wu", [P, KD, FF])
            wg = mid.sb("wg", [P, KD, FF])
            xn = mid.sb("xn", [P, NCH, NT * D])

            def rows_of(w, col=0):
                return lambda it: w[bass.ds(it * P, P), col:col + D]

            dequantize(nc, "qwug", KF, [(rows_of(a["L0_ffn_w_up"]), lambda it: wu[:, :, bass.ds(it * P, P)]),
                                        (rows_of(a["L0_ffn_w_gate"]), lambda it: wg[:, :, bass.ds(it * P, P)])], ident)
            dequantize(nc, "qwd", KD, [(rows_of(a["L0_ffn_w_down"], c * D),
                                        lambda it, c=c: wd[:, c * KD:(c + 1) * KD, bass.ds(it * P, P)]) for c in range(FF // D)], ident)
            normalize_all(nc, x1, xn, big, scal, neghalf)
            up_and_gate(nc, xn, wu, wg, raw_up, raw_gate, big, scal, ident)
        gate = top.sb("gate", [P, NCH * KF * CT], I16)
        gate_product(nc, raw_gate, gate, big, scal)
        output_maximum(nc, raw_up, gate, big, scal)
        down(nc, x1, x2, raw_up, gate, wd, scal)


def over_all(nc, block, ph, mx, col, big, settle, ready, ready_value):
    row_max, all_max = ph.sem("row_max"), ph.sem("all_max")
    settled = ph.sem("settled")

    def vector(dve):
        dve.wait_ge(ready, ready_value)
        dve.tensor_reduce(mx["row"][:], mx["all"][:], AX_X, ALU.max).then_inc(row_max, 1)
        dve.wait_ge(all_max, 1)
        settle(dve, Count(dve, settled))

    def pool(p):
        p.wait_ge(row_max, 1)
        p.partition_all_reduce(big[:, col:col + 1], mx["row"][:], P, RMAX).then_inc(all_max, 1)

    return vector, pool


def scale_of(dve, c, scal, big_col, scale, inverse, unit, raw):
    def col(i):
        return scal[:, i:i + 1]
    if unit is None:
        c.done(dve.tensor_scalar(col(scale), big_col, 1.0 / AMAX, TINY, ALU.mult, ALU.max))
        c.wait()
        c.done(dve.reciprocal(col(inverse), col(scale)))
        c.wait()
        return
    c.done(dve.tensor_scalar(col(scale), big_col, col(unit), raw / AMAX, ALU.mult, ALU.mult))
    c.wait()
    c.done(dve.tensor_scalar(col(scale), col(scale), TINY, None, ALU.max))
    c.wait()
    c.done(dve.reciprocal(col(inverse), col(scale)))
    c.wait()
    c.done(dve.tensor_scalar(col(inverse), col(inverse), col(unit), raw, ALU.mult, ALU.mult))
    c.wait()


def normalize_all(nc, x1, xn, big, scal, neghalf):
    with Phase(nc, "na") as ph:
        xin = ph.sb("xin", [P, NT, D])
        st = ph.sb("st", [P, NT, 6])
        mv = ph.sb("mv", [P, NT, 2])
        var = ph.sb("var", [P, NT])
        rstd = ph.sb("rstd", [P, NT])
        mx = {"all": ph.sb("mx", [P, NCH]), "row": ph.sb("mxrow", [P, 1])}
        x_ready, xn_ready, max_done = ph.sem("x_ready"), ph.sem("xn_ready"), ph.sem("max_done")
        steps_done, mv_ready, rstd_ready, var_done = (ph.sem(n) for n in ("steps", "mv_ready", "rstd_ready", "var_done"))
        spacer_d, spacer_p = ph.sem("spacer_d"), ph.sem("spacer_p")
        with nc.Block() as block:
            def settle(dve, c):
                scale_of(dve, c, scal, big[:, 0:1], S_X, I_X, None, None)
            vector_max, pool_max = over_all(nc, block, ph, mx, 0, big, settle, max_done, NCH)

            @block.sync
            def _(sp):
                sp.sem_inc(xn_ready, 1)
                with sp.Fori(0, NCH) as it:
                    sp.wait_ge(xn_ready, it + 1)
                    sp.dma_start(xin[:], tokens(x1, it)).then_inc(x_ready, 16)

            @block.gpsimd
            def _(pool):
                with pool.Fori(0, NCH) as it:
                    norm_rstd(pool, mv, var, rstd, neghalf, mv_ready, rstd_ready, var_done, it, spacer_p)
                pool_max(pool)

            @block.vector
            def _(dve):
                with dve.Fori(0, NCH) as it:
                    steps = Count(dve, steps_done, NT * it)
                    dve.wait_ge(x_ready, 16 * it + 16)
                    norm_stats(dve, st, mv, steps, mv_ready, spacer_d, xin)
                    dve.wait_ge(rstd_ready, it + 1)
                    for t in range(NT):
                        ins = dve.tensor_scalar(xn[:, bass.ds(it, 1), t * D:(t + 1) * D].rearrange("p a n -> p (a n)"), xin[:, t, :],
                                                mv[:, t, 0:1], rstd[:, t:t + 1], ALU.subtract, ALU.mult)
                    ins.then_inc(xn_ready, 1)
                    dve.wait_ge(xn_ready, it + 2)
                    dve.tensor_reduce(mx["all"][:, bass.ds(it, 1)], xn[:, bass.ds(it, 1), :].rearrange("p a n -> p (a n)"), AX_X, ALU.max,
                                      apply_absolute_value=True).then_inc(max_done, 1)
                vector_max(dve)


def up_and_gate(nc, xn, wu, wg, raw_up, raw_gate, big, scal, ident):
    NBANK = 6
    JOBS = 2 * KF
    JB = JOBS // NBANK
    with Phase(nc, "ug") as ph:
        xq = ph.sb("xq", [P, NT, D])
        xqT = ph.sb("xqT", [P, KD, CT])
        stage = ph.sb("stage", [P, NBANK, CT])
        mxu = {"all": ph.sb("mxu", [P, NCH * KF]), "row": ph.sb("mxurow", [P, 1])}
        mxg = {"all": ph.sb("mxg", [P, NCH * KF]), "row": ph.sb("mxgrow", [P, 1])}
        tp = [ph.ps(f"tp{i}", [P, CT]) for i in range(2)]
        pr = [ph.ps(f"pr{i}", [P, CT]) for i in range(NBANK)]
        xq_ready, t_full, t_done, r_full, r_copied, max_done = (ph.sem(n) for n in ("xq_ready", "t_full", "t_done", "r_full", "r_copied", "max_done"))
        stored = [ph.sem(f"stored{i}") for i in range(NBANK)]
        row_max, all_max, settled = ph.sem("row_max"), ph.sem("all_max"), ph.sem("settled")
        with nc.Block() as block:
            @block.vector
            def _(dve):
                with dve.Fori(0, NCH) as it:
                    dve.wait_ge(t_done, KD * it + 2)
                    dve.tensor_scalar(xq[:].rearrange("p t d -> p (t d)"), xn[:, bass.ds(it, 1), :].rearrange("p a n -> p (a n)"),
                                      scal[:, I_X:I_X + 1], MAGIC, ALU.mult, ALU.add).then_inc(xq_ready, 1)
                    for k in range(KD):
                        dve.wait_ge(t_full, KD * it + k + 1)
                        dve.tensor_scalar(xqT[:, k, :], tp[k % 2][:], MAGIC, None, ALU.subtract).then_inc(t_done, 1)
                    for g in range(JOBS):
                        m = (mxu, mxg)[g % 2]["all"]
                        dve.wait_ge(r_copied, JOBS * it + g + 1 + NBANK)
                        dve.tensor_reduce(m[:, bass.ds(it * KF + g // 2, 1)], stage[:, g % NBANK, :], AX_X, ALU.max,
                                          apply_absolute_value=True).then_inc(max_done, 1)
                dve.wait_ge(max_done, JOBS * NCH + NBANK)
                dve.tensor_reduce(mxu["row"][:], mxu["all"][:], AX_X, ALU.max).then_inc(row_max, 1)
                dve.tensor_reduce(mxg["row"][:], mxg["all"][:], AX_X, ALU.max).then_inc(row_max, 1)
                dve.wait_ge(all_max, 2)
                c = Count(dve, settled)
                scale_of(dve, c, scal, big[:, 0:1], S_U, I_U, S_X, 1.0)
                scale_of(dve, c, scal, big[:, 1:2], S_G, I_G, S_X, 1.0)

            @block.gpsimd
            def _(pool):
                pool.wait_ge(row_max, 2)
                pool.partition_all_reduce(big[:, 0:1], mxu["row"][:], P, RMAX).then_inc(all_max, 1)
                pool.partition_all_reduce(big[:, 1:2], mxg["row"][:], P, RMAX).then_inc(all_max, 1)

            @block.scalar
            def _(act):
                act.sem_inc(max_done, NBANK)
                with act.Fori(0, NCH) as it:
                    for g in range(JOBS):
                        i = g % NBANK
                        act.wait_ge(r_full, JOBS * it + g + 1)
                        act.wait_ge(stored[i], 16 * (JB * it + g // NBANK) + 16)
                        act.wait_ge(max_done, JOBS * it + g + 1)
                        act.activation(stage[:, i, :], pr[i][:], ACT.Copy).then_inc(r_copied, 1)

            @block.sync
            def _(sp):
                for s in stored:
                    sp.sem_inc(s, 16)
                with sp.Fori(0, NCH) as it:
                    for g in range(JOBS):
                        m, i = g // 2, g % NBANK
                        to = (raw_up, raw_gate)[g % 2]
                        sp.wait_ge(r_copied, JOBS * it + g + 1 + NBANK)
                        sp.dma_start(to[bass.ds(it, 1), :, m * CT:(m + 1) * CT].rearrange("a p n -> p (a n)"), stage[:, i, :]).then_inc(stored[i], 16)
                for s in stored:
                    sp.wait_ge(s, 16 * (JB * NCH + 1))

            @block.tensor
            def _(pe):
                pe.sem_inc(t_done, 2)
                pe.sem_inc(r_copied, NBANK)
                with pe.Fori(0, NCH) as it:
                    pe.wait_ge(xq_ready, it + 1)
                    for k in range(KD):
                        pe.wait_ge(t_done, KD * it + k + 1)
                        transpose_job(pe, tp[k % 2], xq, k, ident).then_inc(t_full, 1)
                    for g in range(JOBS):
                        if g == 0:
                            pe.wait_ge(t_done, KD * it + KD + 2)
                        w = (wu, wg)[g % 2]
                        pe.wait_ge(r_copied, JOBS * it + g + 1)
                        for k in range(KD):
                            ins = pe.matmul(pr[g % NBANK][:], w[:, k, (g // 2) * P:(g // 2 + 1) * P], xqT[:, k, :], start=k == 0, stop=k == KD - 1)
                        ins.then_inc(r_full, 1)


def part(raw, it, s):
    return raw[bass.ds(it, 1), :, s * SC:(s + 1) * SC].rearrange("a p n -> p (a n)")


def sigmoid_product(dve, c, sig, sq, prod, gate_part):
    c.done(dve.tensor_scalar(sq, sig, SIGQ, SIGQ - 1, ALU.mult, ALU.min))
    c.wait()
    return dve.tensor_tensor(prod, gate_part, sq, ALU.mult)


def gate_product(nc, raw_gate, gate, big, scal):
    with Phase(nc, "gp") as ph:
        raw = ph.sb("raw", [P, SUB, SC])
        sig = ph.sb("sig", [P, SUB, SC])
        sq = ph.sb("sq", [P, SC], U16)
        prod = ph.sb("prod", [P, SC])
        mx = {"all": ph.sb("mx", [P, NCH * SUB]), "row": ph.sb("mxrow", [P, 1])}
        raw_ready = [ph.sem(f"raw_ready{i}") for i in range(SUB)]
        spacer = ph.sem("spacer")
        gate_ready, sig_ready, steps_done, prod_done, max_done = (ph.sem(n) for n in ("gate_ready", "sig_ready", "steps", "prod_done", "max_done"))
        with nc.Block() as block:
            def settle(dve, c):
                scale_of(dve, c, scal, big[:, 0:1], S_A, I_A, S_G, 1.0 / SIGQ)
            vector_max, pool_max = over_all(nc, block, ph, mx, 0, big, settle, max_done, NCH * SUB)

            @block.sync
            def _(sp):
                sp.sem_inc(gate_ready, SUB)
                with sp.Fori(0, NCH) as it:
                    for s in range(SUB):
                        sp.wait_ge(gate_ready, SUB * it + s + 1)
                        sp.dma_start(raw[:, s, :], part(raw_gate, it, s)).then_inc(raw_ready[s], 16)

            @block.scalar
            def _(act):
                act.sem_inc(prod_done, SUB)
                with act.Fori(0, NCH) as it:
                    for s in range(SUB):
                        g = gate[:, bass.ds(it * (KF * CT) + s * SC, SC)]
                        wait_alone(act, raw_ready[s], 16 * it + 16, spacer)
                        act.activation(g, raw[:, s, :], ACT.Copy, scale=scal[:, I_G:I_G + 1]).then_inc(gate_ready, 1)
                        act.wait_ge(gate_ready, SUB * it + s + 1 + SUB)
                        wait_alone(act, prod_done, SUB * it + s + 1, spacer)
                        act.activation(sig[:, s, :], g, ACT.Sigmoid, scale=scal[:, S_G:S_G + 1]).then_inc(sig_ready, 1)

            @block.vector
            def _(dve):
                with dve.Fori(0, NCH) as it:
                    for s in range(SUB):
                        c = Count(dve, steps_done, SUB * it + s)
                        dve.wait_ge(sig_ready, SUB * it + s + 1)
                        sigmoid_product(dve, c, sig[:, s, :], sq[:], prod[:], gate[:, bass.ds(it * (KF * CT) + s * SC, SC)]).then_inc(prod_done, 1)
                        dve.wait_ge(prod_done, SUB * it + s + 1 + SUB)
                        dve.tensor_reduce(mx["all"][:, bass.ds(it * SUB + s, 1)], prod[:], AX_X, ALU.max, apply_absolute_value=True).then_inc(max_done, 1)
                vector_max(dve)

            @block.gpsimd
            def _(pool):
                pool_max(pool)


def output_maximum(nc, raw_up, gate, big, scal):
    with Phase(nc, "om") as ph:
        raw = ph.sb("raw", [P, SUB, SC])
        sig = ph.sb("sig", [P, 2, SC])
        up = ph.sb("up", [P, 2, SC], I16)
        sq = ph.sb("sq", [P, SC], U16)
        prod = ph.sb("prod", [P, 2, SC])
        mx = {"all": ph.sb("mx", [P, NCH * SUB]), "row": ph.sb("mxrow", [P, 1])}
        raw_ready = [ph.sem(f"raw_ready{i}") for i in range(SUB)]
        up_ready, sig_ready, steps_done, prod_done, gate_ready, out_done, max_done = (
            ph.sem(n) for n in ("up_ready", "sig_ready", "steps", "prod_done", "gate_ready", "out_done", "max_done"))
        spacer = ph.sem("spacer")
        NP2 = NCH * SUB // 2
        with nc.Block() as block:
            def settle(dve, c):
                c.done(dve.tensor_tensor(scal[:, S_AU:S_AU + 1], scal[:, S_A:S_A + 1], scal[:, S_U:S_U + 1], ALU.mult))
                c.wait()
                scale_of(dve, c, scal, big[:, 0:1], S_O, I_O, S_AU, 1.0)
            vector_max, pool_max = over_all(nc, block, ph, mx, 0, big, settle, max_done, NCH * SUB)

            def place(it, s):
                return gate[:, bass.ds(it * (2 * SC) + s * SC, SC)]

            @block.sync
            def _(sp):
                sp.sem_inc(up_ready, 2)
                flat = raw_up.rearrange("c p (s n) -> c p s n", s=SUB)
                with sp.Fori(0, NCH // 2) as it:
                    for r in range(2 * SUB):
                        sp.wait_ge(up_ready, 2 * SUB * it + r + 1)
                        sp.dma_start(raw[:, r % 2, :], part(raw_up, it * 2 + r // SUB, r % SUB)).then_inc(raw_ready[r % 2], 16)

            @block.scalar
            def _(act):
                act.sem_inc(prod_done, 2)
                act.sem_inc(out_done, 2)
                with act.Fori(0, NP2) as it:
                    for s in range(2):
                        wait_alone(act, prod_done, 2 * it + s + 1, spacer)
                        act.activation(sig[:, s, :], place(it, s), ACT.Sigmoid, scale=scal[:, S_G:S_G + 1]).then_inc(sig_ready, 1)
                        act.wait_ge(raw_ready[s], 16 * it + 16)
                        act.wait_ge(out_done, 2 * it + s + 1)
                        act.activation(up[:, s, :], raw[:, s, :], ACT.Copy, scale=scal[:, I_U:I_U + 1]).then_inc(up_ready, 1)
                        wait_alone(act, prod_done, 2 * it + s + 3, spacer)
                        act.activation(place(it, s), prod[:, s, :], ACT.Copy, scale=scal[:, I_A:I_A + 1]).then_inc(gate_ready, 1)

            @block.vector
            def _(dve):
                with dve.Fori(0, NP2) as it:
                    for s in range(2):
                        c = Count(dve, steps_done, 2 * it + s)
                        dve.wait_ge(sig_ready, 2 * it + s + 1)
                        sigmoid_product(dve, c, sig[:, s, :], sq[:], prod[:, s, :], place(it, s)).then_inc(prod_done, 1)
                        dve.wait_ge(gate_ready, 2 * it + s + 1)
                        dve.wait_ge(up_ready, 2 * it + s + 3)
                        dve.tensor_tensor(prod[:, s, :], place(it, s), up[:, s, :], ALU.mult).then_inc(out_done, 1)
                        dve.wait_ge(out_done, 2 * it + s + 3)
                        dve.tensor_reduce(mx["all"][:, bass.ds(it * 2 + s, 1)], prod[:, s, :], AX_X, ALU.max, apply_absolute_value=True).then_inc(max_done, 1)
                vector_max(dve)

            @block.gpsimd
            def _(pool):
                pool_max(pool)


def down(nc, x1, x2, raw_up, gate, wd, scal):
    with Phase(nc, "dn") as ph:
        raw = ph.sb("raw", [P, SUB, SC])
        up = ph.sb("up", [P, SC], I16)
        om = ph.sb("om", [P, SUB, MS, CT])
        xin = ph.sb("xin", [P, NT, D])
        yout = ph.sb("yout", [P, NT, D])
        py = [ph.ps(f"py{i}", [P, D]) for i in range(NT)]
        raw_ready = [ph.sem(f"raw_ready{i}") for i in range(SUB)]
        up_ready, out_done, om_ready, part_used, y_full, y_done, x_ready, stored = (
            ph.sem(n) for n in ("up_ready", "out_done", "om_ready", "part_used", "y_full", "y_done", "x_ready", "stored"))
        steps_done = ph.sem("steps")
        with nc.Block() as block:
            @block.sync
            def _(sp):
                sp.sem_inc(up_ready, SUB)
                sp.sem_inc(y_done, NT)
                with sp.Fori(0, NCH) as it:
                    sp.wait_ge(y_done, NT * it + NT)
                    sp.dma_start(xin[:], tokens(x1, it)).then_inc(x_ready, 16)
                    for s in range(SUB):
                        sp.wait_ge(up_ready, SUB * it + s + 1)
                        sp.dma_start(raw[:, s, :], part(raw_up, it, s)).then_inc(raw_ready[s], 16)

            @block.scalar
            def _(act):
                act.sem_inc(out_done, 1)
                act.sem_inc(stored, 16)
                with act.Fori(0, NCH) as it:
                    for s in range(SUB):
                        act.wait_ge(raw_ready[s], 16 * it + 16)
                        act.wait_ge(out_done, SUB * it + s + 1)
                        act.activation(up[:], raw[:, s, :], ACT.Copy, scale=scal[:, I_U:I_U + 1]).then_inc(up_ready, 1)
                    act.wait_ge(y_done, NT * it + 2 * NT)
                    act.dma_start(tokens(x2, it), yout[:]).then_inc(stored, 16)
                act.wait_ge(stored, 16 * NCH + 16)

            @block.vector
            def _(dve):
                dve.sem_inc(part_used, SUB - 1)
                dve.sem_inc(y_full, NT)
                with dve.Fori(0, NCH) as it:
                    for s in range(SUB):
                        c = Count(dve, steps_done, SUB * it + s)
                        o = om[:, s].rearrange("p m n -> p (m n)")
                        dve.wait_ge(up_ready, SUB * it + s + 1 + SUB)
                        if s < SUB - 1:
                            dve.wait_ge(part_used, (SUB - 1) * it + s + 1)
                        else:
                            dve.wait_ge(y_full, NT * it + NT)
                        dve.tensor_tensor(o, gate[:, bass.ds(it * (KF * CT) + s * SC, SC)], up[:], ALU.mult).then_inc(out_done, 1)
                        dve.wait_ge(out_done, SUB * it + s + 2)
                        c.done(dve.tensor_scalar(o, o, scal[:, I_O:I_O + 1], MAGIC, ALU.mult, ALU.add))
                        c.wait()
                        dve.tensor_scalar(o, o, MAGIC, None, ALU.subtract).then_inc(om_ready, 1)
                    dve.wait_ge(x_ready, 16 * it + 16)
                    dve.wait_ge(stored, 16 * it + 16)
                    for t in range(NT):
                        dve.wait_ge(y_full, NT * it + t + 1 + NT)
                        dve.scalar_tensor_tensor(yout[:, t, :], py[t][:], scal[:, S_O:S_O + 1], xin[:, t, :], ALU.mult, ALU.add).then_inc(y_done, 1)

            @block.tensor
            def _(pe):
                with pe.Fori(0, NCH) as it:
                    for s in range(SUB):
                        pe.wait_ge(om_ready, SUB * it + s + 1)
                        for t in range(NT):
                            if s == 0:
                                pe.wait_ge(y_done, NT * it + t + 1)
                            for m in range(MS):
                                ins = pe.matmul(py[t][:], om[:, s, m, t * P:(t + 1) * P], wd[:, s * MS + m, :],
                                                start=s == 0 and m == 0, stop=s == SUB - 1 and m == MS - 1)
                            if s == SUB - 1:
                                ins.then_inc(y_full, 1)
                        if s < SUB - 1:
                            ins.then_inc(part_used, 1)



def masked_attention(nc, a, x2, ctx_in, x3, ident, neghalf):
    SCALE = D ** -0.5
    JOBS = 3 * KD
    JB = JOBS // 2
    NK = S // P
    with Phase(nc, "ma") as ph:
        gram = ph.sb("gram", [P, KD, D])
        gcol = ph.sb("gcol", [P, KD])
        grow = ph.sb("grow", [P, D])
        bb = ph.sb("bb", [P, 1])
        fold_projections(nc, a, gram, gcol, grow, bb, ident, SCALE)
        mask = ph.sb("mask", [P, NK, S])
        xin = ph.sb("xin", [P, NT, D])
        xkeep = ph.sb("xkeep", [P, NT, D])
        cin = ph.sb("cin", [P, 2, NT, D])
        xn = ph.sb("xn", [P, NT, D])
        junk = ph.sb("junk", [P, D])
        rowc = ph.sb("rowc", [P, NT])
        st = ph.sb("st", [P, NT, 6])
        mv = ph.sb("mv", [P, NT, 2])
        var = ph.sb("var", [P, NT])
        rstd = ph.sb("rstd", [P, NT])
        xT = ph.sb("xT", [P, KD, CT])
        cT = ph.sb("cT", [P, KD, CT])
        rT = ph.sb("rT", [P, KD, CT])
        logit = ph.sb("logit", [P, 2, S])
        nm = ph.sb("nm", [P, 2])
        sums = ph.sb("sums", [P, NT])
        rec = ph.sb("rec", [P, NT])
        prob = ph.sb("prob", [P, 2, S])
        pT = ph.sb("pT", [P, 2, NK, P])
        yout = ph.sb("yout", [P, NT, D])
        pj = [ph.ps(f"pj{i}", [P, CT]) for i in range(2)]
        sc = [ph.ps(f"sc{i}", [P, 512]) for i in range(2)]
        tp = [ph.ps(f"tp{i}", [P, 512]) for i in range(2)]
        po = [ph.ps(f"po{i}", [P, D]) for i in range(2)]
        loaded, x_ready, stored = ph.sem("loaded"), ph.sem("x_ready"), ph.sem("stored")
        c_ready = [ph.sem(f"c_ready{i}") for i in range(2)]
        steps_done, mv_ready, rstd_ready, var_done, xn_ready, rowc_ready, x_kept = (
            ph.sem(n) for n in ("steps", "mv_ready", "rstd_ready", "var_done", "xn_ready", "rowc_ready", "x_kept"))
        spacer_d, spacer_p = ph.sem("spacer_d"), ph.sem("spacer_p")
        job_full = ph.sem("job_full")
        job_done = [ph.sem(f"job_done{i}") for i in range(2)]
        s_full, logit_done, max_done, exp_done, rec_done, t_full, pt_done, o_full, o_done = (
            ph.sem(n) for n in ("s_full", "logit_done", "max_done", "exp_done", "rec_done", "t_full", "pt_done", "o_full", "o_done"))
        block = ph.block()
        NIT = NCH // 2

        @block.sync
        def _(sp):
            sp.dma_start(mask[:], a["fside_1xSxS2_0"].rearrange("o (m p) s -> p (o m) s", p=P)).then_inc(loaded, 16)
            sp.sem_inc(x_kept, 1)
            sp.sem_inc(xn_ready, 1)
            sp.sem_inc(o_full, 2 * NT)
            with sp.Fori(0, NIT) as it:
                for h in range(2):
                    sp.wait_ge(xn_ready, 2 * it + h + 1)
                    sp.wait_ge(x_kept, 2 * it + h + 1)
                    sp.dma_start(xin[:], tokens(x2, 2 * it + h)).then_inc(x_ready, 16)
                    sp.wait_ge(o_full, NT * (2 * it + h) + NT)
                    sp.dma_start(cin[:, h], tokens(ctx_in, 2 * it + h)).then_inc(c_ready[h], 16)

        @block.gpsimd
        def _(pool):
            with pool.Fori(0, NIT) as it:
                for h in range(2):
                    n = 2 * it + h
                    norm_rstd(pool, mv, var, rstd, neghalf, mv_ready, rstd_ready, var_done, n, spacer_p)
                    wait_alone(pool, o_done, NT * n + 2, spacer_p)
                    pool.tensor_copy(xkeep[:], xin[:]).then_inc(x_kept, 1)

        @block.vector
        def _(dve):
            dve.wait_ge(loaded, 16)
            with dve.Fori(0, NIT) as it:
                for h in range(2):
                    n = 2 * it + h
                    steps = Count(dve, steps_done, NT * n)
                    dve.wait_ge(x_ready, 16 * n + 16)
                    norm_stats(dve, st, mv, steps, mv_ready, spacer_d, xin)
                    dve.wait_ge(rstd_ready, n + 1)
                    norm_rows(dve, xn, xin, mv, rstd).then_inc(xn_ready, 1)
                    dve.wait_ge(xn_ready, n + 2)
                    for t in range(NT):
                        ins = dve.tensor_tensor_reduce(junk[:], xn[:, t, :], grow[:], SCALE, bb[:, 0:1], ALU.mult, ALU.add, rowc[:, t:t + 1])
                        ins.then_inc(rowc_ready, 1)
                        dve.wait_ge(rowc_ready, NT * n + t + 1)
                    for k in range(KD):
                        g = KD + k
                        dve.wait_ge(job_full, JOBS * n + g + 1)
                        dve.tensor_copy(cT[:, k, :], pj[g % 2][:]).then_inc(job_done[g % 2], 1)
                    for t in range(NT + 2):
                        i = t % 2
                        if t < NT:
                            dve.wait_ge(s_full, NT * n + t + 1)
                            dve.wait_ge(exp_done, NT * n + t + 1)
                            dve.scalar_tensor_tensor(logit[:, i, :], sc[i][:, 0:S], rowc[:, t:t + 1], mask[:, t % NK, :], ALU.add, ALU.add).then_inc(logit_done, 1)
                            dve.wait_ge(logit_done, NT * n + t + 3)
                            dve.tensor_reduce(nm[:, i:i + 1], logit[:, i, :], AX_X, ALU.max, negate=True).then_inc(max_done, 1)
                        if 0 < t <= NT:
                            u = t - 1
                            dve.wait_ge(exp_done, NT * n + u + 3)
                            dve.reciprocal(rec[:, u:u + 1], sums[:, u:u + 1]).then_inc(rec_done, 1)
                            dve.wait_ge(t_full, NT * n + u + 3)
                            dve.wait_ge(o_full, NT * n + u - 1 + 2 * NT)
                            dve.tensor_copy(pT[:, u % 2].rearrange("p c n -> p (c n)"), tp[u % 2][:, 0:S]).then_inc(pt_done, 1)
                        if t > 1:
                            u = t - 2
                            dve.wait_ge(o_full, NT * n + u + 1 + 2 * NT)
                            if u == 0:
                                dve.wait_ge(x_kept, n + 2)
                                dve.wait_ge(stored, 16 * n + 16)
                            dve.wait_ge(rec_done, NT * n + u + 1)
                            dve.scalar_tensor_tensor(yout[:, u, :], po[u % 2][:], rec[:, u:u + 1], xkeep[:, u, :], ALU.mult, ALU.add).then_inc(o_done, 1)

        @block.scalar
        def _(act):
            act.sem_inc(stored, 16)
            act.sem_inc(t_full, 2)
            with act.Fori(0, NIT) as it:
                for h in range(2):
                    n = 2 * it + h
                    for k in range(KD):
                        act.wait_ge(job_full, JOBS * n + k + 1)
                        act.activation(xT[:, k, :], pj[k % 2][:], ACT.Copy).then_inc(job_done[k % 2], 1)
                    for k in range(KD):
                        g = 2 * KD + k
                        act.wait_ge(job_full, JOBS * n + g + 1)
                        act.activation(rT[:, k, :], pj[g % 2][:], ACT.Identity, bias=gcol[:, k:k + 1], scale=SCALE).then_inc(job_done[g % 2], 1)
                    for t in range(NT):
                        i = t % 2
                        act.wait_ge(max_done, NT * n + t + 1)
                        act.wait_ge(t_full, NT * n + t + 1)
                        act.activation(prob[:, i, :], logit[:, i, :], ACT.Exp, bias=nm[:, i:i + 1], accum_out=sums[:, t:t + 1]).then_inc(exp_done, 1)
                    act.wait_ge(o_done, NT * n + NT + 2)
                    act.dma_start(tokens(x3, n), yout[:]).then_inc(stored, 16)
            act.wait_ge(stored, 16 * NCH + 16)

        @block.tensor
        def _(pe):
            for s in job_done:
                pe.sem_inc(s, 1)
            pe.sem_inc(exp_done, 2)
            pe.sem_inc(logit_done, 2)
            pe.sem_inc(pt_done, 2)
            pe.sem_inc(o_done, 2)
            with pe.Fori(0, NIT) as it:
                for h in range(2):
                    n = 2 * it + h

                    def free(g):
                        pe.wait_ge(job_done[g % 2], JB * n + g // 2 + 1)

                    def taken(g):
                        pe.wait_ge(job_done[g % 2], JB * n + g // 2 + 2)

                    pe.wait_ge(xn_ready, n + 2)
                    for g in range(KD):
                        free(g)
                        transpose_job(pe, pj[g % 2], xn, g, ident).then_inc(job_full, 1)
                    pe.wait_ge(c_ready[h], 16 * it + 16)
                    for g in range(KD, 2 * KD):
                        free(g)
                        transpose_job(pe, pj[g % 2], cin[:, h], g - KD, ident).then_inc(job_full, 1)
                    taken(KD - 2)
                    taken(KD - 1)
                    for m in range(KD):
                        g = 2 * KD + m
                        free(g)
                        for k in range(KD):
                            ins = pe.matmul(pj[g % 2][:], gram[:, k, m * P:(m + 1) * P], xT[:, k, :], start=k == 0, stop=k == KD - 1)
                        ins.then_inc(job_full, 1)
                    taken(JOBS - 2)
                    taken(JOBS - 1)
                    for t in range(NT + 2):
                        if t < NT:
                            b = t // NK
                            pe.wait_ge(logit_done, NT * n + t + 1)
                            for k in range(KD):
                                ins = pe.matmul(sc[t % 2][:, 0:S], rT[:, k, t * P:(t + 1) * P], cT[:, k, b * S:(b + 1) * S], start=k == 0, stop=k == KD - 1)
                            ins.then_inc(s_full, 1)
                        if 0 < t <= NT:
                            u = t - 1
                            pe.wait_ge(exp_done, NT * n + u + 3)
                            pe.wait_ge(pt_done, NT * n + u + 1)
                            for c in range(NK):
                                ins = pe.transpose(tp[u % 2][:, c * P:(c + 1) * P], prob[:, u % 2, c * P:(c + 1) * P], ident[:])
                            ins.then_inc(t_full, 1)
                        if t > 1:
                            u = t - 2
                            pe.wait_ge(pt_done, NT * n + u + 3)
                            pe.wait_ge(o_done, NT * n + u + 1)
                            for c in range(NK):
                                ins = pe.matmul(po[u % 2][:], pT[:, u % 2, c, :], cin[:, h, (u // NK) * NK + c, :], start=c == 0, stop=c == NK - 1)
                            ins.then_inc(o_full, 1)


def fold_projections(nc, a, gram, gcol, grow, bb, ident, scale):
    with Phase(nc, "fp") as ph:
        w1 = ph.sb("w1", [P, KD, D])
        w2 = ph.sb("w2", [P, KD, D])
        w2T = ph.sb("w2T", [P, KD, D])
        b12 = ph.sb("b12", [P, 2, KD])
        m = ph.sb("m", [P, KD, D])
        beta = ph.sb("beta", [P, KD])
        ones = ph.sb("ones", [P, P])
        betas = ph.sb("betas", [P, KD, P])
        pw = [ph.ps(f"pw{i}", [P, D]) for i in range(4)]
        pc = [ph.ps(f"pc{i}", [P, D]) for i in range(4)]
        loaded, turned, turned_out, m_full, m_out, beta_full, beta_out, betas_out, done = (
            ph.sem(n) for n in ("loaded", "turned", "turned_out", "m_full", "m_out", "beta_full", "beta_out", "betas_out", "done"))
        g_full, g_out = ph.sem("g_full"), ph.sem("g_out")
        ones_made = ph.sem("ones_made")
        with nc.Block() as block:
            @block.sync
            def _(sp):
                sp.dma_start(w1[:], a["L1_xattn_W1"].rearrange("(k p) n -> p k n", p=P)).then_inc(loaded, 16)
                sp.dma_start(w2[:], a["L1_xattn_W2"].rearrange("(k p) n -> p k n", p=P)).then_inc(loaded, 16)
                sp.dma_start(b12[:, 0, :], a["L1_xattn_b1"].rearrange("(k p) -> p k", p=P), allow_slow_non_contiguous=True).then_inc(loaded, 16)
                sp.dma_start(b12[:, 1, :], a["L1_xattn_b2"].rearrange("(k p) -> p k", p=P), allow_slow_non_contiguous=True).then_inc(loaded, 16)

            @block.gpsimd
            def _(pool):
                pool.memset(ones[:], 1.0).then_inc(ones_made, 1)

            @block.tensor
            def _(pe):
                pe.wait_ge(loaded, 64)
                for k in range(KD):
                    for t in range(KD):
                        ins = pe.transpose(pw[k][:, t * P:(t + 1) * P], w2[:, t, k * P:(k + 1) * P], ident[:])
                    ins.then_inc(turned, 1)
                pe.wait_ge(turned_out, KD)
                for o in range(KD):
                    for k in range(KD):
                        ins = pe.matmul(pw[o][:], w2T[:, k, o * P:(o + 1) * P], w1[:, k, :], start=k == 0, stop=k == KD - 1)
                    ins.then_inc(m_full, 1)
                for o in range(KD):
                    for k in range(KD):
                        ins = pe.matmul(pc[0][:, o:o + 1], w2T[:, k, o * P:(o + 1) * P], b12[:, 0, k:k + 1], start=k == 0, stop=k == KD - 1)
                ins.then_inc(beta_full, 1)
                pe.wait_ge(m_out, KD)
                for d in range(KD):
                    for o in range(KD):
                        ins = pe.matmul(pw[d][:], m[:, o, d * P:(d + 1) * P], m[:, o, :], start=o == 0, stop=o == KD - 1)
                    ins.then_inc(g_full, 1)
                pe.wait_ge(betas_out, KD)
                for d in range(KD):
                    for o in range(KD):
                        ins = pe.matmul(pc[1][:, d:d + 1], m[:, o, d * P:(d + 1) * P], beta[:, o:o + 1], start=o == 0, stop=o == KD - 1)
                for o in range(KD):
                    ins = pe.matmul(pc[2][:], betas[:, o, :], m[:, o, :], start=o == 0, stop=o == KD - 1)
                for o in range(KD):
                    ins = pe.matmul(pc[3][:, 0:1], betas[:, o, :], beta[:, o:o + 1], start=o == 0, stop=o == KD - 1)
                ins.then_inc(g_full, 1)

            @block.scalar
            def _(act):
                for k in range(KD):
                    act.wait_ge(turned, k + 1)
                    act.activation(w2T[:, k, :], pw[k][:], ACT.Copy).then_inc(turned_out, 1)
                for o in range(KD):
                    act.wait_ge(m_full, o + 1)
                    act.activation(m[:, o, :], pw[o][:], ACT.Copy).then_inc(m_out, 1)
                for d in range(KD):
                    act.wait_ge(g_full, d + 1)
                    act.activation(gram[:, d, :], pw[d][:], ACT.Copy).then_inc(g_out, 1)

            @block.vector
            def _(dve):
                dve.wait_ge(beta_full, 1)
                dve.tensor_tensor(beta[:], pc[0][:, 0:KD], b12[:, 1, :], ALU.add).then_inc(beta_out, 1)
                dve.wait_ge(beta_out, 1)
                dve.wait_ge(ones_made, 1)
                for o in range(KD):
                    dve.tensor_scalar(betas[:, o, :], ones[:], beta[:, o:o + 1], None, ALU.mult).then_inc(betas_out, 1)
                dve.wait_ge(g_full, KD + 1)
                dve.tensor_scalar(gcol[:], pc[1][:, 0:KD], scale, None, ALU.mult).then_inc(done, 1)
                dve.tensor_copy(grow[:], pc[2][:]).then_inc(done, 1)
                dve.tensor_scalar(bb[:], pc[3][:, 0:1], scale, None, ALU.mult).then_inc(done, 1)
                dve.wait_ge(done, 3)


def lora_ffn(nc, a, x3, out, ident, neghalf):
    SCALING = 1.0 / R
    HB = 4
    JOBS = KD + 4
    HJ = KH + NT
    Z1, ZT1, Z2, ZT2 = range(KD, KD + 4)
    with Phase(nc, "lf") as ph:
        w1 = ph.sb("w1", [P, KD, H2])
        w2 = ph.sb("w2", [P, KH, D])
        ra1 = ph.sb("ra1", [P, KD, LZ])
        ra2 = ph.sb("ra2", [P, KH, LZ])
        lb1 = ph.sb("lb1", [P, H2])
        lb2 = ph.sb("lb2", [P, D])
        b1 = ph.sb("b1", [P, KH])
        b2 = ph.sb("b2", [P, D])
        xin = ph.sb("xin", [P, NT, D])
        xres = ph.sb("xres", [P, NT, D])
        xn = ph.sb("xn", [P, NT, D])
        st = ph.sb("st", [P, NT, 6])
        mv = ph.sb("mv", [P, NT, 2])
        var = ph.sb("var", [P, NT])
        rstd = ph.sb("rstd", [P, NT])
        xT = ph.sb("xT", [P, KD, CT])
        hT = ph.sb("hT", [P, KH, CT])
        z = ph.sb("z", [P, NT, LZ])
        zmax = ph.sb("zmax", [P, NT])
        zsum = ph.sb("zsum", [P, NT])
        zrec = ph.sb("zrec", [P, NT])
        gl = ph.sb("gl", [P, NT, E])
        ge = ph.sb("ge", [P, NT, E])
        zg = ph.sb("zg", [P, NT, P])
        zgT = ph.sb("zgT", [P, CT])
        yout = ph.sb("yout", [P, NT, D])
        pj = [ph.ps(f"pj{i}", [P, CT]) for i in range(2)]
        pz = ph.ps("pz", [P, 512])
        hb = [ph.ps(f"hb{i}", [P, CT]) for i in range(HB)]
        loaded, x_ready, stored, cleared = ph.sem("loaded"), ph.sem("x_ready"), ph.sem("stored"), ph.sem("cleared")
        steps_done, mv_ready, rstd_ready, var_done, xn_ready, res_ready = (
            ph.sem(n) for n in ("steps", "mv_ready", "rstd_ready", "var_done", "xn_ready", "res_ready"))
        spacer_d, spacer_p = ph.sem("spacer_d"), ph.sem("spacer_p")
        job_full = ph.sem("job_full")
        job_done = [ph.sem(f"job_done{i}") for i in range(2)]
        h_full = ph.sem("h_full")
        h_done = [ph.sem(f"h_done{i}") for i in range(HB)]
        mix_steps, gl_ready, ge_ready, zg_ready = (ph.sem(n) for n in ("mix_steps", "gl_ready", "ge_ready", "zg_ready"))
        MIX = 5
        NLOAD = 2 + 2 * (1 + E) + 4
        block = ph.block()

        @block.sync
        def _(sp):
            def load(to, src):
                sp.dma_start(to, src, allow_slow_non_contiguous=True).then_inc(loaded, 16)

            load(w1[:], a["L1_ffn_W1"].rearrange("(k p) n -> p k n", p=P))
            load(w2[:], a["L1_ffn_W2"].rearrange("(k p) n -> p k n", p=P))
            for ra, r, low in ((ra1, "L1_ffn_R1", "L1_ffn_A1"), (ra2, "L1_ffn_R2", "L1_ffn_A2")):
                load(ra[:, :, 0:E], a[r].rearrange("(k p) e -> p k e", p=P))
                for e in range(E):
                    load(ra[:, :, E + e * R:E + (e + 1) * R], a[low][e].rearrange("(k p) r -> p k r", p=P))
            sp.wait_ge(cleared, 2)
            load(lb1[0:ER, :], a["L1_ffn_B1"].rearrange("e r n -> (e r) n"))
            load(lb2[0:ER, :], a["L1_ffn_B2"].rearrange("e r n -> (e r) n"))
            load(b1[:], a["L1_ffn_b1"].rearrange("(k p) -> p k", p=P))
            load(b2[:], a["L1_ffn_b2"].rearrange("(o n) -> o n", o=1).broadcast_to([P, D]))
            sp.sem_inc(xn_ready, 1)
            sp.sem_inc(res_ready, 1)
            with sp.Fori(0, NCH) as it:
                sp.wait_ge(xn_ready, it + 1)
                sp.wait_ge(res_ready, it + 1)
                sp.dma_start(xin[:], tokens(x3, it)).then_inc(x_ready, 16)

        @block.gpsimd
        def _(pool):
            pool.memset(lb1[:], 0.0).then_inc(cleared, 1)
            pool.memset(lb2[:], 0.0).then_inc(cleared, 1)
            pool.memset(zg[:], 0.0).then_inc(cleared, 1)
            pool.wait_ge(loaded, 16 * NLOAD)
            with pool.Fori(0, NCH) as it:
                norm_rstd(pool, mv, var, rstd, neghalf, mv_ready, rstd_ready, var_done, it, spacer_p)
                for s in h_done:
                    wait_alone(pool, s, (HJ // HB) * it + 1, spacer_p)
                for t in range(NT):
                    ins = pool.tensor_tensor(xres[:, t, :], xin[:, t, :], b2[:], ALU.add)
                ins.then_inc(res_ready, 1)

        @block.vector
        def _(dve):
            dve.wait_ge(cleared, 3)
            with dve.Fori(0, NCH) as it:
                steps = Count(dve, steps_done, NT * it)
                dve.wait_ge(x_ready, 16 * it + 16)
                norm_stats(dve, st, mv, steps, mv_ready, spacer_d, xin)
                dve.wait_ge(rstd_ready, it + 1)
                norm_rows(dve, xn, xin, mv, rstd).then_inc(xn_ready, 1)

                def mixture(layer, g):
                    c = Count(dve, mix_steps, 2 * MIX * it + layer * MIX)
                    dve.wait_ge(job_full, JOBS * it + g + 1)
                    c.done(dve.tensor_copy(z[:].rearrange("p t n -> p (t n)"), pz[:, 0:NT * LZ]))
                    c.wait()
                    c.done(dve.tensor_reduce(zmax[:], z[:, :, 0:E], AX_X, ALU.max))
                    c.wait()
                    dve.tensor_tensor(gl[:], z[:, :, 0:E], zmax[:].unsqueeze(2).broadcast_to([P, NT, E]), ALU.subtract).then_inc(gl_ready, 1)
                    dve.wait_ge(ge_ready, 2 * it + layer + 1)
                    c.done(dve.tensor_reduce(zsum[:], ge[:], AX_X, ALU.add))
                    c.wait()
                    c.done(dve.reciprocal(zrec[:], zsum[:]))
                    c.wait()
                    c.done(dve.scalar_tensor_tensor(gl[:], ge[:], SCALING, zrec[:].unsqueeze(2).broadcast_to([P, NT, E]), ALU.mult, ALU.mult))
                    c.wait()
                    assert c.n == MIX
                    for t in range(NT):
                        ins = dve.tensor_tensor(zg[:, t, 0:ER].rearrange("p (e r) -> p e r", e=E), z[:, t, E:LZ].rearrange("p (e r) -> p e r", e=E),
                                                gl[:, t, :].unsqueeze(2).broadcast_to([P, E, R]), ALU.mult)
                    ins.then_inc(zg_ready, 1)

                mixture(0, Z1)
                mixture(1, Z2)
                for t in range(NT):
                    g = KH + t
                    dve.wait_ge(h_full, HJ * it + g + 1)
                    if t == 0:
                        dve.wait_ge(res_ready, it + 2)
                        dve.wait_ge(stored, 16 * it + 16)
                    dve.tensor_tensor(yout[:, t, :], hb[g % HB][:], xres[:, t, :], ALU.add).then_inc(h_done[g % HB], 1)

        @block.scalar
        def _(act):
            act.sem_inc(stored, 16)
            act.wait_ge(loaded, 16 * NLOAD)
            with act.Fori(0, NCH) as it:
                for k in range(KD):
                    act.wait_ge(job_full, JOBS * it + k + 1)
                    act.activation(xT[:, k, :], pj[k % 2][:], ACT.Copy).then_inc(job_done[k % 2], 1)

                def exps(layer):
                    act.wait_ge(gl_ready, 2 * it + layer + 1)
                    act.activation(ge[:], gl[:], ACT.Exp).then_inc(ge_ready, 1)

                def turned(g):
                    act.wait_ge(job_full, JOBS * it + g + 1)
                    bank = 1 if g == ZT1 else 0
                    act.activation(zgT[:], pj[bank][:], ACT.Copy).then_inc(job_done[bank], 1)

                exps(0)
                turned(ZT1)
                for m in range(KH):
                    act.wait_ge(h_full, HJ * it + m + 1)
                    act.activation(hT[:, m, :], hb[m % HB][:], ACT.Relu, bias=b1[:, m:m + 1]).then_inc(h_done[m % HB], 1)
                exps(1)
                turned(ZT2)
                for s in h_done:
                    act.wait_ge(s, (HJ // HB) * it + HJ // HB + 1)
                act.dma_start(tokens(out, it), yout[:]).then_inc(stored, 16)
            act.wait_ge(stored, 16 * NCH + 16)

        @block.tensor
        def _(pe):
            for s in (*job_done, *h_done):
                pe.sem_inc(s, 1)
            pe.wait_ge(loaded, 16 * NLOAD)
            pe.wait_ge(cleared, 3)
            JB, HN = (KD + 2) // 2, HJ // HB
            with pe.Fori(0, NCH) as it:
                def free(bank, nth):
                    pe.wait_ge(job_done[bank], JB * it + nth + 1)

                def taken(bank, nth):
                    pe.wait_ge(job_done[bank], JB * it + nth + 2)

                def h_free(g):
                    pe.wait_ge(h_done[g % HB], HN * it + g // HB + 1)

                def h_taken(g):
                    pe.wait_ge(h_done[g % HB], HN * it + g // HB + 2)

                def projections(src, ra, kn):
                    for t in range(NT):
                        for k in range(kn):
                            ins = pe.matmul(pz[:, t * LZ:(t + 1) * LZ], src[:, k, t * P:(t + 1) * P], ra[:, k, :], start=k == 0, stop=k == kn - 1)
                    ins.then_inc(job_full, 1)

                def turn_mixture(layer, bank, nth):
                    pe.wait_ge(zg_ready, 2 * it + layer + 1)
                    free(bank, nth)
                    for t in range(NT):
                        ins = pe.transpose(pj[bank][:, t * P:(t + 1) * P], zg[:, t, :], ident[:])
                    ins.then_inc(job_full, 1)

                pe.wait_ge(xn_ready, it + 2)
                for g in range(KD):
                    free(g % 2, g // 2)
                    transpose_job(pe, pj[g % 2], xn, g, ident).then_inc(job_full, 1)
                taken(0, 1)
                taken(1, 1)
                projections(xT, ra1, KD)
                LAG = HB - 1
                for m in range(KH + LAG):
                    if m < KH:
                        h_free(m)
                        for k in range(KD):
                            pe.matmul(hb[m % HB][:], w1[:, k, m * P:(m + 1) * P], xT[:, k, :], start=k == 0, stop=False)
                    if m == LAG - 1:
                        turn_mixture(0, 1, 2)
                    if m >= LAG:
                        u = m - LAG
                        if u == 0:
                            taken(1, 2)
                        pe.matmul(hb[u % HB][:], lb1[:, u * P:(u + 1) * P], zgT[:], start=False, stop=True).then_inc(h_full, 1)
                for m in range(KH - HB, KH):
                    h_taken(m)
                projections(hT, ra2, KH)
                for t in range(NT):
                    h_free(KH + t)
                    for k in range(KH):
                        pe.matmul(hb[(KH + t) % HB][:], hT[:, k, t * P:(t + 1) * P], w2[:, k, :], start=k == 0, stop=False)
                    if t == 1:
                        turn_mixture(1, 0, 2)
                taken(0, 2)
                for t in range(NT):
                    pe.matmul(hb[(KH + t) % HB][:], zgT[:, t * P:(t + 1) * P], lb2[:], start=False, stop=True).then_inc(h_full, 1)


_INS = ['x', 'ctx_1024', 'fside_1xSxS2_0', 'L0_xattn_Wq', 'L0_xattn_Wk', 'L0_xattn_Wv', 'L0_xattn_Wk_ip', 'L0_xattn_Wv_ip',
        'L0_xattn_Wo', 'L0_xattn_bo', 'L0_ffn_w_gate', 'L0_ffn_w_up', 'L0_ffn_w_down', 'L1_xattn_W1', 'L1_xattn_b1',
        'L1_xattn_W2', 'L1_xattn_b2', 'L1_ffn_W1', 'L1_ffn_b1', 'L1_ffn_A1', 'L1_ffn_B1', 'L1_ffn_R1', 'L1_ffn_W2',
        'L1_ffn_b2', 'L1_ffn_A2', 'L1_ffn_B2', 'L1_ffn_R2']
_OUTS = [((B, S, D), 'float32')]


def kernel(**inputs):
    import numpy as _np
    import concourse.bacc as _bacc
    from concourse import mybir as _mybir
    from concourse.bass_utils import run_bass_kernel_spmd as _run

    nc = _bacc.Bacc("TRN2", target_bir_lowering=False, num_devices=1)
    arrays, args = {}, {}
    for name in _INS:
        a = _np.ascontiguousarray(inputs[name])
        arrays[f"in_{name}_dram"] = a
        args[name] = nc.dram_tensor(f"in_{name}_dram", a.shape, _mybir.dt.from_np(a.dtype), kind="ExternalInput").ap()
    outs = []
    for i, (shape, dtype) in enumerate(_OUTS):
        outs.append(nc.dram_tensor(f"out_{i}_dram", shape, _mybir.dt.from_np(_np.dtype(dtype)), kind="ExternalOutput").ap())
    kernel_program(nc, args, outs[0])
    r = _run(nc, [arrays], core_ids=[0])
    return r.results[0]["out_0_dram"]
```

```python
from contextlib import ExitStack

import concourse.bass as bass
from concourse import mybir

ALU = mybir.AluOpType
ACT = mybir.ActivationFunctionType
F32 = mybir.dt.float32
F32R = mybir.dt.float32r
I16 = mybir.dt.int16
U16 = mybir.dt.uint16
AX_X = mybir.AxisListType.X
RMAX = bass.bass_isa.ReduceOp.max

P = 128
B, S, D = 16, 256, 512
TOK = B * S
CT = 512
NCH = TOK // CT
NT = CT // P
KD = D // P
NB = CT // S
EPS = 1e-5

HEADS, DH = 16, 64
INNER = HEADS * DH
TEXT = 77
NPAIR = HEADS // 2

FF = 1536
KF = FF // P
QB = 32
WMAX = 7.0
AMAX = 32767.0
TINY = 1e-12
SIGQ = 65536.0
MAGIC = 12582912.0

H2 = 2048
KH = H2 // P
E, R = 3, 8
ER = E * R
LZ = E + ER


class Count:

    def __init__(self, eng, sem, base=0):
        self.eng, self.sem, self.base, self.n = eng, sem, base, 0

    def done(self, ins):
        ins.then_inc(self.sem, 1)
        self.n += 1
        return self.n

    def wait(self, n=None):
        self.eng.wait_ge(self.sem, self.base + (self.n if n is None else n))


class Phase:

    def __init__(self, nc, name):
        self.nc, self.name, self.ctx = nc, name, ExitStack()
        self.sems, self.blocks = [], ExitStack()

    def __enter__(self):
        self.ctx.__enter__()
        return self

    def __exit__(self, *a):
        self.blocks.close()
        if self.sems:
            with self.nc.Block() as block:
                @block.sync
                def _(sp):
                    for s in self.sems:
                        sp.sem_clear(s)
        return self.ctx.__exit__(*a)

    def block(self):
        return self.blocks.enter_context(self.nc.Block())

    def sb(self, name, shape, dt=F32):
        return self.ctx.enter_context(self.nc.sbuf_tensor(f"{self.name}_{name}", shape, dt))

    def ps(self, name, shape):
        return self.ctx.enter_context(self.nc.psum_tensor(f"{self.name}_{name}", shape, F32))

    def sem(self, name):
        self.sems.append(self.ctx.enter_context(self.nc.semaphore(f"{self.name}_{name}")))
        return self.sems[-1]


def wait_alone(eng, sem, value, spacer):
    eng.wait_ge(sem, value)
    eng.sem_inc(spacer, 1)


def tokens(ap, c):
    return ap[bass.ds(c * CT, CT), :].rearrange("(t p) d -> p t d", p=P)


def flat3(ap):
    return ap.rearrange("b s d -> (b s) d")


def kernel_program(nc, a, out):
    x_in, ctx_in, out_f = flat3(a["x"]), flat3(a["ctx_1024"]), flat3(out)
    x1 = nc.dram_tensor("x1", (TOK, D), F32).ap()
    x2 = nc.dram_tensor("x2", (TOK, D), F32).ap()
    x3 = nc.dram_tensor("x3", (TOK, D), F32).ap()
    raw_up = nc.dram_tensor("raw_up", (NCH, P, KF * CT), F32).ap()
    raw_gate = nc.dram_tensor("raw_gate", (NCH, P, KF * CT), F32).ap()
    with ExitStack() as top:
        ident = top.enter_context(nc.sbuf_tensor("ident", [P, P], F32))
        neghalf = top.enter_context(nc.sbuf_tensor("neghalf", [P, NT], F32))
        consts(nc, ident, neghalf)
        cross_attention(nc, a, x_in, ctx_in, x1, ident, neghalf)
        quantized_ffn(nc, a, x1, x2, raw_up, raw_gate, ident, neghalf)
        masked_attention(nc, a, x2, ctx_in, x3, ident, neghalf)
        lora_ffn(nc, a, x3, out_f, ident, neghalf)


def consts(nc, ident, neghalf):
    with Phase(nc, "c0") as ph:
        cleared = ph.sem("cleared")
        made = ph.sem("made")
        with nc.Block() as block:
            @block.gpsimd
            def _(pool):
                pool.memset(neghalf[:], -0.5).then_inc(made, 1)
                pool.memset(ident[:], 0.0).then_inc(cleared, 1)
                pool.wait_ge(cleared, 1)
                pool.affine_select(out=ident[:], in_=ident[:], compare_op=ALU.not_equal, fill=1.0, base=0,
                                   pattern=[[-1, P]], channel_multiplier=1).then_inc(made, 1)
                pool.wait_ge(made, 2)



def norm_stats(dve, st, mv, steps, mv_ready, spacer, x):
    for t in range(NT):
        n = steps.done(dve.bn_stats(st[:, t, :], x[:, t, :]))
    steps.eng.wait_ge(steps.sem, steps.base + n)
    dve.sem_inc(spacer, 1)
    for t in range(NT):
        ins = dve.bn_aggr(mv[:, t, :], st[:, t, :])
    ins.then_inc(mv_ready, 1)


def norm_rstd(pool, mv, var, rstd, neghalf, mv_ready, rstd_ready, var_done, it, spacer):
    wait_alone(pool, mv_ready, it + 1, spacer)
    pool.tensor_scalar(var[:], mv[:, :, 1], EPS, None, ALU.add).then_inc(var_done, 1)
    pool.wait_ge(var_done, it + 1)
    pool.tensor_tensor(rstd[:], var[:], neghalf[:], ALU.pow).then_inc(rstd_ready, 1)


def norm_rows(dve, xn, x, mv, rstd):
    for t in range(NT):
        ins = dve.tensor_scalar(xn[:, t, :], x[:, t, :], mv[:, t, 0:1], rstd[:, t:t + 1], ALU.subtract, ALU.mult)
    return ins


def transpose_job(pe, bank, src, k, ident):
    for t in range(NT):
        ins = pe.transpose(bank[:, t * P:(t + 1) * P], src[:, t, k * P:(k + 1) * P], ident[:])
    return ins


def product(pe, out, left, right, start, stop, check=True):
    (lh, ll), (rh, rl) = left, right
    kw = {} if check else {"skip_group_check": True}
    pe.matmul(out, lh, rh, start=start, stop=False, **kw)
    pe.matmul(out, lh, rl, start=False, stop=False, **kw)
    return pe.matmul(out, ll, rh, start=False, stop=stop, **kw)


def cross_attention(nc, a, x_in, ctx_in, x1, ident, neghalf):
    JOBS = 2 * KD + 3 * NPAIR + NT
    JB = JOBS // 2
    U = NB * HEADS
    SEG = [(0, TEXT), (TEXT, S)]
    XT0, CT0, PR0, OU0 = 0, KD, 2 * KD, 2 * KD + 3 * NPAIR
    with Phase(nc, "xa") as ph:
        w = {n: ph.sb(n, [P, KD, INNER]) for n in ("Wq", "Wk", "Wv", "Wk_ip", "Wv_ip")}
        wo = ph.sb("Wo", [P, NPAIR, D])
        bo = ph.sb("bo", [P, D])
        xin = ph.sb("xin", [P, NT, D])
        cin = ph.sb("cin", [P, NT, D])
        xres = ph.sb("xres", [P, NT, D])
        xn = ph.sb("xn", [P, NT, D])
        st = ph.sb("st", [P, NT, 6])
        mv = ph.sb("mv", [P, NT, 2])
        var = ph.sb("var", [P, NT])
        rstd = ph.sb("rstd", [P, NT])
        xT = ph.sb("xT", [P, KD, CT])
        cT = ph.sb("cT", [P, KD, CT])
        cimg = ph.sb("cimg", [P, KD, NB, P])
        qT = ph.sb("qT", [P, 2, CT])
        kT = ph.sb("kT", [P, 2, CT])
        v = ph.sb("v", [P, 2, 2 * NB, P])
        nm = ph.sb("nm", [P, 2, 2, 2])
        sums = ph.sb("sums", [P, 2, 2, 2])
        rec = ph.sb("rec", [P, 2, 2, 2])
        prob = ph.sb("prob", [P, 2, 2, S])
        pT = ph.sb("pT", [P, 2, 2, S])
        oT = ph.sb("oT", [P, NPAIR, CT])
        yout = ph.sb("yout", [P, NT, D])
        pj = [ph.ps(f"pj{i}", [P, CT]) for i in range(2)]
        sc = [ph.ps(f"sc{i}", [P, 2, S]) for i in range(2)]
        tp = [ph.ps(f"tp{i}", [P, 2, S]) for i in range(2)]
        po = [ph.ps(f"po{i}", [P, 512]) for i in range(2)]
        loaded = ph.sem("weights")
        x_ready, c_ready, stored = ph.sem("x_ready"), ph.sem("c_ready"), ph.sem("stored")
        c_used, res_ready = ph.sem("c_used"), ph.sem("res_ready")
        cimg_clear, var_done = ph.sem("cimg_clear"), ph.sem("var_done")
        steps_done, mv_ready, rstd_ready, xn_ready = (ph.sem(n) for n in ("steps", "mv_ready", "rstd_ready", "xn_ready"))
        spacer_d, spacer_p = ph.sem("spacer_d"), ph.sem("spacer_p")
        job_full = ph.sem("job_full")
        job_done = [ph.sem(f"job_done{i}") for i in range(2)]
        s_full, max_done, exp_done, norm_done = (ph.sem(n) for n in ("s_full", "max_done", "exp_done", "norm_done"))
        t_full, pt_done, pv_full, o_done = (ph.sem(n) for n in ("t_full", "pt_done", "pv_full", "o_done"))
        rec_done = ph.sem("rec_done")
        block = ph.block()

        def slot_job(t):
            p = t // 4 + 1
            return (p, t % 4, PR0 + 3 * p + t % 4) if p < NPAIR and t % 4 < 3 and t < U else None

        @block.sync
        def _(sp):
            for n, t in w.items():
                sp.dma_start(t[:], a["L0_xattn_" + n].rearrange("(k p) n -> p k n", p=P)).then_inc(loaded, 16)
            sp.dma_start(bo[:], a["L0_xattn_bo"].rearrange("(o n) -> o n", o=1).broadcast_to([P, D])).then_inc(loaded, 16)
            sp.dma_start(wo[:], a["L0_xattn_Wo"].rearrange("(k p) n -> p k n", p=P)).then_inc(loaded, 16)
            sp.sem_inc(xn_ready, 1)
            sp.sem_inc(res_ready, 1)
            sp.sem_inc(c_used, 1)
            with sp.Fori(0, NCH) as it:
                sp.wait_ge(xn_ready, it + 1)
                sp.wait_ge(res_ready, it + 1)
                sp.dma_start(xin[:], tokens(x_in, it)).then_inc(x_ready, 16)
                sp.wait_ge(c_used, it + 1)
                sp.dma_start(cin[:], tokens(ctx_in, it)).then_inc(c_ready, 16)

        @block.gpsimd
        def _(pool):
            pool.memset(cimg[:, :, :, 0:TEXT], 0.0).then_inc(cimg_clear, 1)
            pool.wait_ge(loaded, 16 * 7)
            with pool.Fori(0, NCH) as it:
                norm_rstd(pool, mv, var, rstd, neghalf, mv_ready, rstd_ready, var_done, it, spacer_p)
                for s in job_done:
                    wait_alone(pool, s, JB * it + 1, spacer_p)
                wait_alone(pool, x_ready, 16 * it + 16, spacer_p)
                for t in range(NT):
                    ins = pool.tensor_tensor(xres[:, t, :], xin[:, t, :], bo[:], ALU.add)
                ins.then_inc(res_ready, 1)

        @block.vector
        def _(dve):
            dve.wait_ge(cimg_clear, 1)
            with dve.Fori(0, NCH) as it:
                steps = Count(dve, steps_done, NT * it)
                dve.wait_ge(x_ready, 16 * it + 16)
                norm_stats(dve, st, mv, steps, mv_ready, spacer_d, xin)
                dve.wait_ge(rstd_ready, it + 1)
                norm_rows(dve, xn, xin, mv, rstd).then_inc(xn_ready, 1)

                def evacuate(p, what, g):
                    dve.wait_ge(job_full, JOBS * it + g + 1)
                    to = kT[:, p % 2, :] if what == 1 else v[:, p % 2].rearrange("p j n -> p (j n)")
                    dve.tensor_copy(to, pj[g % 2][:]).then_inc(job_done[g % 2], 1)

                evacuate(0, 1, PR0 + 1)
                evacuate(0, 2, PR0 + 2)
                for t in range(U + 1):
                    i = t % 2
                    if t < U:
                        dve.wait_ge(s_full, U * it + t + 1)
                        for g, (lo, hi) in enumerate(SEG):
                            ins = dve.tensor_reduce(nm[:, i, g, :], sc[i][:, :, lo:hi], AX_X, ALU.max, negate=True)
                        ins.then_inc(max_done, 1)
                        job = slot_job(t)
                        if job and job[1] > 0:
                            evacuate(*job)
                        dve.wait_ge(exp_done, U * it + t + 3)
                        dve.reciprocal(rec[:, i].rearrange("p a b -> p (a b)"),
                                       sums[:, i].rearrange("p a b -> p (a b)")).then_inc(rec_done, 1)
                        dve.wait_ge(rec_done, U * it + t + 1)
                        for g, (lo, hi) in enumerate(SEG):
                            for m in range(2):
                                ins = dve.tensor_scalar(prob[:, i, m, lo:hi], prob[:, i, m, lo:hi], rec[:, i, g, m:m + 1],
                                                        None, ALU.mult)
                        ins.then_inc(norm_done, 1)
                    if t > 0:
                        j = (t - 1) % 2
                        dve.wait_ge(t_full, U * it + t + 2)
                        dve.wait_ge(pv_full, U * it + t)
                        dve.tensor_copy(pT[:, j], tp[j][:]).then_inc(pt_done, 1)
                for t in range(NT):
                    g = OU0 + t
                    dve.wait_ge(job_full, JOBS * it + g + 1)
                    if t == 0:
                        dve.wait_ge(res_ready, it + 2)
                        dve.wait_ge(stored, 16 * it + 16)
                    dve.tensor_tensor(yout[:, t, :], pj[g % 2][:], xres[:, t, :], ALU.add).then_inc(job_done[g % 2], 1)

        @block.scalar
        def _(act):
            act.sem_inc(t_full, 2)
            act.sem_inc(stored, 16)
            act.wait_ge(cimg_clear, 1)
            with act.Fori(0, NCH) as it:
                for g in range(2 * KD):
                    k = g % KD
                    act.wait_ge(job_full, JOBS * it + g + 1)
                    if g < KD:
                        ins = act.activation(xT[:, k, :], pj[g % 2][:], ACT.Copy)
                    else:
                        act.activation(cT[:, k, :], pj[g % 2][:], ACT.Copy)
                        ins = act.activation(cimg[:, k, :, TEXT:P], pj[g % 2][:].rearrange("p (b s) -> p b s", b=NB)[:, :, TEXT:P], ACT.Copy)
                    ins.then_inc(job_done[g % 2], 1)

                def query(p, what, g):
                    act.wait_ge(job_full, JOBS * it + g + 1)
                    act.activation(qT[:, p % 2, :], pj[g % 2][:], ACT.Copy, scale=DH ** -0.5).then_inc(job_done[g % 2], 1)

                query(0, 0, PR0)
                for t in range(U + 2):
                    i = t % 2
                    if t < U:
                        act.wait_ge(max_done, U * it + t + 1)
                        act.wait_ge(t_full, U * it + t + 1)
                        for g, (lo, hi) in enumerate(SEG):
                            for m in range(2):
                                ins = act.activation(prob[:, i, m, lo:hi], sc[i][:, m, lo:hi], ACT.Exp,
                                                     bias=nm[:, i, g, m:m + 1], accum_out=sums[:, i, g, m:m + 1])
                        ins.then_inc(exp_done, 1)
                        job = slot_job(t)
                        if job and job[1] == 0:
                            query(*job)
                    if t > 1:
                        u = t - 2
                        p, b, h = u // 4, u // 2 % 2, u % 2
                        act.wait_ge(pv_full, U * it + u + 3)
                        act.activation(oT[64 * h:64 * h + 64, p, b * S:(b + 1) * S], po[u % 2][0:DH, 0:S], ACT.Copy).then_inc(o_done, 1)
                for s in job_done:
                    act.wait_ge(s, JB * it + JB + 1)
                act.dma_start(tokens(x1, it), yout[:]).then_inc(stored, 16)
            act.wait_ge(stored, 16 * NCH + 16)

        @block.tensor
        def _(pe):
            for s in job_done:
                pe.sem_inc(s, 1)
            pe.sem_inc(exp_done, 2)
            pe.sem_inc(pt_done, 2)
            pe.sem_inc(pv_full, 2)
            pe.sem_inc(o_done, 2)
            pe.wait_ge(loaded, 16 * 7)
            with pe.Fori(0, NCH) as it:
                def free(g):
                    pe.wait_ge(job_done[g % 2], JB * it + g // 2 + 1)

                def taken(g):
                    pe.wait_ge(job_done[g % 2], JB * it + g // 2 + 2)

                pe.wait_ge(xn_ready, it + 2)
                for g in range(KD):
                    free(g)
                    transpose_job(pe, pj[g % 2], xn, g, ident).then_inc(job_full, 1)
                pe.wait_ge(c_ready, 16 * it + 16)
                for g in range(KD, 2 * KD):
                    free(g)
                    ins = transpose_job(pe, pj[g % 2], cin, g - KD, ident)
                    ins.then_inc(job_full, 1)

                def project(p, what, g):
                    free(g)
                    out = pj[g % 2]
                    cols = slice(p * P, (p + 1) * P)
                    if what == 0:
                        for k in range(KD):
                            ins = pe.matmul(out[:], w["Wq"][:, k, cols], xT[:, k, :], start=k == 0, stop=k == KD - 1)
                    elif what == 1:
                        for name, (lo, hi) in zip(("Wk", "Wk_ip"), SEG):
                            for k in range(KD):
                                ins = pe.matmul(out[:].rearrange("p (b s) -> p b s", b=NB)[:, :, lo:hi], w[name][:, k, cols],
                                                cT[:, k, :].rearrange("p (b s) -> p b s", b=NB)[:, :, lo:hi],
                                                start=k == 0, stop=k == KD - 1)
                    else:
                        for j in range(2 * NB):
                            b, c = j // 2, j % 2
                            o = out[:, j * P:(j + 1) * P]
                            for k in range(KD):
                                keys = cT[:, k, b * S + P:(b + 1) * S] if c else cimg[:, k, b, :]
                                ins = pe.matmul(o, keys, w["Wv_ip"][:, k, cols], start=k == 0, stop=k == KD - 1)
                            if c == 0:
                                for k in range(KD):
                                    ins = pe.matmul(out[0:TEXT, j * P:(j + 1) * P], cT[:, k, b * S:b * S + TEXT],
                                                    w["Wv"][:, k, cols], start=False, stop=False, skip_group_check=True)
                    ins.then_inc(job_full, 1)

                taken(KD - 1)
                taken(KD - 2)
                project(0, 0, PR0)
                taken(2 * KD - 1)
                taken(2 * KD - 2)
                pe.sem_inc(c_used, 1)
                project(0, 1, PR0 + 1)
                project(0, 2, PR0 + 2)
                for t in range(U + 2):
                    if t < U:
                        p, b, h = t // 4, t // 2 % 2, t % 2
                        if t % 4 == 0:
                            taken(PR0 + 3 * p)
                            taken(PR0 + 3 * p + 1)
                            taken(PR0 + 3 * p + 2)
                        pe.wait_ge(exp_done, U * it + t + 1)
                        rows = slice(64 * h, 64 * h + 64)
                        for m in range(2):
                            q0 = b * S + m * P
                            ins = pe.matmul(sc[t % 2][:, m, :], qT[rows, p % 2, q0:q0 + P], kT[rows, p % 2, b * S:(b + 1) * S],
                                            start=True, stop=True)
                        ins.then_inc(s_full, 1)
                        job = slot_job(t)
                        if job:
                            project(*job)
                    if 0 < t <= U:
                        u = t - 1
                        pe.wait_ge(norm_done, U * it + u + 1)
                        pe.wait_ge(pt_done, U * it + u + 1)
                        for c in range(2):
                            for m in range(2):
                                ins = pe.transpose(tp[u % 2][:, c, m * P:(m + 1) * P], prob[:, u % 2, m, c * P:(c + 1) * P], ident[:])
                        ins.then_inc(t_full, 1)
                    if t > 1:
                        u = t - 2
                        p, b, h = u // 4, u // 2 % 2, u % 2
                        pe.wait_ge(pt_done, U * it + u + 3)
                        pe.wait_ge(o_done, U * it + u + 1)
                        for c in range(2):
                            ins = pe.matmul(po[u % 2][0:DH, 0:S], v[:, p % 2, 2 * b + c, DH * h:DH * h + DH], pT[:, u % 2, c, :],
                                            start=c == 0, stop=c == 1)
                        ins.then_inc(pv_full, 1)
                pe.wait_ge(o_done, U * it + U + 2)
                for t in range(NT):
                    g = OU0 + t
                    free(g)
                    for k in range(NPAIR):
                        ins = pe.matmul(pj[g % 2][:], oT[:, k, t * P:(t + 1) * P], wo[:, k, :], start=k == 0, stop=k == NPAIR - 1)
                    ins.then_inc(job_full, 1)



SUB = 6
SC = KF * CT // SUB
MS = KF // SUB
S_X, I_X, S_G, I_G, S_U, I_U, S_A, I_A, S_O, I_O, S_AU = range(11)


def chunk_loop(eng, body):
    body(0, 0, True, False)
    with eng.Fori(0, (NCH - 2) // 2) as i:
        body(2 * i + 1, 1, False, False)
        body(2 * i + 2, 0, False, False)
    body(NCH - 1, 1, False, True)


def dequantize(nc, name, loops, pieces, ident):
    n = len(pieces)
    NQ = D // QB
    with Phase(nc, name) as ph:
        raw = ph.sb("raw", [P, n, NQ, QB])
        amax = ph.sb("amax", [P, n, NQ])
        scale = ph.sb("scale", [P, n, NQ])
        inv = ph.sb("inv", [P, n, NQ])
        whole = ph.sb("whole", [P, NQ, QB], I16)
        deq = ph.sb("deq", [P, n, NQ, QB])
        turned = [ph.ps(f"turned{i}", [P, KD, P]) for i in range(n)]
        raw_ready = [ph.sem(f"raw_ready{i}") for i in range(n)]
        steps_done, deq_ready, turned_full = ph.sem("steps"), ph.sem("deq_ready"), ph.sem("turned_full")
        hi_done, placed = ph.sem("hi_done"), ph.sem("placed")
        spacer = ph.sem("spacer")
        STEPS = 4
        with nc.Block() as block:
            @block.sync
            def _(sp):
                sp.sem_inc(deq_ready, n)
                with sp.Fori(0, loops) as it:
                    for i, (src, _) in enumerate(pieces):
                        sp.wait_ge(deq_ready, n * it + i + 1)
                        sp.dma_start(raw[:, i], src(it).rearrange("p (a b) -> p a b", b=QB)).then_inc(raw_ready[i], 16)

            @block.vector
            def _(dve):
                def integers(it, i):
                    c = Count(dve, steps_done, (n * STEPS) * it + i * STEPS)
                    dve.wait_ge(raw_ready[i], 16 * it + 16)
                    c.done(dve.tensor_reduce(amax[:, i], raw[:, i], AX_X, ALU.max, apply_absolute_value=True))
                    c.wait()
                    c.done(dve.tensor_scalar(scale[:, i], amax[:, i], 1.0 / WMAX, TINY, ALU.mult, ALU.max))
                    c.wait()
                    c.done(dve.reciprocal(inv[:, i], scale[:, i]))
                    c.wait()
                    c.done(dve.tensor_tensor(whole[:], raw[:, i], inv[:, i].unsqueeze(2).broadcast_to([P, NQ, QB]), ALU.mult))
                    c.wait()
                    dve.tensor_tensor(deq[:, i], whole[:], scale[:, i].unsqueeze(2).broadcast_to([P, NQ, QB]), ALU.mult).then_inc(deq_ready, 1)
                    assert c.n == STEPS

                def low_part(it, i):
                    dst = pieces[i][1]
                    dve.wait_ge(hi_done, n * it + i + 1)
                    dve.tensor_tensor(dst(it, 1), turned[i][:], dst(it, 0).bitcast(F32), ALU.subtract).then_inc(placed, 1)

                with dve.Fori(0, loops) as it:
                    for i in range(n):
                        integers(it, i)
                        if i:
                            low_part(it, i - 1)
                    low_part(it, n - 1)

            @block.tensor
            def _(pe):
                pe.sem_inc(placed, n)
                with pe.Fori(0, loops) as it:
                    for i in range(n):
                        pe.wait_ge(deq_ready, n * it + i + 1 + n)
                        pe.wait_ge(placed, n * it + i + 1)
                        rows = deq[:, i].rearrange("p a b -> p (a b)")
                        for k in range(KD):
                            ins = pe.transpose(turned[i][:, k, :], rows[:, k * P:(k + 1) * P], ident[:])
                        ins.then_inc(turned_full, 1)

            @block.scalar
            def _(act):
                with act.Fori(0, loops) as it:
                    for i, (_, dst) in enumerate(pieces):
                        wait_alone(act, turned_full, n * it + i + 1, spacer)
                        act.activation(dst(it, 0), turned[i][:], ACT.Copy).then_inc(hi_done, 1)


def quantized_ffn(nc, a, x1, x2, raw_up, raw_gate, ident, neghalf):
    xq = nc.dram_tensor("xq", (NCH, P, KD * CT), I16).ap()

    def pieces_of(w, parts, rows_per, cols=(0,)):
        return [(lambda it, r=r, c=c: w[bass.ds(it * (rows_per * P) + r * P, P), c * D:(c + 1) * D],
                 lambda it, part, r=r, c=c: parts[:, part, c * KD:(c + 1) * KD, bass.ds(it * (rows_per * P) + r * P, P)])
                for r in range(rows_per) for c in cols]

    with Phase(nc, "qf") as top:
        scal = top.sb("scal", [P, 16])
        big = top.sb("big", [P, 4])
        with ExitStack() as gates:
            with Phase(nc, "qu") as mid:
                wu = mid.sb("wu", [P, 2, KD, FF], F32R)
                with Phase(nc, "qg") as low:
                    wg = low.sb("wg", [P, 2, KD, FF], F32R)
                    dequantize(nc, "qwug", KF // 2, pieces_of(a["L0_ffn_w_up"], wu, 2) + pieces_of(a["L0_ffn_w_gate"], wg, 2), ident)
                    normalize_all(nc, x1, xq, big, scal, ident, neghalf)
                    project(nc, "pg", xq, wg, raw_gate, big, S_G, I_G, scal)
                gate = gates.enter_context(nc.sbuf_tensor("qf_gate", [P, NCH * KF * CT], I16, side="right"))
                project(nc, "pu", xq, wu, raw_up, big, S_U, I_U, scal, raw_gate, gate)
            wd = top.sb("wd", [P, 2, KF, D], F32R)
            dequantize(nc, "qwd", KD, pieces_of(a["L0_ffn_w_down"], wd, 1, range(FF // D)), ident)
            output_maximum(nc, raw_up, gate, big, scal)
            down(nc, x1, x2, raw_up, gate, wd, scal)


def scale_of(dve, c, scal, big_col, scale, inverse, unit, raw):
    def col(i):
        return scal[:, i:i + 1]
    if unit is None:
        c.done(dve.tensor_scalar(col(scale), big_col, 1.0 / AMAX, TINY, ALU.mult, ALU.max))
        c.wait()
        c.done(dve.reciprocal(col(inverse), col(scale)))
        c.wait()
        return
    c.done(dve.tensor_scalar(col(scale), big_col, col(unit), raw / AMAX, ALU.mult, ALU.mult))
    c.wait()
    c.done(dve.tensor_scalar(col(scale), col(scale), TINY, None, ALU.max))
    c.wait()
    c.done(dve.reciprocal(col(inverse), col(scale)))
    c.wait()
    c.done(dve.tensor_scalar(col(inverse), col(inverse), col(unit), raw, ALU.mult, ALU.mult))
    c.wait()


def normalize_all(nc, x1, xq, big, scal, ident, neghalf):
    with Phase(nc, "na") as ph:
        xn = ph.sb("xn", [P, NCH, NT * D])
        with Phase(nc, "nr") as rows:
            normalized_rows(nc, rows, x1, xn, big, scal, neghalf)
        stage = ph.sb("stage", [P, 2, KD, CT], I16)
        bank = [ph.ps(f"bank{i}", [P, CT]) for i in range(2 * KD)]
        filled = ph.sem("filled")
        turned = [ph.sem("turned_act"), ph.sem("turned_dve")]
        stored = [ph.sem(f"stored{i}") for i in range(2)]
        with nc.Block() as block:
            def take(eng, it, half, e, op):
                for k in range(e, KD, 2):
                    eng.wait_ge(filled, 2 * KD * it + half * KD + k + 1)
                    if k == e:
                        eng.wait_ge(stored[half], 16 * it + 16)
                    op(stage[:, half, k, :], bank[half * KD + k][:]).then_inc(turned[e], 1)

            @block.tensor
            def _(pe):
                for e in range(2):
                    pe.sem_inc(turned[e], 4)
                for c in range(NCH):
                    for k in range(KD):
                        pe.wait_ge(turned[k % 2], 2 * c + k // 2 + 1)
                        for t in range(NT):
                            ins = pe.transpose(bank[c % 2 * KD + k][:, t * P:(t + 1) * P], xn[:, c, t * D + k * P:t * D + (k + 1) * P], ident[:])
                        ins.then_inc(filled, 1)

            @block.scalar
            def _(act):
                with act.Fori(0, NCH // 2) as it:
                    for half in range(2):
                        take(act, it, half, 0, lambda o, i: act.activation(o, i, ACT.Copy, scale=scal[:, I_X:I_X + 1]))

            @block.vector
            def _(dve):
                with dve.Fori(0, NCH // 2) as it:
                    for half in range(2):
                        take(dve, it, half, 1, lambda o, i: dve.tensor_scalar(o, i, scal[:, I_X:I_X + 1], None, ALU.mult))

            @block.sync
            def _(sp):
                for s in stored:
                    sp.sem_inc(s, 16)
                with sp.Fori(0, NCH // 2) as it:
                    for half in range(2):
                        for e in range(2):
                            sp.wait_ge(turned[e], 4 * it + 2 * half + 2 + 4)
                        sp.dma_start(xq[bass.ds(2 * it + half, 1)].rearrange("a p n -> p (a n)"),
                                     stage[:, half].rearrange("p k n -> p (k n)")).then_inc(stored[half], 16)
                for s in stored:
                    sp.wait_ge(s, 16 * (NCH // 2 + 1))


def normalized_rows(nc, ph, x1, xn, big, scal, neghalf):
    xin = ph.sb("xin", [P, 2, NT, D])
    st = ph.sb("st", [P, NT, 6])
    mv = ph.sb("mv", [P, NT, 2])
    var = ph.sb("var", [P, NT])
    rstd = ph.sb("rstd", [P, NT])
    mx = ph.sb("mx", [P, NCH])
    mx_row = ph.sb("mx_row", [P, 1])
    x_ready = [ph.sem(f"x_ready{i}") for i in range(2)]
    xn_ready, max_done, row_max, all_max, settled = (ph.sem(n) for n in ("xn_ready", "max_done", "row_max", "all_max", "settled"))
    steps_done, mv_ready, rstd_ready, var_done = (ph.sem(n) for n in ("steps", "mv_ready", "rstd_ready", "var_done"))
    spacer_d, spacer_p = ph.sem("spacer_d"), ph.sem("spacer_p")
    block = ph.block()

    @block.sync
    def _(sp):
        sp.sem_inc(xn_ready, 2)
        with sp.Fori(0, NCH // 2) as it:
            for i in range(2):
                sp.wait_ge(xn_ready, 2 * it + i + 1)
                sp.dma_start(xin[:, i], tokens(x1, 2 * it + i)).then_inc(x_ready[i], 16)

    @block.gpsimd
    def _(pool):
        with pool.Fori(0, NCH) as it:
            norm_rstd(pool, mv, var, rstd, neghalf, mv_ready, rstd_ready, var_done, it, spacer_p)
        pool.wait_ge(row_max, 1)
        pool.partition_all_reduce(big[:, 0:1], mx_row[:], P, RMAX).then_inc(all_max, 1)

    @block.vector
    def _(dve):
        def largest(c):
            dve.wait_ge(xn_ready, c + 3)
            dve.tensor_reduce(mx[:, bass.ds(c, 1)], xn[:, bass.ds(c, 1), :].rearrange("p a n -> p (a n)"), AX_X, ALU.max,
                              apply_absolute_value=True).then_inc(max_done, 1)

        with dve.Fori(0, NCH // 2) as it:
            for i in range(2):
                c = 2 * it + i
                steps = Count(dve, steps_done, NT * c)
                dve.wait_ge(x_ready[i], 16 * it + 16)
                norm_stats(dve, st, mv, steps, mv_ready, spacer_d, xin[:, i])
                dve.wait_ge(rstd_ready, c + 1)
                for t in range(NT):
                    ins = dve.tensor_scalar(xn[:, bass.ds(c, 1), t * D:(t + 1) * D].rearrange("p a n -> p (a n)"), xin[:, i, t, :],
                                            mv[:, t, 0:1], rstd[:, t:t + 1], ALU.subtract, ALU.mult)
                ins.then_inc(xn_ready, 1)
                largest(c)
        dve.wait_ge(max_done, NCH)
        dve.tensor_reduce(mx_row[:], mx[:], AX_X, ALU.max).then_inc(row_max, 1)
        dve.wait_ge(all_max, 1)
        scale_of(dve, Count(dve, settled), scal, big[:, 0:1], S_X, I_X, None, None)


def project(nc, name, xq, w, raw, big, scale, inverse, scal, raw_gate=None, gate=None):
    NBANK = 4
    NR = 3
    LAG = 1
    with Phase(nc, name) as ph:
        xi = ph.sb("xi", [P, 2, KD * CT], I16)
        xs = ph.sb("xs", [P, 2, 2, KD, CT], F32R)
        stage = ph.sb("stage", [P, NBANK, CT])
        mx = {0: ph.sb("mx", [P, NCH * KF])}
        mx_row = {0: ph.sb("mx_row", [P, 1])}
        if gate is not None:
            rg = ph.sb("rg", [P, NR, CT])
            sig = ph.sb("sig", [P, 2, CT])
            sq = ph.sb("sq", [P, CT], U16)
            prod = ph.sb("prod", [P, CT])
            mx[1] = ph.sb("mxg", [P, NCH * KF])
            mx_row[1] = ph.sb("mxg_row", [P, 1])
        bank = [ph.ps(f"bank{i}", [P, CT]) for i in range(NBANK)]
        xi_ready = [ph.sem(f"xi_ready{i}") for i in range(2)]
        x_hi, x_lo = ph.sem("x_hi"), ph.sem("x_lo")
        r_full, r_copied, max_done = ph.sem("r_full"), ph.sem("r_copied"), ph.sem("max_done")
        stored = [ph.sem(f"stored{i}") for i in range(NBANK)]
        rg_ready = [ph.sem(f"rg_ready{i}") for i in range(NR)]
        g_ready, sig_ready, sq_done, prod_done, prod_max = (ph.sem(n) for n in ("g_ready", "sig_ready", "sq_done", "prod_done", "prod_max"))
        row_max, all_max, settled, spacer, spacer_s = (ph.sem(n) for n in ("row_max", "all_max", "settled", "spacer", "spacer_s"))
        SPLIT = 5

        with nc.Block() as block:
            def gate_place(c, j):
                return gate[:, bass.ds(c * (KF * CT) + j * CT, CT)]

            @block.sync
            def _(sp):
                sp.sem_inc(x_lo, 2)
                for s in stored:
                    sp.sem_inc(s, 16)

                def load_rows(c, par):
                    sp.wait_ge(x_lo, c + 1)
                    sp.dma_start(xi[:, par], xq[bass.ds(c, 1)].rearrange("a p n -> p (a n)")).then_inc(xi_ready[par], 16)

                def load_gate(c, j):
                    sp.wait_ge(g_ready, KF * c + j + 1)
                    sp.dma_start(rg[:, j % NR, :], raw_gate[bass.ds(c, 1), :, (j % KF) * CT:(j % KF + 1) * CT].rearrange("a p n -> p (a n)")
                                 ).then_inc(rg_ready[j % NR], 16)

                load_rows(0, 0)
                if gate is not None:
                    sp.sem_inc(g_ready, NR)
                    load_gate(0, 0)
                    load_gate(0, 1)

                def body(c, par, first, last):
                    if not last:
                        load_rows(c + 1, 1 - par)
                    for j in range(KF):
                        if gate is not None and not (last and j + 2 >= KF):
                            nxt = j + 2 >= KF
                            load_gate(c + 1 if nxt else c, j + 2 - KF if nxt else j + 2)
                        wait_alone(sp, r_copied, KF * c + j + 1 + NBANK, spacer_s)
                        sp.dma_start(raw[bass.ds(c, 1), :, j * CT:(j + 1) * CT].rearrange("a p n -> p (a n)"), stage[:, j % NBANK, :]
                                     ).then_inc(stored[j % NBANK], 16)
                chunk_loop(sp, body)
                for s in stored:
                    sp.wait_ge(s, 16 * (KF // NBANK * NCH + 1))

            @block.scalar
            def _(act):
                act.sem_inc(max_done, NBANK)
                if gate is not None:
                    act.sem_inc(sq_done, 2)

                def high_part(c, par, half):
                    act.wait_ge(xi_ready[par], 16 * half + 16)
                    if not (isinstance(c, int) and c < 2):
                        act.wait_ge(r_full, KF * (c - 1))
                    act.activation(xs[:, par, 0].rearrange("p k n -> p (k n)"), xi[:, par], ACT.Copy).then_inc(x_hi, 1)

                def gates(c, j):
                    wait_alone(act, rg_ready[j % NR], 16 * (KF // NR) * c + 16 * (j // NR) + 16, spacer)
                    act.activation(gate_place(c, j), rg[:, j % NR, :], ACT.Copy, scale=scal[:, I_G:I_G + 1]).then_inc(g_ready, 1)
                    act.wait_ge(sq_done, KF * c + j + 1)
                    wait_alone(act, g_ready, KF * c + j + 1 + NR, spacer)
                    act.activation(sig[:, j % 2, :], gate_place(c, j), ACT.Sigmoid, scale=scal[:, S_G:S_G + 1]).then_inc(sig_ready, 1)

                high_part(0, 0, 0)

                def body(c, par, first, last, half):
                    for j in range(KF):
                        i = j % NBANK
                        if gate is not None:
                            gates(c, j)
                        if j == SPLIT and not last:
                            high_part(c + 1, 1 - par, half + (1 if par else 0))
                        act.wait_ge(r_full, KF * c + j + 1)
                        act.wait_ge(stored[i], 16 * (KF // NBANK) * c + 16 * (j // NBANK) + 16)
                        act.wait_ge(max_done, KF * c + j + 1)
                        act.activation(stage[:, i, :], bank[i][:], ACT.Copy).then_inc(r_copied, 1)
                body(0, 0, True, False, 0)
                with act.Fori(0, (NCH - 2) // 2) as i:
                    body(2 * i + 1, 1, False, False, i)
                    body(2 * i + 2, 0, False, False, i + 1)
                body(NCH - 1, 1, False, True, 0)

            @block.vector
            def _(dve):
                def low_part(c, par):
                    dve.wait_ge(x_hi, c + 1)
                    dve.tensor_tensor(xs[:, par, 1].rearrange("p k n -> p (k n)"), xi[:, par],
                                      xs[:, par, 0].rearrange("p k n -> p (k n)").bitcast(F32), ALU.subtract).then_inc(x_lo, 1)

                def gates(c, j):
                    n = KF * c + j
                    dve.wait_ge(sig_ready, n + 1)
                    dve.tensor_scalar(sq[:], sig[:, j % 2, :], SIGQ, SIGQ - 1, ALU.mult, ALU.min).then_inc(sq_done, 1)
                    dve.wait_ge(sq_done, n + 3)
                    dve.tensor_tensor(prod[:], gate_place(c, j), sq[:], ALU.mult).then_inc(prod_done, 1)
                    dve.wait_ge(prod_done, n + 1)
                    dve.tensor_reduce(mx[1][:, bass.ds(n, 1)], prod[:], AX_X, ALU.max, apply_absolute_value=True).then_inc(prod_max, 1)

                low_part(0, 0)

                def body(c, par, first, last):
                    for j in range(KF):
                        if gate is not None:
                            gates(c, j)
                        if j == SPLIT and not last:
                            low_part(c + 1, 1 - par)
                        dve.wait_ge(r_copied, KF * c + j + 1 + NBANK)
                        dve.tensor_reduce(mx[0][:, bass.ds(c * KF + j, 1)], stage[:, j % NBANK, :], AX_X, ALU.max,
                                          apply_absolute_value=True).then_inc(max_done, 1)
                chunk_loop(dve, body)
                dve.wait_ge(max_done, KF * NCH + NBANK)
                if gate is not None:
                    dve.wait_ge(prod_max, KF * NCH)
                for i in mx:
                    dve.tensor_reduce(mx_row[i][:], mx[i][:], AX_X, ALU.max).then_inc(row_max, 1)
                dve.wait_ge(all_max, len(mx))
                count = Count(dve, settled)
                scale_of(dve, count, scal, big[:, 0:1], scale, inverse, S_X, 1.0)
                if gate is not None:
                    scale_of(dve, count, scal, big[:, 1:2], S_A, I_A, S_G, 1.0 / SIGQ)

            @block.gpsimd
            def _(pool):
                pool.wait_ge(row_max, len(mx))
                for i in mx:
                    pool.partition_all_reduce(big[:, i:i + 1], mx_row[i][:], P, RMAX).then_inc(all_max, 1)

            @block.tensor
            def _(pe):
                pe.sem_inc(r_copied, NBANK)

                def body(c, par, first, last):
                    pe.wait_ge(x_lo, c + 3)
                    for j in range(KF):
                        pe.wait_ge(r_copied, KF * c + j + 1)
                        cols = slice(j * P, (j + 1) * P)
                        for k in range(KD):
                            ins = product(pe, bank[j % NBANK][:], (w[:, 0, k, cols], w[:, 1, k, cols]), (xs[:, par, 0, k, :], xs[:, par, 1, k, :]),
                                          k == 0, k == KD - 1)
                        ins.then_inc(r_full, 1)
                chunk_loop(pe, body)


def part(raw, it, s):
    return raw[bass.ds(it, 1), :, s * SC:(s + 1) * SC].rearrange("a p n -> p (a n)")


def output_maximum(nc, raw_up, gate, big, scal):
    with Phase(nc, "om") as ph:
        raw = ph.sb("raw", [P, 2, SC])
        sig = ph.sb("sig", [P, 2, SC])
        up = ph.sb("up", [P, 2, SC], I16)
        sq = ph.sb("sq", [P, SC], U16)
        prod = ph.sb("prod", [P, 2, SC])
        outp = ph.sb("outp", [P, SC])
        mx = ph.sb("mx", [P, NCH * SUB])
        mx_row = ph.sb("mx_row", [P, 1])
        raw_ready = [ph.sem(f"raw_ready{i}") for i in range(2)]
        up_ready, sig_ready, sq_done, prod_done, gate_ready, out_done, max_done = (
            ph.sem(n) for n in ("up_ready", "sig_ready", "sq_done", "prod_done", "gate_ready", "out_done", "max_done"))
        row_max, all_max, settled = ph.sem("row_max"), ph.sem("all_max"), ph.sem("settled")
        spacer = ph.sem("spacer")
        N = NCH * SUB
        with nc.Block() as block:
            def place(n):
                return gate[:, bass.ds(n * SC, SC)]

            @block.sync
            def _(sp):
                sp.sem_inc(up_ready, 2)
                with sp.Fori(0, NCH) as it:
                    for s in range(SUB):
                        sp.wait_ge(up_ready, SUB * it + s + 1)
                        sp.dma_start(raw[:, s % 2, :], part(raw_up, it, s)).then_inc(raw_ready[s % 2], 16)

            @block.scalar
            def _(act):
                act.sem_inc(sq_done, 2)
                act.sem_inc(out_done, 2)
                act.sem_inc(max_done, 1)

                def sigmoid(n, s):
                    wait_alone(act, sq_done, n + 1, spacer)
                    act.activation(sig[:, s, :], place(n), ACT.Sigmoid, scale=scal[:, S_G:S_G + 1]).then_inc(sig_ready, 1)

                def products(n, s, half):
                    act.wait_ge(raw_ready[s], 16 * half + 16)
                    act.wait_ge(out_done, n + 1)
                    act.activation(up[:, s, :], raw[:, s, :], ACT.Copy, scale=scal[:, I_U:I_U + 1]).then_inc(up_ready, 1)
                    wait_alone(act, prod_done, n + 1, spacer)
                    act.activation(place(n), prod[:, s, :], ACT.Copy, scale=scal[:, I_A:I_A + 1]).then_inc(gate_ready, 1)

                sigmoid(0, 0)
                with act.Fori(0, N // 2 - 1) as it:
                    for s in range(2):
                        sigmoid(2 * it + s + 1, 1 - s)
                        products(2 * it + s, s, it)
                sigmoid(N - 1, 1)
                products(N - 2, 0, N // 2 - 1)
                products(N - 1, 1, N // 2 - 1)

            @block.vector
            def _(dve):
                def gates(n, s):
                    dve.wait_ge(sig_ready, n + 1)
                    if not (isinstance(n, int) and n == 0):
                        dve.wait_ge(prod_done, n)
                    dve.tensor_scalar(sq[:], sig[:, s, :], SIGQ, SIGQ - 1, ALU.mult, ALU.min).then_inc(sq_done, 1)
                    dve.wait_ge(sq_done, n + 3)
                    if not (isinstance(n, int) and n < 2):
                        dve.wait_ge(gate_ready, n - 1)
                    dve.tensor_tensor(prod[:, s, :], place(n), sq[:], ALU.mult).then_inc(prod_done, 1)

                def outputs(n, s):
                    dve.wait_ge(gate_ready, n + 1)
                    dve.wait_ge(up_ready, n + 3)
                    dve.wait_ge(max_done, n + 1)
                    dve.tensor_tensor(outp[:], place(n), up[:, s, :], ALU.mult).then_inc(out_done, 1)
                    dve.wait_ge(out_done, n + 3)
                    dve.tensor_reduce(mx[:, bass.ds(n, 1)], outp[:], AX_X, ALU.max, apply_absolute_value=True).then_inc(max_done, 1)

                gates(0, 0)
                gates(1, 1)
                with dve.Fori(0, N // 2 - 1) as it:
                    for s in range(2):
                        outputs(2 * it + s, s)
                        gates(2 * it + s + 2, s)
                outputs(N - 2, 0)
                outputs(N - 1, 1)
                dve.wait_ge(max_done, N + 1)
                dve.tensor_reduce(mx_row[:], mx[:], AX_X, ALU.max).then_inc(row_max, 1)
                dve.wait_ge(all_max, 1)
                c = Count(dve, settled)
                c.done(dve.tensor_tensor(scal[:, S_AU:S_AU + 1], scal[:, S_A:S_A + 1], scal[:, S_U:S_U + 1], ALU.mult))
                c.wait()
                scale_of(dve, c, scal, big[:, 0:1], S_O, I_O, S_AU, 1.0)

            @block.gpsimd
            def _(pool):
                pool.wait_ge(row_max, 1)
                pool.partition_all_reduce(big[:, 0:1], mx_row[:], P, RMAX).then_inc(all_max, 1)


def down(nc, x1, x2, raw_up, gate, wd, scal):
    NO = 3
    with Phase(nc, "dn") as ph:
        raw = ph.sb("raw", [P, 2, SC])
        up = ph.sb("up", [P, SC], I16)
        prod = ph.sb("prod", [P, SC])
        oq = ph.sb("oq", [P, SC], I16)
        om = ph.sb("om", [P, NO, 2, MS, CT], F32R)
        y = ph.sb("y", [P, 2, NT, D])
        py = [[ph.ps(f"py{i}_{t}", [P, D]) for t in range(NT)] for i in range(2)]
        raw_ready = [ph.sem(f"raw_ready{i}") for i in range(2)]
        up_ready, out_done, oq_ready, om_hi, om_lo, om_used = (ph.sem(n) for n in ("up_ready", "out_done", "oq_ready", "om_hi", "om_lo", "om_used"))
        y_full, y_done = ph.sem("y_full"), ph.sem("y_done")
        res_ready = [ph.sem(f"res_ready{i}") for i in range(2)]
        stored, y_free = ph.sem("stored"), ph.sem("y_free")
        with nc.Block() as block:
            @block.sync
            def _(sp):
                sp.sem_inc(up_ready, 2)
                sp.sem_inc(y_free, 2)
                with sp.Fori(0, NCH // 2) as it:
                    for par in range(2):
                        sp.wait_ge(y_free, 2 * it + par + 1)
                        sp.dma_start(y[:, par], tokens(x1, 2 * it + par)).then_inc(res_ready[par], 16)
                        for s in range(SUB):
                            sp.wait_ge(up_ready, 2 * SUB * it + SUB * par + s + 1)
                            sp.dma_start(raw[:, s % 2, :], part(raw_up, 2 * it + par, s)).then_inc(raw_ready[s % 2], 16)

            @block.gpsimd
            def _(pool):
                with pool.Fori(0, NCH // 2) as it:
                    for par in range(2):
                        pool.wait_ge(y_done, NT * (2 * it + par) + 2 * NT + NT)
                        pool.dma_start(tokens(x2, 2 * it + par), y[:, par]).then_inc(stored, 16)
                        pool.wait_ge(stored, 16 * (2 * it + par) + 16)
                        pool.sem_inc(y_free, 1)

            @block.scalar
            def _(act):
                act.sem_inc(out_done, 1)
                act.sem_inc(om_used, 2)
                act.sem_inc(y_full, NT)
                act.sem_inc(oq_ready, 1)
                with act.Fori(0, NCH) as it:
                    for s in range(SUB):
                        n = SUB * it + s
                        act.wait_ge(raw_ready[s % 2], 16 * (SUB // 2) * it + 16 * (s // 2) + 16)
                        act.wait_ge(out_done, n + 1)
                        act.activation(up[:], raw[:, s % 2, :], ACT.Copy, scale=scal[:, I_U:I_U + 1]).then_inc(up_ready, 1)
                        act.wait_ge(out_done, n + 2)
                        act.wait_ge(om_lo, n + 1)
                        act.activation(oq[:], prod[:], ACT.Copy, scale=scal[:, I_O:I_O + 1]).then_inc(oq_ready, 1)
                        act.wait_ge(oq_ready, n + 2)
                        if s == SUB - 1 - NO:
                            act.wait_ge(y_full, NT * it + NT)
                        else:
                            act.wait_ge(om_used, (SUB - 1) * it + s + (1 if s < NO else 0))
                        act.activation(om[:, s % NO, 0].rearrange("p m n -> p (m n)"), oq[:], ACT.Copy).then_inc(om_hi, 1)

            @block.vector
            def _(dve):
                dve.sem_inc(om_lo, 1)
                dve.sem_inc(y_done, 2 * NT)

                def outputs(c, s):
                    n = SUB * c + s
                    dve.wait_ge(up_ready, n + 3)
                    dve.wait_ge(oq_ready, n + 1)
                    dve.tensor_tensor(prod[:], gate[:, bass.ds(c * (KF * CT) + s * SC, SC)], up[:], ALU.mult).then_inc(out_done, 1)
                    dve.wait_ge(om_hi, n + 1)
                    dve.tensor_tensor(om[:, s % NO, 1].rearrange("p m n -> p (m n)"), oq[:],
                                      om[:, s % NO, 0].rearrange("p m n -> p (m n)").bitcast(F32), ALU.subtract).then_inc(om_lo, 1)

                def ends(c, par, half):
                    dve.wait_ge(res_ready[par], 16 * half + 16)
                    for t in range(NT):
                        dve.wait_ge(y_full, NT * c + NT + t + 1)
                        dve.scalar_tensor_tensor(y[:, par, t, :], py[par][t][:], scal[:, S_O:S_O + 1], y[:, par, t, :], ALU.mult, ALU.add
                                                 ).then_inc(y_done, 1)

                for s in range(SUB):
                    outputs(0, s)
                with dve.Fori(0, NCH // 2 - 1) as it:
                    for par in range(2):
                        for s in range(SUB):
                            if s == 3:
                                ends(2 * it + par, par, it)
                            outputs(2 * it + par + 1, s)
                for s in range(SUB):
                    if s == 3:
                        ends(NCH - 2, 0, NCH // 2 - 1)
                    outputs(NCH - 1, s)
                ends(NCH - 1, 1, NCH // 2 - 1)

            @block.tensor
            def _(pe):
                with pe.Fori(0, NCH // 2) as it:
                    for par in range(2):
                        c = 2 * it + par
                        for s in range(SUB):
                            pe.wait_ge(om_lo, SUB * c + s + 2)
                            for t in range(NT):
                                if s == 0:
                                    pe.wait_ge(y_done, NT * c + t + 1)
                                cols = slice(t * P, (t + 1) * P)
                                for m in range(MS):
                                    ins = product(pe, py[par][t][:], (om[:, s % NO, 0, m, cols], om[:, s % NO, 1, m, cols]),
                                                  (wd[:, 0, s * MS + m, :], wd[:, 1, s * MS + m, :]),
                                                  s == 0 and m == 0, s == SUB - 1 and m == MS - 1)
                                if s == SUB - 1:
                                    ins.then_inc(y_full, 1)
                            if s < SUB - 1:
                                ins.then_inc(om_used, 1)


def masked_attention(nc, a, x2, ctx_in, x3, ident, neghalf):
    SCALE = D ** -0.5
    JOBS = 3 * KD
    JB = JOBS // 2
    NK = S // P
    with Phase(nc, "ma") as ph:
        gram = ph.sb("gram", [P, KD, D])
        gcol = ph.sb("gcol", [P, KD])
        grow = ph.sb("grow", [P, D])
        bb = ph.sb("bb", [P, 1])
        fold_projections(nc, a, gram, gcol, grow, bb, ident, SCALE)
        mask = ph.sb("mask", [P, NK, S])
        xin = ph.sb("xin", [P, NT, D])
        xkeep = ph.sb("xkeep", [P, NT, D])
        cin = ph.sb("cin", [P, 2, NT, D])
        xn = ph.sb("xn", [P, NT, D])
        junk = ph.sb("junk", [P, D])
        rowc = ph.sb("rowc", [P, NT])
        st = ph.sb("st", [P, NT, 6])
        mv = ph.sb("mv", [P, NT, 2])
        var = ph.sb("var", [P, NT])
        rstd = ph.sb("rstd", [P, NT])
        xT = ph.sb("xT", [P, KD, CT])
        cT = ph.sb("cT", [P, KD, CT])
        rT = ph.sb("rT", [P, KD, CT])
        logit = ph.sb("logit", [P, 2, S])
        nm = ph.sb("nm", [P, 2])
        sums = ph.sb("sums", [P, NT])
        rec = ph.sb("rec", [P, NT])
        prob = ph.sb("prob", [P, 2, S])
        pT = ph.sb("pT", [P, 2, NK, P])
        yout = ph.sb("yout", [P, NT, D])
        pj = [ph.ps(f"pj{i}", [P, CT]) for i in range(2)]
        sc = [ph.ps(f"sc{i}", [P, 512]) for i in range(2)]
        tp = [ph.ps(f"tp{i}", [P, 512]) for i in range(2)]
        po = [ph.ps(f"po{i}", [P, D]) for i in range(2)]
        loaded, x_ready, stored = ph.sem("loaded"), ph.sem("x_ready"), ph.sem("stored")
        c_ready = [ph.sem(f"c_ready{i}") for i in range(2)]
        steps_done, mv_ready, rstd_ready, var_done, xn_ready, rowc_ready, x_kept = (
            ph.sem(n) for n in ("steps", "mv_ready", "rstd_ready", "var_done", "xn_ready", "rowc_ready", "x_kept"))
        spacer_d, spacer_p = ph.sem("spacer_d"), ph.sem("spacer_p")
        job_full = ph.sem("job_full")
        job_done = [ph.sem(f"job_done{i}") for i in range(2)]
        s_full, logit_done, max_done, exp_done, rec_done, t_full, pt_done, o_full, o_done = (
            ph.sem(n) for n in ("s_full", "logit_done", "max_done", "exp_done", "rec_done", "t_full", "pt_done", "o_full", "o_done"))
        block = ph.block()
        NIT = NCH // 2

        @block.sync
        def _(sp):
            sp.dma_start(mask[:], a["fside_1xSxS2_0"].rearrange("o (m p) s -> p (o m) s", p=P)).then_inc(loaded, 16)
            sp.sem_inc(x_kept, 1)
            sp.sem_inc(xn_ready, 1)
            sp.sem_inc(o_full, 2 * NT)
            with sp.Fori(0, NIT) as it:
                for h in range(2):
                    sp.wait_ge(xn_ready, 2 * it + h + 1)
                    sp.wait_ge(x_kept, 2 * it + h + 1)
                    sp.dma_start(xin[:], tokens(x2, 2 * it + h)).then_inc(x_ready, 16)
                    sp.wait_ge(o_full, NT * (2 * it + h) + NT)
                    sp.dma_start(cin[:, h], tokens(ctx_in, 2 * it + h)).then_inc(c_ready[h], 16)

        @block.gpsimd
        def _(pool):
            with pool.Fori(0, NIT) as it:
                for h in range(2):
                    n = 2 * it + h
                    norm_rstd(pool, mv, var, rstd, neghalf, mv_ready, rstd_ready, var_done, n, spacer_p)
                    wait_alone(pool, o_done, NT * n + 2, spacer_p)
                    pool.tensor_copy(xkeep[:], xin[:]).then_inc(x_kept, 1)

        @block.vector
        def _(dve):
            dve.wait_ge(loaded, 16)
            with dve.Fori(0, NIT) as it:
                for h in range(2):
                    n = 2 * it + h
                    steps = Count(dve, steps_done, NT * n)
                    dve.wait_ge(x_ready, 16 * n + 16)
                    norm_stats(dve, st, mv, steps, mv_ready, spacer_d, xin)
                    dve.wait_ge(rstd_ready, n + 1)
                    norm_rows(dve, xn, xin, mv, rstd).then_inc(xn_ready, 1)
                    dve.wait_ge(xn_ready, n + 2)
                    for t in range(NT):
                        ins = dve.tensor_tensor_reduce(junk[:], xn[:, t, :], grow[:], SCALE, bb[:, 0:1], ALU.mult, ALU.add, rowc[:, t:t + 1])
                        ins.then_inc(rowc_ready, 1)
                        dve.wait_ge(rowc_ready, NT * n + t + 1)
                    for k in range(KD):
                        g = KD + k
                        dve.wait_ge(job_full, JOBS * n + g + 1)
                        dve.tensor_copy(cT[:, k, :], pj[g % 2][:]).then_inc(job_done[g % 2], 1)
                    for t in range(NT + 2):
                        i = t % 2
                        if t < NT:
                            dve.wait_ge(s_full, NT * n + t + 1)
                            dve.wait_ge(exp_done, NT * n + t + 1)
                            dve.scalar_tensor_tensor(logit[:, i, :], sc[i][:, 0:S], rowc[:, t:t + 1], mask[:, t % NK, :], ALU.add, ALU.add).then_inc(logit_done, 1)
                            dve.wait_ge(logit_done, NT * n + t + 3)
                            dve.tensor_reduce(nm[:, i:i + 1], logit[:, i, :], AX_X, ALU.max, negate=True).then_inc(max_done, 1)
                        if 0 < t <= NT:
                            u = t - 1
                            dve.wait_ge(exp_done, NT * n + u + 3)
                            dve.reciprocal(rec[:, u:u + 1], sums[:, u:u + 1]).then_inc(rec_done, 1)
                            dve.wait_ge(t_full, NT * n + u + 3)
                            dve.wait_ge(o_full, NT * n + u - 1 + 2 * NT)
                            dve.tensor_copy(pT[:, u % 2].rearrange("p c n -> p (c n)"), tp[u % 2][:, 0:S]).then_inc(pt_done, 1)
                        if t > 1:
                            u = t - 2
                            dve.wait_ge(o_full, NT * n + u + 1 + 2 * NT)
                            if u == 0:
                                dve.wait_ge(x_kept, n + 2)
                                dve.wait_ge(stored, 16 * n + 16)
                            dve.wait_ge(rec_done, NT * n + u + 1)
                            dve.scalar_tensor_tensor(yout[:, u, :], po[u % 2][:], rec[:, u:u + 1], xkeep[:, u, :], ALU.mult, ALU.add).then_inc(o_done, 1)

        @block.scalar
        def _(act):
            act.sem_inc(stored, 16)
            act.sem_inc(t_full, 2)
            with act.Fori(0, NIT) as it:
                for h in range(2):
                    n = 2 * it + h
                    for k in range(KD):
                        act.wait_ge(job_full, JOBS * n + k + 1)
                        act.activation(xT[:, k, :], pj[k % 2][:], ACT.Copy).then_inc(job_done[k % 2], 1)
                    for k in range(KD):
                        g = 2 * KD + k
                        act.wait_ge(job_full, JOBS * n + g + 1)
                        act.activation(rT[:, k, :], pj[g % 2][:], ACT.Identity, bias=gcol[:, k:k + 1], scale=SCALE).then_inc(job_done[g % 2], 1)
                    for t in range(NT):
                        i = t % 2
                        act.wait_ge(max_done, NT * n + t + 1)
                        act.wait_ge(t_full, NT * n + t + 1)
                        act.activation(prob[:, i, :], logit[:, i, :], ACT.Exp, bias=nm[:, i:i + 1], accum_out=sums[:, t:t + 1]).then_inc(exp_done, 1)
                    act.wait_ge(o_done, NT * n + NT + 2)
                    act.dma_start(tokens(x3, n), yout[:]).then_inc(stored, 16)
            act.wait_ge(stored, 16 * NCH + 16)

        @block.tensor
        def _(pe):
            for s in job_done:
                pe.sem_inc(s, 1)
            pe.sem_inc(exp_done, 2)
            pe.sem_inc(logit_done, 2)
            pe.sem_inc(pt_done, 2)
            pe.sem_inc(o_done, 2)
            with pe.Fori(0, NIT) as it:
                for h in range(2):
                    n = 2 * it + h

                    def free(g):
                        pe.wait_ge(job_done[g % 2], JB * n + g // 2 + 1)

                    def taken(g):
                        pe.wait_ge(job_done[g % 2], JB * n + g // 2 + 2)

                    pe.wait_ge(xn_ready, n + 2)
                    for g in range(KD):
                        free(g)
                        transpose_job(pe, pj[g % 2], xn, g, ident).then_inc(job_full, 1)
                    pe.wait_ge(c_ready[h], 16 * it + 16)
                    for g in range(KD, 2 * KD):
                        free(g)
                        transpose_job(pe, pj[g % 2], cin[:, h], g - KD, ident).then_inc(job_full, 1)
                    taken(KD - 2)
                    taken(KD - 1)
                    for m in range(KD):
                        g = 2 * KD + m
                        free(g)
                        for k in range(KD):
                            ins = pe.matmul(pj[g % 2][:], gram[:, k, m * P:(m + 1) * P], xT[:, k, :], start=k == 0, stop=k == KD - 1)
                        ins.then_inc(job_full, 1)
                    taken(JOBS - 2)
                    taken(JOBS - 1)
                    for t in range(NT + 2):
                        if t < NT:
                            b = t // NK
                            pe.wait_ge(logit_done, NT * n + t + 1)
                            for k in range(KD):
                                ins = pe.matmul(sc[t % 2][:, 0:S], rT[:, k, t * P:(t + 1) * P], cT[:, k, b * S:(b + 1) * S], start=k == 0, stop=k == KD - 1)
                            ins.then_inc(s_full, 1)
                        if 0 < t <= NT:
                            u = t - 1
                            pe.wait_ge(exp_done, NT * n + u + 3)
                            pe.wait_ge(pt_done, NT * n + u + 1)
                            for c in range(NK):
                                ins = pe.transpose(tp[u % 2][:, c * P:(c + 1) * P], prob[:, u % 2, c * P:(c + 1) * P], ident[:])
                            ins.then_inc(t_full, 1)
                        if t > 1:
                            u = t - 2
                            pe.wait_ge(pt_done, NT * n + u + 3)
                            pe.wait_ge(o_done, NT * n + u + 1)
                            for c in range(NK):
                                ins = pe.matmul(po[u % 2][:], pT[:, u % 2, c, :], cin[:, h, (u // NK) * NK + c, :], start=c == 0, stop=c == NK - 1)
                            ins.then_inc(o_full, 1)


def fold_projections(nc, a, gram, gcol, grow, bb, ident, scale):
    with Phase(nc, "fp") as ph:
        w1 = ph.sb("w1", [P, KD, D])
        w2 = ph.sb("w2", [P, KD, D])
        w2T = ph.sb("w2T", [P, KD, D])
        b12 = ph.sb("b12", [P, 2, KD])
        m = ph.sb("m", [P, KD, D])
        beta = ph.sb("beta", [P, KD])
        ones = ph.sb("ones", [P, P])
        betas = ph.sb("betas", [P, KD, P])
        pw = [ph.ps(f"pw{i}", [P, D]) for i in range(4)]
        pc = [ph.ps(f"pc{i}", [P, D]) for i in range(4)]
        loaded, turned, turned_out, m_full, m_out, beta_full, beta_out, betas_out, done = (
            ph.sem(n) for n in ("loaded", "turned", "turned_out", "m_full", "m_out", "beta_full", "beta_out", "betas_out", "done"))
        g_full, g_out = ph.sem("g_full"), ph.sem("g_out")
        ones_made = ph.sem("ones_made")
        with nc.Block() as block:
            @block.sync
            def _(sp):
                sp.dma_start(w1[:], a["L1_xattn_W1"].rearrange("(k p) n -> p k n", p=P)).then_inc(loaded, 16)
                sp.dma_start(w2[:], a["L1_xattn_W2"].rearrange("(k p) n -> p k n", p=P)).then_inc(loaded, 16)
                sp.dma_start(b12[:, 0, :], a["L1_xattn_b1"].rearrange("(k p) -> p k", p=P), allow_slow_non_contiguous=True).then_inc(loaded, 16)
                sp.dma_start(b12[:, 1, :], a["L1_xattn_b2"].rearrange("(k p) -> p k", p=P), allow_slow_non_contiguous=True).then_inc(loaded, 16)

            @block.gpsimd
            def _(pool):
                pool.memset(ones[:], 1.0).then_inc(ones_made, 1)

            @block.tensor
            def _(pe):
                pe.wait_ge(loaded, 64)
                for k in range(KD):
                    for t in range(KD):
                        ins = pe.transpose(pw[k][:, t * P:(t + 1) * P], w2[:, t, k * P:(k + 1) * P], ident[:])
                    ins.then_inc(turned, 1)
                pe.wait_ge(turned_out, KD)
                for o in range(KD):
                    for k in range(KD):
                        ins = pe.matmul(pw[o][:], w2T[:, k, o * P:(o + 1) * P], w1[:, k, :], start=k == 0, stop=k == KD - 1)
                    ins.then_inc(m_full, 1)
                for o in range(KD):
                    for k in range(KD):
                        ins = pe.matmul(pc[0][:, o:o + 1], w2T[:, k, o * P:(o + 1) * P], b12[:, 0, k:k + 1], start=k == 0, stop=k == KD - 1)
                ins.then_inc(beta_full, 1)
                pe.wait_ge(m_out, KD)
                for d in range(KD):
                    for o in range(KD):
                        ins = pe.matmul(pw[d][:], m[:, o, d * P:(d + 1) * P], m[:, o, :], start=o == 0, stop=o == KD - 1)
                    ins.then_inc(g_full, 1)
                pe.wait_ge(betas_out, KD)
                for d in range(KD):
                    for o in range(KD):
                        ins = pe.matmul(pc[1][:, d:d + 1], m[:, o, d * P:(d + 1) * P], beta[:, o:o + 1], start=o == 0, stop=o == KD - 1)
                for o in range(KD):
                    ins = pe.matmul(pc[2][:], betas[:, o, :], m[:, o, :], start=o == 0, stop=o == KD - 1)
                for o in range(KD):
                    ins = pe.matmul(pc[3][:, 0:1], betas[:, o, :], beta[:, o:o + 1], start=o == 0, stop=o == KD - 1)
                ins.then_inc(g_full, 1)

            @block.scalar
            def _(act):
                for k in range(KD):
                    act.wait_ge(turned, k + 1)
                    act.activation(w2T[:, k, :], pw[k][:], ACT.Copy).then_inc(turned_out, 1)
                for o in range(KD):
                    act.wait_ge(m_full, o + 1)
                    act.activation(m[:, o, :], pw[o][:], ACT.Copy).then_inc(m_out, 1)
                for d in range(KD):
                    act.wait_ge(g_full, d + 1)
                    act.activation(gram[:, d, :], pw[d][:], ACT.Copy).then_inc(g_out, 1)

            @block.vector
            def _(dve):
                dve.wait_ge(beta_full, 1)
                dve.tensor_tensor(beta[:], pc[0][:, 0:KD], b12[:, 1, :], ALU.add).then_inc(beta_out, 1)
                dve.wait_ge(beta_out, 1)
                dve.wait_ge(ones_made, 1)
                for o in range(KD):
                    dve.tensor_scalar(betas[:, o, :], ones[:], beta[:, o:o + 1], None, ALU.mult).then_inc(betas_out, 1)
                dve.wait_ge(g_full, KD + 1)
                dve.tensor_scalar(gcol[:], pc[1][:, 0:KD], scale, None, ALU.mult).then_inc(done, 1)
                dve.tensor_copy(grow[:], pc[2][:]).then_inc(done, 1)
                dve.tensor_scalar(bb[:], pc[3][:, 0:1], scale, None, ALU.mult).then_inc(done, 1)
                dve.wait_ge(done, 3)


def lora_ffn(nc, a, x3, out, ident, neghalf):
    SCALING = 1.0 / R
    ZC = 2 * LZ + 2 * (LZ % 2)
    ROWH, ROWL = 0, 32
    LAG = 1
    HEAD = NT + 3
    TAIL = 2
    with Phase(nc, "lf") as ph:
        w1 = ph.sb("w1", [P, 2, KD, H2], F32R)
        w2 = ph.sb("w2", [P, 2, KH, D], F32R)
        ra1 = ph.sb("ra1", [P, KD * ZC + P], F32R)
        ra2 = ph.sb("ra2", [P, KH * ZC + P], F32R)
        lb1 = ph.sb("lb1", [P, H2], F32R)
        lb2 = ph.sb("lb2", [P, D], F32R)
        lora_weights(nc, a, w1, w2, ra1, ra2, lb1, lb2, ZC)
        xin = ph.sb("xin", [P, 2, D])
        y = ph.sb("y", [P, NT, D])
        st = ph.sb("st", [P, 2, 6])
        mv = ph.sb("mv", [P, 2, 2])
        var = ph.sb("var", [P, 2])
        rstd = ph.sb("rstd", [P, 2])
        xT = ph.sb("xT", [P, 2, 2, KD, CT], F32R)
        hT = ph.sb("hT", [P, 2, 2, CT], F32R)
        zT = ph.sb("zT", [P, CT])
        z2 = ph.sb("z2", [P, NT, ZC])
        z = ph.sb("z", [P, NT, LZ])
        zmax = ph.sb("zmax", [P, NT])
        zsum = ph.sb("zsum", [P, NT])
        zrec = ph.sb("zrec", [P, NT])
        gl = ph.sb("gl", [P, NT, E])
        ge = ph.sb("ge", [P, NT, E])
        zg = ph.sb("zg", [P, NT, P])
        zf = ph.sb("zf", [P, NT, ER])
        mixT = ph.sb("mixT", [P, 2, CT], F32R)
        pj = ph.ps("pj", [P, CT])
        pz = ph.ps("pz", [P, CT])
        hb = [ph.ps(f"hb{i}", [P, CT]) for i in range(2)]
        py = [ph.ps(f"py{i}", [P, D]) for i in range(NT)]
        x_ready = [ph.sem(f"x_ready{i}") for i in range(2)]
        res_ready, stored, cleared = ph.sem("res_ready"), ph.sem("stored"), ph.sem("cleared")
        stat_done, mv_ready, var_done, rstd_ready, xn_ready = (ph.sem(n) for n in ("stat_done", "mv_ready", "var_done", "rstd_ready", "xn_ready"))
        spacer_d, spacer_p = ph.sem("spacer_d"), ph.sem("spacer_p")
        pj_full, pj_hi, pj_done = ph.sem("pj_full"), ph.sem("pj_hi"), ph.sem("pj_done")
        h_full, h_hi, h_done, h_used = ph.sem("h_full"), ph.sem("h_hi"), ph.sem("h_done"), ph.sem("h_used")
        z_full, z_done = ph.sem("z_full"), ph.sem("z_done")
        y_full, y_done = ph.sem("y_full"), ph.sem("y_done")
        mix_steps, gl_ready, ge_ready, zg_ready = ([ph.sem(f"{n}{i}") for i in range(2)] for n in ("mix_steps", "gl_ready", "ge_ready", "zg_ready"))
        MIX = 9
        block = ph.block()

        def head_base(c):
            return 0 if isinstance(c, int) and c == 0 else (HEAD + TAIL) * c - TAIL

        def tail_base(c):
            return (HEAD + TAIL) * c + (HEAD if isinstance(c, int) and c == NCH - 1 else 2 * HEAD)

        def chunks(eng, body):
            body(0, 0, False, True)
            with eng.Fori(0, (NCH - 2) // 2) as i:
                body(2 * i + 1, 1, True, True)
                body(2 * i + 2, 0, True, True)
            body(NCH - 1, 1, True, False)

        @block.sync
        def _(sp):
            sp.sem_inc(pj_done, 1)
            sp.sem_inc(y_done, NT)

            def head(c):
                for t in range(NT):
                    if t >= 2:
                        sp.wait_ge(pj_done, head_base(c) + t - 2 + 2)
                    elif not (isinstance(c, int) and c == 0):
                        sp.wait_ge(pj_done, head_base(c - 1) + t + 2 + 2)
                    sp.dma_start(xin[:, t % 2, :], x3[bass.ds(c * CT + t * P, P), :]).then_inc(x_ready[t % 2], 16)

            def end(c):
                sp.wait_ge(y_done, NT * c + 2 * NT)
                sp.dma_start(tokens(out, c), y[:]).then_inc(stored, 16)

            head(0)

            def body(c, par, tail, nxt):
                if tail:
                    end(c - 1)
                    sp.wait_ge(stored, 16 * c)
                sp.dma_start(y[:], tokens(x3, c)).then_inc(res_ready, 16)
                if nxt:
                    head(c + 1)
            chunks(sp, body)
            end(NCH - 1)
            sp.wait_ge(stored, 16 * NCH)

        @block.gpsimd
        def _(pool):
            pool.memset(zg[:], 0.0).then_inc(cleared, 1)
            pool.wait_ge(cleared, 1)
            pool.memset(zg[:, :, ROWH + ER:ROWH + ER + 1], 1.0).then_inc(cleared, 1)
            pool.memset(zg[:, :, ROWL + ER:ROWL + ER + 1], 1.0).then_inc(cleared, 1)
            with pool.Fori(0, NCH) as c:
                for t in range(NT):
                    wait_alone(pool, mv_ready, NT * c + t + 1, spacer_p)
                    pool.tensor_scalar(var[:, t % 2:t % 2 + 1], mv[:, t % 2, 1:2], EPS, None, ALU.add).then_inc(var_done, 1)
                    pool.wait_ge(var_done, NT * c + t + 1)
                    pool.tensor_tensor(rstd[:, t % 2:t % 2 + 1], var[:, t % 2:t % 2 + 1], neghalf[:, 0:1], ALU.pow).then_inc(rstd_ready, 1)

        @block.vector
        def _(dve):
            dve.wait_ge(cleared, 3)

            def stats(c, t):
                i = t % 2
                dve.wait_ge(x_ready[i], 32 * c + 16 * (t // 2) + 16)
                dve.bn_stats(st[:, i, :], xin[:, i, :]).then_inc(stat_done, 1)
                wait_alone(dve, stat_done, NT * c + t + 1, spacer_d)
                dve.bn_aggr(mv[:, i, :], st[:, i, :]).then_inc(mv_ready, 1)

            def rows(c, t):
                i = t % 2
                dve.wait_ge(rstd_ready, NT * c + t + 1)
                dve.tensor_scalar(xin[:, i, :], xin[:, i, :], mv[:, i, 0:1], rstd[:, i:i + 1], ALU.subtract, ALU.mult).then_inc(xn_ready, 1)

            def turned_lo(c, t, par):
                cols = slice(t * P, (t + 1) * P)
                dve.wait_ge(pj_hi, NT * c + t + 1)
                dve.tensor_tensor(xT[:, par, 1, :, cols], pj[:].rearrange("p (k n) -> p k n", k=KD), xT[:, par, 0, :, cols].bitcast(F32),
                                  ALU.subtract).then_inc(pj_done, 1)

            def mixture(c, layer, job):
                s = Count(dve, mix_steps[layer], MIX * c)
                dve.wait_ge(pj_full, job + 1)
                dve.tensor_copy(z2[:], pj[:].rearrange("p (t n) -> p t n", t=NT)[:, :, 0:ZC]).then_inc(pj_done, 1)
                dve.wait_ge(pj_done, job + 2)
                s.done(dve.tensor_tensor(z[:], z2[:, :, 0:LZ], z2[:, :, ZC // 2:ZC // 2 + LZ], ALU.add))
                s.wait()
                s.done(dve.tensor_reduce(zmax[:], z[:, :, 0:E], AX_X, ALU.max))
                s.wait()
                dve.tensor_tensor(gl[:], z[:, :, 0:E], zmax[:].unsqueeze(2).broadcast_to([P, NT, E]), ALU.subtract).then_inc(gl_ready[layer], 1)
                dve.wait_ge(ge_ready[layer], c + 1)
                s.done(dve.tensor_reduce(zsum[:], ge[:], AX_X, ALU.add))
                s.wait()
                s.done(dve.reciprocal(zrec[:], zsum[:]))
                s.wait()
                s.done(dve.scalar_tensor_tensor(gl[:], ge[:], SCALING, zrec[:].unsqueeze(2).broadcast_to([P, NT, E]), ALU.mult, ALU.mult))
                s.wait()
                for e in range(E):
                    ins = dve.tensor_tensor(zf[:, :, e * R:(e + 1) * R], z[:, :, E + e * R:E + (e + 1) * R],
                                            gl[:, :, e:e + 1].broadcast_to([P, NT, R]), ALU.mult)
                s.done(ins)
                s.wait()
                s.done(dve.tensor_copy(zg[:, :, ROWH:ROWH + ER].bitcast(F32R), zf[:]))
                s.wait()
                s.done(dve.tensor_copy(zg[:, :, ROWL:ROWL + ER], zg[:, :, ROWH:ROWH + ER]))
                s.done(dve.tensor_tensor(zg[:, :, 64:64 + ER].bitcast(F32R), zf[:], zg[:, :, ROWH:ROWH + ER], ALU.subtract))
                s.wait()
                dve.sem_inc(zg_ready[layer], 1)
                assert s.n == MIX, s.n

            def hidden_lo(c, m):
                i = m % 2
                dve.wait_ge(h_hi, KH * c + m + 1)
                dve.scalar_tensor_tensor(hT[:, i, 1, :], hb[i][:], 0.0, hT[:, i, 0, :].bitcast(F32), ALU.max, ALU.subtract).then_inc(h_done, 1)

            def end(c):
                dve.wait_ge(res_ready, 16 * c + 16)
                for t in range(NT):
                    dve.wait_ge(y_full, NT * c + t + 1)
                    dve.tensor_tensor(y[:, t, :], py[t][:], y[:, t, :], ALU.add).then_inc(y_done, 1)

            for t in range(NT):
                stats(0, t)
                rows(0, t)
                turned_lo(0, t, 0)
            mixture(0, 0, head_base(0) + NT + 1)

            def body(c, par, tail, nxt):
                for m in range(KH + LAG):
                    if m < KH:
                        hidden_lo(c, m)
                    if tail and m == 0:
                        mixture(c - 1, 1, tail_base(c - 1))
                    if tail and m == 1:
                        end(c - 1)
                    if nxt:
                        if m in (1, 3, 5, 7):
                            stats(c + 1, m // 2)
                        if m in (2, 4, 6, 8):
                            rows(c + 1, m // 2 - 1)
                        if m in (3, 5, 7, 9):
                            turned_lo(c + 1, m // 2 - 1, 1 - par)
                        if m == 11:
                            mixture(c + 1, 0, head_base(c + 1) + NT + 1)
            chunks(dve, body)
            mixture(NCH - 1, 1, tail_base(NCH - 1))
            end(NCH - 1)

        @block.scalar
        def _(act):
            act.sem_inc(h_used, 2)

            def turned_hi(c, t, par):
                act.wait_ge(pj_full, head_base(c) + t + 1)
                act.activation(xT[:, par, 0, :, t * P:(t + 1) * P], pj[:].rearrange("p (k n) -> p k n", k=KD), ACT.Copy).then_inc(pj_hi, 1)

            def projected(job):
                act.wait_ge(pj_full, job + 1)
                act.activation(zT[:], pj[:], ACT.Copy).then_inc(pj_done, 1)

            def exps(c, layer):
                act.wait_ge(gl_ready[layer], c + 1)
                act.activation(ge[:], gl[:], ACT.Exp).then_inc(ge_ready[layer], 1)

            def mixed(job, layer):
                act.wait_ge(pj_full, job + 1)
                act.activation(mixT[:, layer, :], pj[:], ACT.Copy).then_inc(pj_done, 1)

            def hidden_hi(c, m):
                act.wait_ge(h_full, KH * c + m + 1)
                act.wait_ge(h_used, KH * c + m + 1)
                act.activation(hT[:, m % 2, 0, :], hb[m % 2][:], ACT.Relu).then_inc(h_hi, 1)

            def second_projected(c):
                act.wait_ge(z_full, c + 1)
                act.activation(zT[:], pz[:], ACT.Copy).then_inc(z_done, 1)

            for t in range(NT):
                turned_hi(0, t, 0)
            projected(head_base(0) + NT)
            exps(0, 0)
            mixed(head_base(0) + NT + 2, 0)

            def body(c, par, tail, nxt):
                for m in range(KH + LAG):
                    if m < KH:
                        hidden_hi(c, m)
                    if tail and m == 0:
                        exps(c - 1, 1)
                    if tail and m == 1:
                        mixed(tail_base(c - 1) + 1, 1)
                    if nxt:
                        if m in (3, 5, 7, 9):
                            turned_hi(c + 1, m // 2 - 1, 1 - par)
                        if m == 10:
                            projected(head_base(c + 1) + NT)
                        if m == 11:
                            exps(c + 1, 0)
                        if m == KH:
                            mixed(head_base(c + 1) + NT + 2, 0)
                second_projected(c)
            chunks(act, body)
            exps(NCH - 1, 1)
            mixed(tail_base(NCH - 1) + 1, 1)

        @block.tensor
        def _(pe):
            pe.sem_inc(z_done, 1)
            pe.sem_inc(h_done, 2)
            pe.wait_ge(cleared, 3)

            def pj_free(job):
                pe.wait_ge(pj_done, job + 1)

            def pj_taken(job):
                pe.wait_ge(pj_done, job + 2)

            def turn_tile(c, t):
                pe.wait_ge(xn_ready, NT * c + t + 1)
                pj_free(head_base(c) + t)
                for k in range(KD):
                    ins = pe.transpose(pj[:, k * P:(k + 1) * P], xin[:, t % 2, k * P:(k + 1) * P], ident[:])
                ins.then_inc(pj_full, 1)

            def first_projections(c, par):
                job = head_base(c) + NT
                pj_taken(job - 1)
                for k in range(KD):
                    for part in range(2):
                        ins = pe.matmul(pj[:], ra1[:, k * ZC:k * ZC + P], xT[:, par, part, k, :], start=k == 0 and part == 0,
                                        stop=k == KD - 1 and part == 1)
                ins.then_inc(pj_full, 1)

            def turn_projections(job):
                pj_free(job)
                for t in range(NT):
                    ins = pe.transpose(pj[:, t * P:(t + 1) * P], zT[:, t * P:(t + 1) * P], ident[:])
                ins.then_inc(pj_full, 1)

            def turn_mixture(c, layer, job):
                pe.wait_ge(zg_ready[layer], c + 1)
                pj_free(job)
                for t in range(NT):
                    ins = pe.transpose(pj[:, t * P:(t + 1) * P], zg[:, t, :], ident[:])
                ins.then_inc(pj_full, 1)

            def hidden(c, m, par):
                pe.wait_ge(h_done, KH * c + m + 1)
                cols = slice(m * P, (m + 1) * P)
                for k in range(KD):
                    product(pe, hb[m % 2][:], (w1[:, 0, k, cols], w1[:, 1, k, cols]), (xT[:, par, 0, k, :], xT[:, par, 1, k, :]), k == 0, False)
                if m == 0:
                    pj_taken(head_base(c) + NT + 2)
                pe.matmul(hb[m % 2][:], lb1[:, cols], mixT[:, 0, :], start=False, stop=True).then_inc(h_full, 1)

            def use_hidden(c, u):
                i = u % 2
                pe.wait_ge(h_done, KH * c + u + 3)
                if u == 0:
                    pe.wait_ge(z_done, c + 1)
                    pe.wait_ge(y_done, NT * c + NT)
                for part in range(2):
                    ins = pe.matmul(pz[:], ra2[:, u * ZC:u * ZC + P], hT[:, i, part, :], start=u == 0 and part == 0, stop=u == KH - 1 and part == 1)
                if u == KH - 1:
                    ins.then_inc(z_full, 1)
                for t in range(NT):
                    cols = slice(t * P, (t + 1) * P)
                    ins = product(pe, py[t][:], (hT[:, i, 0, cols], hT[:, i, 1, cols]), (w2[:, 0, u, :], w2[:, 1, u, :]), u == 0, False)
                ins.then_inc(h_used, 1)

            def second_lora(c):
                pj_taken(tail_base(c) + 1)
                for t in range(NT):
                    pe.matmul(py[t][:], mixT[:, 1, t * P:(t + 1) * P], lb2[:], start=False, stop=True).then_inc(y_full, 1)

            def end(c, between):
                pe.wait_ge(z_done, c + 2)
                turn_projections(tail_base(c))
                between()
                turn_mixture(c, 1, tail_base(c) + 1)
                second_lora(c)

            for t in range(NT):
                turn_tile(0, t)
            first_projections(0, 0)
            pj_taken(head_base(0) + NT)
            turn_projections(head_base(0) + NT + 1)
            turn_mixture(0, 0, head_base(0) + NT + 2)

            def body(c, par, tail, nxt):
                for m in range(KH + LAG):
                    if m < KH and not (tail and m == 1):
                        hidden(c, m, par)
                    if tail and m == 0:
                        end(c - 1, lambda: hidden(c, 1, par))
                    if nxt:
                        if m in (3, 5, 7, 9):
                            turn_tile(c + 1, m // 2 - 1)
                        if m == 10:
                            first_projections(c + 1, 1 - par)
                        if m == 11:
                            pj_taken(head_base(c + 1) + NT)
                            turn_projections(head_base(c + 1) + NT + 1)
                        if m == KH:
                            turn_mixture(c + 1, 0, head_base(c + 1) + NT + 2)
                    if m >= LAG:
                        use_hidden(c, m - LAG)
            chunks(pe, body)
            end(NCH - 1, lambda: None)


def split_pieces(nc, name, pieces, cols):
    NB_ = 3
    with Phase(nc, name) as ph:
        raw = ph.sb("raw", [P, NB_, cols])
        raw_ready = [ph.sem(f"raw_ready{i}") for i in range(NB_)]
        hi_done, lo_done = ph.sem("hi_done"), ph.sem("lo_done")
        block = ph.block()

        def place(i, hi):
            n = 1
            for s in hi.shape[1:]:
                n *= s
            r = raw[:, i % NB_, 0:n]
            return r.rearrange("p (k n) -> p k n", k=hi.shape[1]) if len(hi.shape) == 3 else r

        @block.sync
        def _(sp):
            for i, (src, hi, lo) in enumerate(pieces):
                if i >= NB_:
                    sp.wait_ge(lo_done, i - NB_ + 1)
                sp.dma_start(place(i, hi), src).then_inc(raw_ready[i % NB_], 16)

        @block.scalar
        def _(act):
            for i, (src, hi, lo) in enumerate(pieces):
                act.wait_ge(raw_ready[i % NB_], 16 * (i // NB_ + 1))
                act.activation(hi, place(i, hi), ACT.Copy).then_inc(hi_done, 1)

        @block.vector
        def _(dve):
            for i, (src, hi, lo) in enumerate(pieces):
                dve.wait_ge(hi_done, i + 1)
                dve.tensor_tensor(lo, place(i, hi), hi.bitcast(F32), ALU.subtract).then_inc(lo_done, 1)
            dve.wait_ge(lo_done, len(pieces))


def lora_weights(nc, a, w1, w2, ra1, ra2, lb1, lb2, ZC):
    W1, W2 = a["L1_ffn_W1"], a["L1_ffn_W2"]
    pieces = [(W1[k * P:(k + 1) * P, :], w1[:, 0, k, :], w1[:, 1, k, :]) for k in range(KD)]
    KP = H2 // D
    for g in range(KH // KP):
        rows = slice(g * KP, (g + 1) * KP)
        pieces.append((W2[g * KP * P:(g + 1) * KP * P, :].rearrange("(k p) n -> p k n", p=P), w2[:, 0, rows, :], w2[:, 1, rows, :]))
    split_pieces(nc, "lw", pieces, H2)
    with Phase(nc, "ls") as ph:
        s1 = ph.sb("s1", [P, KD, LZ])
        s2 = ph.sb("s2", [P, KH, LZ])
        t1 = ph.sb("t1", [P, H2])
        t2 = ph.sb("t2", [P, D])
        cleared, loaded, hi_done, lo_done = (ph.sem(n) for n in ("cleared", "loaded", "hi_done", "lo_done"))
        NL = 2 * (1 + E) + 2 * 5
        block = ph.block()

        def side(ra, kn, part):
            lo = part * (ZC // 2)
            return ra[:, 0:kn * ZC].rearrange("p (k z) -> p k z", z=ZC)[:, :, lo:lo + LZ]

        @block.gpsimd
        def _(pool):
            pool.memset(t1[:], 0.0).then_inc(cleared, 1)
            pool.memset(t2[:], 0.0).then_inc(cleared, 1)
            pool.memset(ra1[:].bitcast(F32), 0.0).then_inc(cleared, 1)
            pool.memset(ra2[:].bitcast(F32), 0.0).then_inc(cleared, 1)

        @block.sync
        def _(sp):
            for s, r, low in ((s1, "L1_ffn_R1", "L1_ffn_A1"), (s2, "L1_ffn_R2", "L1_ffn_A2")):
                sp.dma_start(s[:, :, 0:E], a[r].rearrange("(k p) e -> p k e", p=P)).then_inc(loaded, 16)
                for e in range(E):
                    sp.dma_start(s[:, :, E + e * R:E + (e + 1) * R], a[low][e].rearrange("(k p) r -> p k r", p=P)).then_inc(loaded, 16)
            sp.wait_ge(cleared, 4)
            for t, w, bias in ((t1, "L1_ffn_B1", "L1_ffn_b1"), (t2, "L1_ffn_B2", "L1_ffn_b2")):
                for row in (0, 32, 64):
                    sp.dma_start(t[row:row + ER, :], a[w].rearrange("e r n -> (e r) n")).then_inc(loaded, 16)
                for row in (0, 32):
                    sp.dma_start(t[row + ER:row + ER + 1, :], a[bias].rearrange("(o n) -> o n", o=1)).then_inc(loaded, 16)

        @block.scalar
        def _(act):
            act.wait_ge(loaded, 16 * NL)
            act.wait_ge(cleared, 4)
            for hi, src in ((side(ra1, KD, 0), s1[:]), (side(ra2, KH, 0), s2[:]), (lb1[:], t1[:]), (lb2[:], t2[:])):
                act.activation(hi, src, ACT.Copy).then_inc(hi_done, 1)

        @block.vector
        def _(dve):
            dve.wait_ge(hi_done, 4)
            for ra, kn, src in ((ra1, KD, s1), (ra2, KH, s2)):
                dve.tensor_tensor(side(ra, kn, 1), src[:], side(ra, kn, 0).bitcast(F32), ALU.subtract).then_inc(lo_done, 1)
            for t, lb in ((t1, lb1), (t2, lb2)):
                dve.tensor_tensor(lb[32:64, :], t[32:64, :], lb[32:64, :].bitcast(F32), ALU.subtract).then_inc(lo_done, 1)
            dve.wait_ge(lo_done, 4)


_INS = ['x', 'ctx_1024', 'fside_1xSxS2_0', 'L0_xattn_Wq', 'L0_xattn_Wk', 'L0_xattn_Wv', 'L0_xattn_Wk_ip', 'L0_xattn_Wv_ip',
        'L0_xattn_Wo', 'L0_xattn_bo', 'L0_ffn_w_gate', 'L0_ffn_w_up', 'L0_ffn_w_down', 'L1_xattn_W1', 'L1_xattn_b1',
        'L1_xattn_W2', 'L1_xattn_b2', 'L1_ffn_W1', 'L1_ffn_b1', 'L1_ffn_A1', 'L1_ffn_B1', 'L1_ffn_R1', 'L1_ffn_W2',
        'L1_ffn_b2', 'L1_ffn_A2', 'L1_ffn_B2', 'L1_ffn_R2']
_OUTS = [((B, S, D), 'float32')]


def kernel(**inputs):
    import numpy as _np
    import concourse.bacc as _bacc
    from concourse import mybir as _mybir
    from concourse.bass_utils import run_bass_kernel_spmd as _run

    nc = _bacc.Bacc("TRN2", target_bir_lowering=False, num_devices=1)
    arrays, args = {}, {}
    for name in _INS:
        a = _np.ascontiguousarray(inputs[name])
        arrays[f"in_{name}_dram"] = a
        args[name] = nc.dram_tensor(f"in_{name}_dram", a.shape, _mybir.dt.from_np(a.dtype), kind="ExternalInput").ap()
    outs = []
    for i, (shape, dtype) in enumerate(_OUTS):
        outs.append(nc.dram_tensor(f"out_{i}_dram", shape, _mybir.dt.from_np(_np.dtype(dtype)), kind="ExternalOutput").ap())
    kernel_program(nc, args, outs[0])
    r = _run(nc, [arrays], core_ids=[0])
    return r.results[0]["out_0_dram"]
```

```python
from contextlib import ExitStack

import concourse.bass as bass
from concourse import mybir

ALU = mybir.AluOpType
ACT = mybir.ActivationFunctionType
F32 = mybir.dt.float32
F32R = mybir.dt.float32r
I16 = mybir.dt.int16
U16 = mybir.dt.uint16
AX_X = mybir.AxisListType.X
RMAX = bass.bass_isa.ReduceOp.max

P = 128
B, S, D = 16, 256, 512
TOK = B * S
CT = 512
NCH = TOK // CT
NT = CT // P
KD = D // P
NB = CT // S
EPS = 1e-5

HEADS, DH = 16, 64
INNER = HEADS * DH
TEXT = 77
NPAIR = HEADS // 2

FF = 1536
KF = FF // P
QB = 32
WMAX = 7.0
AMAX = 32767.0
TINY = 1e-12
SIGQ = 65536.0
MAGIC = 12582912.0

H2 = 2048
KH = H2 // P
E, R = 3, 8
ER = E * R
LZ = E + ER


class Count:

    def __init__(self, eng, sem, base=0):
        self.eng, self.sem, self.base, self.n = eng, sem, base, 0

    def done(self, ins):
        ins.then_inc(self.sem, 1)
        self.n += 1
        return self.n

    def wait(self, n=None):
        self.eng.wait_ge(self.sem, self.base + (self.n if n is None else n))


class Phase:

    def __init__(self, nc, name):
        self.nc, self.name, self.ctx = nc, name, ExitStack()
        self.sems, self.blocks = [], ExitStack()

    def __enter__(self):
        self.ctx.__enter__()
        return self

    def __exit__(self, *a):
        self.blocks.close()
        if self.sems:
            with self.nc.Block() as block:
                @block.sync
                def _(sp):
                    for s in self.sems:
                        sp.sem_clear(s)
        return self.ctx.__exit__(*a)

    def block(self):
        return self.blocks.enter_context(self.nc.Block())

    def sb(self, name, shape, dt=F32):
        return self.ctx.enter_context(self.nc.sbuf_tensor(f"{self.name}_{name}", shape, dt))

    def ps(self, name, shape):
        return self.ctx.enter_context(self.nc.psum_tensor(f"{self.name}_{name}", shape, F32))

    def sem(self, name):
        self.sems.append(self.ctx.enter_context(self.nc.semaphore(f"{self.name}_{name}")))
        return self.sems[-1]


def wait_alone(eng, sem, value, spacer):
    eng.wait_ge(sem, value)
    eng.sem_inc(spacer, 1)


def tokens(ap, c):
    return ap[bass.ds(c * CT, CT), :].rearrange("(t p) d -> p t d", p=P)


def flat3(ap):
    return ap.rearrange("b s d -> (b s) d")


def kernel_program(nc, a, out):
    x_in, ctx_in, out_f = flat3(a["x"]), flat3(a["ctx_1024"]), flat3(out)
    x1 = nc.dram_tensor("x1", (TOK, D), F32).ap()
    x2 = nc.dram_tensor("x2", (TOK, D), F32).ap()
    x3 = nc.dram_tensor("x3", (TOK, D), F32).ap()
    raw_up = nc.dram_tensor("raw_up", (NCH, P, KF * CT), F32).ap()
    raw_gate = nc.dram_tensor("raw_gate", (NCH, P, KF * CT), F32).ap()
    with ExitStack() as top:
        ident = top.enter_context(nc.sbuf_tensor("ident", [P, P], F32))
        neghalf = top.enter_context(nc.sbuf_tensor("neghalf", [P, NT], F32))
        consts(nc, ident, neghalf)
        cross_attention(nc, a, x_in, ctx_in, x1, ident, neghalf)
        quantized_ffn(nc, a, x1, x2, raw_up, raw_gate, ident, neghalf)
        masked_attention(nc, a, x2, ctx_in, x3, ident, neghalf)
        lora_ffn(nc, a, x3, out_f, ident, neghalf)


def consts(nc, ident, neghalf):
    with Phase(nc, "c0") as ph:
        cleared = ph.sem("cleared")
        made = ph.sem("made")
        with nc.Block() as block:
            @block.gpsimd
            def _(pool):
                pool.memset(neghalf[:], -0.5).then_inc(made, 1)
                pool.memset(ident[:], 0.0).then_inc(cleared, 1)
                pool.wait_ge(cleared, 1)
                pool.affine_select(out=ident[:], in_=ident[:], compare_op=ALU.not_equal, fill=1.0, base=0,
                                   pattern=[[-1, P]], channel_multiplier=1).then_inc(made, 1)
                pool.wait_ge(made, 2)



def norm_stats(dve, st, mv, steps, mv_ready, spacer, x):
    for t in range(NT):
        n = steps.done(dve.bn_stats(st[:, t, :], x[:, t, :]))
    steps.eng.wait_ge(steps.sem, steps.base + n)
    dve.sem_inc(spacer, 1)
    for t in range(NT):
        ins = dve.bn_aggr(mv[:, t, :], st[:, t, :])
    ins.then_inc(mv_ready, 1)


def norm_rstd(pool, mv, var, rstd, neghalf, mv_ready, rstd_ready, var_done, it, spacer):
    wait_alone(pool, mv_ready, it + 1, spacer)
    pool.tensor_scalar(var[:], mv[:, :, 1], EPS, None, ALU.add).then_inc(var_done, 1)
    pool.wait_ge(var_done, it + 1)
    pool.tensor_tensor(rstd[:], var[:], neghalf[:], ALU.pow).then_inc(rstd_ready, 1)


def product(pe, out, left, right, start, stop, check=True):
    (lh, ll), (rh, rl) = left, right
    kw = {} if check else {"skip_group_check": True}
    pe.matmul(out, lh, rh, start=start, stop=False, **kw)
    pe.matmul(out, lh, rl, start=False, stop=False, **kw)
    return pe.matmul(out, ll, rh, start=False, stop=stop, **kw)


def cross_attention(nc, a, x_in, ctx_in, x1, ident, neghalf):
    xh = nc.dram_tensor("x1_half", (TOK, D), F32).ap()
    head_half(nc, a, 0, x_in, ctx_in, x_in, xh, ident, neghalf)
    head_half(nc, a, 1, x_in, ctx_in, xh, x1, ident, neghalf)


def head_half(nc, a, half, x_in, ctx_in, res, out, ident, neghalf):
    NP = NPAIR // 2
    U = 2 * NP
    NTE = S // P
    HC = NP * P
    IM0 = TEXT - 1
    IMP = P
    with Phase(nc, f"xa{half}") as ph:
        names = ("Wq", "Wk", "Wv", "Wk_ip", "Wv_ip")
        w = {n: ph.sb(n, [P, 2, KD, HC], F32R) for n in names}
        wo = ph.sb("Wo", [P, 2, NP, D], F32R)
        cols = slice(half * HC, (half + 1) * HC)
        pieces = [(a["L0_xattn_" + n][:, cols].rearrange("(k p) n -> p k n", p=P), w[n][:, 0], w[n][:, 1]) for n in names]
        pieces.append((a["L0_xattn_Wo"][cols, :].rearrange("(k p) n -> p k n", p=P), wo[:, 0], wo[:, 1]))
        split_pieces(nc, f"xw{half}", pieces, KD * HC)
        bo = ph.sb("bo", [P, D])
        xin = ph.sb("xin", [P, NTE, D])
        cin = ph.sb("cin", [P, NTE, D])
        y = ph.sb("y", [P, 2, NTE, D])
        st = ph.sb("st", [P, NTE, 6])
        mv = ph.sb("mv", [P, NTE, 2])
        var = ph.sb("var", [P, NTE])
        rstd = ph.sb("rstd", [P, NTE])
        xT = ph.sb("xT", [P, 2, 2, KD, S], F32R)
        cT = ph.sb("cT", [P, 2, 2, KD, S], F32R)
        q = ph.sb("q", [P, 2, 2, 2, S], F32R)
        kT = ph.sb("kT", [P, 2, 2, S], F32R)
        ktext = ph.sb("ktext", [P, 2, 2 * P])
        cimg = ph.sb("cimg", [P, 2, 2, KD, P], F32R)
        v = ph.sb("v", [P, 2, 2, NTE, 2 * P], F32R)
        pT = ph.sb("pT", [P, 2, 2, NTE, S], F32R)
        oT = ph.sb("oT", [P, 2, 2, NP, S], F32R)
        prob = ph.sb("prob", [P, 2, NTE, S])
        nm = ph.sb("nm", [P, 2, 2, NTE])
        sums = ph.sb("sums", [P, 2, 2, NTE])
        rec = ph.sb("rec", [P, 2, 2, NTE])
        pj = [ph.ps(f"pj{i}", [P, CT]) for i in range(2)]
        sc = [ph.ps(f"sc{i}", [P, NTE, S]) for i in range(2)]
        tp = [ph.ps(f"tp{i}", [P, NTE, S]) for i in range(2)]
        po = [ph.ps(f"po{i}", [P, 512]) for i in range(2)]
        bo_ready, q_clear = ph.sem("bo_ready"), ph.sem("q_clear")
        x_ready = [ph.sem(f"x_ready{i}") for i in range(NTE)]
        c_ready = [ph.sem(f"c_ready{i}") for i in range(NTE)]
        res_ready = [ph.sem(f"res_ready{i}") for i in range(2)]
        res_biased, y_done, stored = ph.sem("res_biased"), ph.sem("y_done"), ph.sem("stored")
        stat_done, mv_ready, var_done, rstd_ready, xn_ready = (ph.sem(n) for n in ("stat_done", "mv_ready", "var_done", "rstd_ready", "xn_ready"))
        spacer_d, spacer_p = ph.sem("spacer_d"), ph.sem("spacer_p")
        job_full, job_hi = ph.sem("job_full"), ph.sem("job_hi")
        job_done = [ph.sem(f"job_done{i}") for i in range(2)]
        s_full, max_done, exp_done, rec_done, norm_done = (ph.sem(n) for n in ("s_full", "max_done", "exp_done", "rec_done", "norm_done"))
        t_full, pt_hi, pt_done, pv_full, o_hi, o_done = (ph.sem(n) for n in ("t_full", "pt_hi", "pt_done", "pv_full", "o_hi", "o_done"))
        block = ph.block()
        SEG = [(0, TEXT), (TEXT, S)]

        FIRST = [("x", 0, 0), ("x", 0, 1), ("c", 0, 0), ("c", 0, 1), ("q", 0, 0), ("kt", 0, 0), ("v", 0, 1), ("k", 0, 0),
                 ("v", 0, 0), ("kt", 0, 1)]
        STEPS = [([("q", 0, 1)], [("k", 0, 1)]),
                 ([("q", 0, 2)], [("k", 0, 2)]),
                 ([("o", -1, 0)], [("x", 1, 0), ("v", 0, 3)]),
                 ([("o", -1, 1)], [("x", 1, 1), ("c", 1, 0)]),
                 ([("v", 0, 2)], [("c", 1, 1), ("q", 0, 3)]),
                 ([("k", 0, 3)], [("q", 1, 0)]),
                 ([("kt", 1, 0)], [("v", 1, 1), ("k", 1, 0)]),
                 ([("v", 1, 0)], [("kt", 1, 1)])]
        Q0, KT0, V01, K0, V00, KT1 = range(-6, 0)

        def jobs_of(first, last):
            plan = {(t, place): [j for j in jobs[place] if not (last and j[1] > 0) and not (first and j[1] < 0)]
                    for t, jobs in enumerate(STEPS) for place in range(2)}
            number, exact, numbered = 0, 0, {}
            for place in sorted(plan):
                numbered[place] = []
                for job in plan[place]:
                    numbered[place].append((number, exact, job))
                    number += 1
                    exact += job[0] not in ("o", "kt")
            return numbered, number, exact

        PER = jobs_of(False, False)[1]
        PER1, EX = jobs_of(True, False)[1:]
        EX0 = len(FIRST) - 2
        assert PER % 2 == 0 and PER1 % 2 == 0 and jobs_of(False, True)[1] % 2 == 0 and jobs_of(False, False)[2] == EX

        def job_base(c):
            return len(FIRST) if isinstance(c, int) and c == 0 else PER * c + (len(FIRST) + PER1 - PER)

        def base2(c):
            return job_base(c) // 2 if isinstance(c, int) else (PER // 2) * c + (len(FIRST) + PER1 - PER) // 2

        def number_of(kind, off, i, last=False, first=False):
            for l in jobs_of(first, last)[0].values():
                for n, e, job in l:
                    if job == (kind, off, i):
                        return n
            raise KeyError

        LASTJOBS = job_base(B - 1) + jobs_of(False, True)[1]

        def wait_taken(eng, c, n):
            eng.wait_ge(job_done[n % 2], base2(c) + n // 2 + 2)

        def wait_jobs(eng, c, taken, free=None):
            least = {}
            for n in taken:
                least[n % 2] = max(least.get(n % 2, -99), n // 2 + 2)
            if free is not None:
                least[free % 2] = max(least.get(free % 2, -99), free // 2 + 1)
            for b, value in least.items():
                eng.wait_ge(job_done[b], base2(c) + value)

        def elements(eng, body):
            body(0, 0, True, False)
            with eng.Fori(0, (B - 2) // 2) as i:
                body(2 * i + 1, 1, False, False)
                body(2 * i + 2, 0, False, False)
            body(B - 1, 1, False, True)

        def rows(ap, c, t):
            return ap[bass.ds(c * S + t * P, P), :]

        @block.sync
        def _(sp):
            if half == 0:
                sp.dma_start(bo[:], a["L0_xattn_bo"].rearrange("(o n) -> o n", o=1).broadcast_to([P, D])).then_inc(bo_ready, 16)
            for ap, tile, ready in ((x_in, xin, x_ready), (ctx_in, cin, c_ready)):
                for t in range(NTE):
                    sp.dma_start(tile[:, t, :], rows(ap, 0, t)).then_inc(ready[t], 16)

            def next_rows(ap, tile, ready, c, n, t):
                if n < 0:
                    n += len(FIRST)
                    sp.wait_ge(job_done[n % 2], n // 2 + 2)
                else:
                    wait_taken(sp, c - 1, n)
                sp.dma_start(tile[:, t, :], rows(ap, c + 1, t)).then_inc(ready[t], 16)

            def load_next(c, first, second):
                for kind, ap, tile, ready in (("x", x_in, xin, x_ready), ("c", ctx_in, cin, c_ready)):
                    for t in range(NTE):
                        n = FIRST.index((kind, 0, t)) - len(FIRST) if first else number_of(kind, 1, t, first=second)
                        next_rows(ap, tile, ready, c, n, t)

            def body(c, par, first, last):
                if not first:
                    if not last:
                        load_next(c, False, isinstance(c, int) and c == 1)
                if first:
                    load_next(c, True, False)
                if not (isinstance(c, int) and c == 0):
                    sp.wait_ge(stored, 16 * c)
                sp.dma_start(y[:, par], res[bass.ds(c * S, S), :].rearrange("(t p) d -> p t d", p=P)).then_inc(res_ready[par], 16)
                if not first:
                    sp.wait_ge(y_done, NTE * c)
                    sp.dma_start(out[bass.ds((c - 1) * S, S), :].rearrange("(t p) d -> p t d", p=P), y[:, 1 - par]).then_inc(stored, 16)

            sp.sem_inc(stored, 16)
            body(0, 0, True, False)
            body(1, 1, False, False)
            with sp.Fori(0, (B - 4) // 2) as i:
                body(2 * i + 2, 0, False, False)
                body(2 * i + 3, 1, False, False)
            body(B - 2, 0, False, False)
            body(B - 1, 1, False, True)
            sp.wait_ge(y_done, NTE * B)
            sp.dma_start(out[(B - 1) * S:B * S, :].rearrange("(t p) d -> p t d", p=P), y[:, 1]).then_inc(stored, 16)
            sp.wait_ge(stored, 16 * (B + 1))

        @block.gpsimd
        def _(pool):
            pool.memset(q[:].bitcast(F32), 0.0).then_inc(q_clear, 1)
            pool.memset(cimg[:].bitcast(F32), 0.0).then_inc(q_clear, 1)
            if half == 0:
                pool.wait_ge(bo_ready, 16)

            def scale_rows(c):
                wait_alone(pool, mv_ready, c + 1, spacer_p)
                pool.tensor_scalar(var[:], mv[:, :, 1], EPS, None, ALU.add).then_inc(var_done, 1)
                pool.wait_ge(var_done, c + 1)
                pool.tensor_tensor(rstd[:], var[:], neghalf[:, 0:NTE], ALU.pow).then_inc(rstd_ready, 1)

            scale_rows(0)

            def body(c, par, first, last):
                for t in range(U):
                    if t == 0 and not last:
                        scale_rows(c + 1)
                    n, i = U * c + t, t % 2
                    pool.wait_ge(rec_done, n + 1)
                    for g, (lo, hi) in enumerate(SEG):
                        ins = pool.tensor_tensor(prob[:, i, :, lo:hi], prob[:, i, :, lo:hi],
                                                 rec[:, i, g, :].unsqueeze(2).broadcast_to([P, NTE, hi - lo]), ALU.mult)
                    ins.then_inc(norm_done, 1)
                    if half == 0 and t == 5:
                        pool.wait_ge(res_ready[par], 8 * (c - par) + 16)
                        for tt in range(NTE):
                            ins = pool.tensor_tensor(y[:, par, tt, :], y[:, par, tt, :], bo[:], ALU.add)
                        ins.then_inc(res_biased, 1)
            elements(pool, body)

        @block.vector
        def _(dve):
            dve.wait_ge(q_clear, 2)

            def stats(c, par):
                for t in range(NTE):
                    dve.wait_ge(x_ready[t], 16 * c + 16)
                    dve.bn_stats(st[:, t, :], xin[:, t, :]).then_inc(stat_done, 1)
                wait_alone(dve, stat_done, NTE * c + NTE, spacer_d)
                for t in range(NTE):
                    ins = dve.bn_aggr(mv[:, t, :], st[:, t, :])
                ins.then_inc(mv_ready, 1)

            def normalize(c):
                dve.wait_ge(rstd_ready, c + 1)
                for t in range(NTE):
                    dve.tensor_scalar(xin[:, t, :], xin[:, t, :], mv[:, t, 0:1], rstd[:, t:t + 1], ALU.subtract, ALU.mult).then_inc(xn_ready, 1)

            def low_part(kind, par, i, bank, exact):
                minus = lambda o, x, h: dve.tensor_tensor(o, x, h.bitcast(F32), ALU.subtract)
                dve.wait_ge(job_hi, exact + 1)
                if kind in ("x", "c"):
                    to = (xT if kind == "x" else cT)[:, par, :, :, i * P:(i + 1) * P]
                    turned = bank[:].rearrange("p (k n) -> p k n", k=KD)
                    if kind == "c" and i == 0:
                        minus(cimg[:, par, 1, :, TEXT:P], turned[:, :, TEXT:P], cimg[:, par, 0, :, TEXT:P])
                    return minus(to[:, 1], turned, to[:, 0])
                if kind == "q":
                    for h in range(2):
                        r = slice(64 * h, 64 * h + 64)
                        ins = dve.scalar_tensor_tensor(q[r, i % 2, h, 1, :], bank[r, 0:S], DH ** -0.5, q[r, i % 2, h, 0, :].bitcast(F32),
                                                       ALU.mult, ALU.subtract)
                    return ins
                if kind == "k":
                    minus(kT[:, i % 2, 1, 0:TEXT], bank[:, 0:TEXT], kT[:, i % 2, 0, 0:TEXT])
                    return minus(kT[:, i % 2, 1, TEXT:S], bank[:, IMP + 1:IMP + S - IM0], kT[:, i % 2, 0, TEXT:S])
                return minus(v[:, i // 2, 1, i % 2], bank[:, 0:2 * P], v[:, i // 2, 0, i % 2])

            def take(c, par, number, exact, job):
                kind, off, i = job
                bank = pj[number % 2]
                if kind == "kt":
                    return
                if kind == "o":
                    prev = c - 1
                    dve.wait_ge(job_full, job_base(c) + number + 1)
                    output(prev, 1 - par, i, bank, number)
                    return
                low_part(kind, par if off == 0 else 1 - par, i, bank, exact).then_inc(job_done[number % 2], 1)

            def output(c, par, t, bank, number):
                if half == 0:
                    dve.wait_ge(res_biased, c + 1)
                else:
                    dve.wait_ge(res_ready[par], 8 * (c - par) + 16)
                dve.tensor_tensor(y[:, par, t, :], bank[:], y[:, par, t, :], ALU.add).then_inc(y_done, 1)
                dve.wait_ge(y_done, NTE * c + t + 1)
                dve.sem_inc(job_done[number % 2], 1)

            def turned_low(n, i):
                dve.wait_ge(pt_hi, n + 1)
                dve.tensor_tensor(pT[:, i, 1], tp[i][:], pT[:, i, 0].bitcast(F32), ALU.subtract).then_inc(pt_done, 1)

            def values_low(n, par, t):
                p, h = t // 2, t % 2
                r = slice(64 * h, 64 * h + 64)
                dve.wait_ge(o_hi, n + 1)
                dve.tensor_tensor(oT[r, par, 1, p, :], po[t % 2][r, 0:S], oT[r, par, 0, p, :].bitcast(F32), ALU.subtract).then_inc(o_done, 1)

            stats(0, 0)
            normalize(0)
            exact = 0
            for n, (kind, off, i) in enumerate(FIRST):
                if kind != "kt":
                    low_part(kind, 0, i, pj[n % 2], exact).then_inc(job_done[n % 2], 1)
                    exact += 1

            def body(c, par, first, last):
                plan = jobs_of(first, last)[0]
                for t in range(U):
                    n, i = U * c + t, t % 2
                    dve.wait_ge(s_full, n + 1)
                    dve.wait_ge(exp_done, n + 1)
                    for g, (lo, hi) in enumerate(SEG):
                        ins = dve.tensor_reduce(nm[:, i, g, :], sc[i][:, :, lo:hi], AX_X, ALU.max, negate=True)
                    ins.then_inc(max_done, 1)
                    if t == 0 and not last:
                        stats(c + 1, 1 - par)
                    if t == 1 and not last:
                        normalize(c + 1)
                    for number, exact, job in plan.get((t, 0), []):
                        take(c, par, number, EX * c + EX0 + exact, job)
                    dve.wait_ge(exp_done, n + 3)
                    dve.reciprocal(rec[:, i].rearrange("p a b -> p (a b)"), sums[:, i].rearrange("p a b -> p (a b)")).then_inc(rec_done, 1)
                    if not (first and t < 1):
                        turned_low(n - 1, 1 - i)
                    if not (first and t < 2):
                        values_low(n - 2, par if t > 1 else 1 - par, (t - 2) % U)
                    for number, exact, job in plan.get((t, 1), []):
                        take(c, par, number, EX * c + EX0 + exact, job)
            elements(dve, body)
            values_low(U * B - 2, 1, U - 2)
            turned_low(U * B - 1, 1)
            values_low(U * B - 1, 1, U - 1)
            for t in range(NTE):
                dve.wait_ge(job_full, LASTJOBS + t + 1)
                output(B - 1, 1, t, pj[(LASTJOBS + t) % 2], LASTJOBS + t)

        @block.scalar
        def _(act):
            act.wait_ge(q_clear, 2)

            def high_part(kind, par, i, bank):
                copy = lambda o, x: act.activation(o, x, ACT.Copy)
                if kind in ("x", "c"):
                    turned = bank[:].rearrange("p (k n) -> p k n", k=KD)
                    if kind == "c" and i == 0:
                        copy(cimg[:, par, 0, :, TEXT:P], turned[:, :, TEXT:P])
                    return copy((xT if kind == "x" else cT)[:, par, 0, :, i * P:(i + 1) * P], turned)
                if kind == "q":
                    for h in range(2):
                        r = slice(64 * h, 64 * h + 64)
                        ins = act.activation(q[r, i % 2, h, 0, :], bank[r, 0:S], ACT.Copy, scale=DH ** -0.5)
                    return ins
                if kind == "kt":
                    return copy(ktext[0:TEXT, i, :], bank[0:TEXT, 0:2 * P])
                if kind == "k":
                    copy(kT[:, i % 2, 0, 0:TEXT], bank[:, 0:TEXT])
                    return copy(kT[:, i % 2, 0, TEXT:S], bank[:, IMP + 1:IMP + S - IM0])
                return copy(v[:, i // 2, 0, i % 2], bank[:, 0:2 * P])

            def take(c, par, number, job):
                kind, off, i = job
                if kind == "o":
                    return
                act.wait_ge(job_full, job_base(c) + number + 1)
                high_part(kind, par if off == 0 else 1 - par, i, pj[number % 2]).then_inc(job_done[number % 2] if kind == "kt" else job_hi, 1)

            def turned_high(n, i):
                act.wait_ge(t_full, n + 3)
                act.wait_ge(pv_full, n + 1)
                act.activation(pT[:, i, 0], tp[i][:], ACT.Copy).then_inc(pt_hi, 1)

            def values_high(n, par, t):
                p, h = t // 2, t % 2
                r = slice(64 * h, 64 * h + 64)
                act.wait_ge(pv_full, n + 3)
                act.activation(oT[r, par, 0, p, :], po[t % 2][r, 0:S], ACT.Copy).then_inc(o_hi, 1)

            for n, (kind, off, i) in enumerate(FIRST):
                act.wait_ge(job_full, n + 1)
                high_part(kind, 0, i, pj[n % 2]).then_inc(job_done[n % 2] if kind == "kt" else job_hi, 1)

            def body(c, par, first, last):
                plan = jobs_of(first, last)[0]
                for t in range(U):
                    n, i = U * c + t, t % 2
                    act.wait_ge(max_done, n + 1)
                    act.wait_ge(t_full, n + 1)
                    for g, (lo, hi) in enumerate(SEG):
                        for m in range(NTE):
                            ins = act.activation(prob[:, i, m, lo:hi], sc[i][:, m, lo:hi], ACT.Exp, bias=nm[:, i, g, m:m + 1],
                                                 accum_out=sums[:, i, g, m:m + 1])
                    ins.then_inc(exp_done, 1)
                    for number, _, job in plan.get((t, 0), []):
                        take(c, par, number, job)
                    if not (first and t < 1):
                        turned_high(n - 1, 1 - i)
                    if not (first and t < 2):
                        values_high(n - 2, par if t > 1 else 1 - par, (t - 2) % U)
                    for number, _, job in plan.get((t, 1), []):
                        take(c, par, number, job)
            elements(act, body)
            values_high(U * B - 2, 1, U - 2)
            turned_high(U * B - 1, 1)
            values_high(U * B - 1, 1, U - 1)

        @block.tensor
        def _(pe):
            for s in job_done:
                pe.sem_inc(s, 1)
            for s in (exp_done, t_full, pt_done, pv_full, o_done):
                pe.sem_inc(s, 2)
            pe.wait_ge(q_clear, 2)

            def make(kind, par, i, bank):
                if kind in ("x", "c"):
                    tile = xin if kind == "x" else cin
                    for k in range(KD):
                        ins = pe.transpose(bank[:, k * P:(k + 1) * P], tile[:, i, k * P:(k + 1) * P], ident[:])
                    return ins
                if kind == "q":
                    cols = slice(i * P, (i + 1) * P)
                    for k in range(KD):
                        ins = product(pe, bank[:, 0:S], (w["Wq"][:, 0, k, cols], w["Wq"][:, 1, k, cols]), (xT[:, par, 0, k, :], xT[:, par, 1, k, :]),
                                      k == 0, k == KD - 1)
                    return ins
                if kind == "kt":
                    cols = slice(i * 2 * P, (i + 1) * 2 * P)
                    for k in range(KD):
                        ins = product(pe, bank[0:TEXT, 0:2 * P], [cT[:, par, part, k, 0:TEXT] for part in range(2)],
                                      (w["Wk"][:, 0, k, cols], w["Wk"][:, 1, k, cols]), k == 0, k == KD - 1)
                    return ins
                if kind == "k":
                    cols = slice(i * P, (i + 1) * P)
                    for k in range(KD):
                        product(pe, bank[:, IMP:IMP + S - IM0], (w["Wk_ip"][:, 0, k, cols], w["Wk_ip"][:, 1, k, cols]),
                                (cT[:, par, 0, k, IM0:S], cT[:, par, 1, k, IM0:S]), k == 0, k == KD - 1)
                    return pe.transpose(bank[:, 0:TEXT], ktext[0:TEXT, i // 2, i % 2 * P:(i % 2 + 1) * P], ident[0:TEXT, 0:TEXT])
                if kind == "v":
                    cols = slice(i // 2 * 2 * P, (i // 2 + 1) * 2 * P)
                    for k in range(KD):
                        keys = [cT[:, par, part, k, P:S] if i % 2 else cimg[:, par, part, k, :] for part in range(2)]
                        ins = product(pe, bank[:, 0:2 * P], keys, (w["Wv_ip"][:, 0, k, cols], w["Wv_ip"][:, 1, k, cols]), k == 0, k == KD - 1)
                    if i % 2 == 0:
                        for k in range(KD):
                            keys = [cT[:, par, part, k, 0:TEXT] for part in range(2)]
                            ins = product(pe, bank[0:TEXT, 0:2 * P], keys, (w["Wv"][:, 0, k, cols], w["Wv"][:, 1, k, cols]), False, False, check=False)
                    return ins
                for p in range(NP):
                    rows_ = slice(i * P, (i + 1) * P)
                    ins = product(pe, bank[:], (oT[:, par, 0, p, rows_], oT[:, par, 1, p, rows_]), (wo[:, 0, p, :], wo[:, 1, p, :]), p == 0, p == NP - 1)
                return ins

            def job_of(c, par, number, job, plan_first, plan_last):
                kind, off, i = job
                taken = []
                if kind == "x":
                    pe.wait_ge(xn_ready, NTE * (c + off) + i + 1)
                if kind == "c":
                    pe.wait_ge(c_ready[i], 16 * (c + off) + 16)
                if kind in ("q", "kt") and off:
                    taken = [number_of("x" if kind == "q" else "c", 1, t, plan_last, plan_first) for t in range(NTE)]
                if kind == "k":
                    taken = [number_of("kt", 1, 0, plan_last, plan_first) if off else KT0 if i < 2 else KT1]
                wait_jobs(pe, c, taken, number)
                if kind == "o" and i == 0:
                    pe.wait_ge(o_done, U * c + 2)
                make(kind, par if off == 0 else 1 - par, i, pj[number % 2]).then_inc(job_full, 1)

            def scores(c, par, t):
                n, i, p, h = U * c + t, t % 2, t // 2, t % 2
                pe.wait_ge(exp_done, n + 1)
                for m in range(NTE):
                    rows_ = slice(m * P, (m + 1) * P)
                    ins = product(pe, sc[i][:, m, :], (q[:, p % 2, h, 0, rows_], q[:, p % 2, h, 1, rows_]), (kT[:, p % 2, 0, :], kT[:, p % 2, 1, :]), True, True)
                ins.then_inc(s_full, 1)

            def turn(n, i):
                pe.wait_ge(norm_done, n + 1)
                pe.wait_ge(pt_done, n + 1)
                for k in range(NTE):
                    for m in range(NTE):
                        ins = pe.transpose(tp[i][:, k, m * P:(m + 1) * P], prob[:, i, m, k * P:(k + 1) * P], ident[:])
                ins.then_inc(t_full, 1)

            def values(n, t):
                i, p = t % 2, t // 2
                cols = slice(p % 2 * P, (p % 2 + 1) * P)
                pe.wait_ge(pt_done, n + 3)
                pe.wait_ge(o_done, n + 1)
                for k in range(NTE):
                    ins = product(pe, po[i][:, 0:S], (v[:, p // 2, 0, k, cols], v[:, p // 2, 1, k, cols]), (pT[:, i, 0, k, :], pT[:, i, 1, k, :]), k == 0, k == NTE - 1)
                ins.then_inc(pv_full, 1)

            for n, (kind, off, i) in enumerate(FIRST):
                pe.wait_ge(job_done[n % 2], n // 2 + 1)
                if kind == "x":
                    pe.wait_ge(xn_ready, i + 1)
                elif kind == "c":
                    pe.wait_ge(c_ready[i], 16)
                else:
                    pe.wait_ge(job_done[1 - n % 2], (n - 1) // 2 + 2)
                make(kind, 0, i, pj[n % 2]).then_inc(job_full, 1)

            def body(c, par, first, last):
                plan = jobs_of(first, last)[0]
                for t in range(U):
                    n, i, p = U * c + t, t % 2, t // 2
                    if t == 0:
                        wait_jobs(pe, c, (Q0, K0))
                    elif t % 2 == 0:
                        wait_jobs(pe, c, [number_of(kind, 0, p, last, first) for kind in ("q", "k")])
                    scores(c, par, t)
                    for number, _, job in plan.get((t, 0), []):
                        job_of(c, par, number, job, first, last)
                    if not (first and t < 1):
                        turn(n - 1, 1 - i)
                    if not (first and t < 2):
                        if t in (2, 6):
                            wait_jobs(pe, c, (V01, V00) if t == 2 else [number_of("v", 0, j, last, first) for j in (2, 3)])
                        values(n - 2, (t - 2) % U)
                    for number, _, job in plan.get((t, 1), []):
                        job_of(c, par, number, job, first, last)

            elements(pe, body)
            values(U * B - 2, U - 2)
            turn(U * B - 1, 1)
            values(U * B - 1, U - 1)
            pe.wait_ge(o_done, U * B + 2)
            for t in range(NTE):
                g = LASTJOBS + t
                pe.wait_ge(job_done[g % 2], g // 2 + 1)
                make("o", 1, t, pj[g % 2]).then_inc(job_full, 1)


SUB = 6
SC = KF * CT // SUB
MS = KF // SUB
S_X, I_X, S_G, I_G, S_U, I_U, S_A, I_A, S_O, I_O, S_AU = range(11)


def chunk_loop(eng, body):
    body(0, 0, True, False, 0)
    with eng.Fori(0, (NCH - 2) // 2) as i:
        body(2 * i + 1, 1, False, False, i)
        body(2 * i + 2, 0, False, False, i + 1)
    body(NCH - 1, 1, False, True, NCH // 2 - 1)


def integers_times_scale(dve, c, raw, amax, scale, inv, whole, deq):
    shape = list(raw.shape)
    c.done(dve.tensor_reduce(amax, raw, AX_X, ALU.max, apply_absolute_value=True))
    c.wait()
    c.done(dve.tensor_scalar(scale, amax, 1.0 / WMAX, TINY, ALU.mult, ALU.max))
    c.wait()
    c.done(dve.reciprocal(inv, scale))
    c.wait()
    c.done(dve.tensor_tensor(whole, raw, inv.unsqueeze(2).broadcast_to(shape), ALU.mult))
    c.wait()
    return dve.tensor_tensor(deq, whole, scale.unsqueeze(2).broadcast_to(shape), ALU.mult)


class Meanwhile:
    PIECES, STEPS = 3, 4

    def __init__(self, nc, ph, w_up, w_down, wu, wd_parts, ident):
        n, nq = self.PIECES, D // QB
        self.w_up, self.w_down, self.wu, self.wd_parts, self.ident = w_up, w_down, wu, wd_parts, ident
        self.raw = ph.sb("w_raw", [P, n, nq, QB])
        self.amax, self.scale, self.inv = (ph.sb(f"w_{x}", [P, n, nq]) for x in ("amax", "scale", "inv"))
        self.whole = ph.sb("w_whole", [P, nq, QB], I16)
        self.deq = ph.sb("w_deq", [P, n, nq, QB])
        self.out = ph.sb("w_out", [P, n, 2, KD, P], F32R)
        self.turned = [ph.ps(f"w_turned{i}", [P, KD, P]) for i in range(n)]
        self.raw_ready = [ph.sem(f"w_raw_ready{i}") for i in range(n)]
        self.stored = [ph.sem(f"w_stored{i}") for i in range(n)]
        self.steps, self.deq_ready, self.turned_full, self.hi_done, self.placed, self.spacer = (
            ph.sem(f"w_{x}") for x in ("steps", "deq_ready", "turned_full", "hi_done", "placed", "spacer"))

    def place(self, par, half, m, part):
        if par:
            return self.out[:, m, part]
        return self.wu[:, part, :, bass.ds(half * (self.PIECES * P) + m * P, P)]

    def load(self, sp, c, par, half, m):
        sp.wait_ge(self.deq_ready, self.PIECES * c + m + 1)
        src = self.w_down[bass.ds(half * P, P), m * D:(m + 1) * D] if par else self.w_up[bass.ds(half * (self.PIECES * P) + m * P, P), :]
        sp.dma_start(self.raw[:, m], src.rearrange("p (a b) -> p a b", b=QB)).then_inc(self.raw_ready[m], 16)

    def prefill(self, sp):
        sp.sem_inc(self.deq_ready, self.PIECES)
        for s in self.stored:
            sp.sem_inc(s, 32)
        for m in range(self.PIECES):
            self.load(sp, 0, 0, 0, m)

    def sync_step(self, sp, c, par, last, half, j):
        if j % 4 != 3:
            return
        m = j // 4
        if par:
            wait_alone(sp, self.placed, self.PIECES * c + m + 1 + self.PIECES, self.spacer)
            for part in range(2):
                sp.dma_start(self.wd_parts[:, part, m * KD:(m + 1) * KD, bass.ds(half * P, P)].bitcast(F32), self.out[:, m, part].bitcast(F32)
                             ).then_inc(self.stored[m], 16)
        if not last:
            self.load(sp, c + 1, 1 - par, half + par, m)

    def finish(self, sp):
        for s in self.stored:
            sp.wait_ge(s, 32 * (NCH // 2) + 32)

    def vector_step(self, dve, c, par, half, j):
        m = j // 4
        n = self.PIECES * c + m
        if j % 4 == 0:
            if j == 0 and isinstance(c, int) and c == 0:
                dve.sem_inc(self.turned_full, self.PIECES)
            dve.wait_ge(self.raw_ready[m], 16 * c + 16)
            dve.wait_ge(self.turned_full, n + 1)
            count = Count(dve, self.steps, self.STEPS * n)
            integers_times_scale(dve, count, self.raw[:, m], self.amax[:, m], self.scale[:, m], self.inv[:, m], self.whole[:],
                                 self.deq[:, m]).then_inc(self.deq_ready, 1)
            assert count.n == self.STEPS
        if j % 4 == 3:
            dve.wait_ge(self.hi_done, n + 1)
            dve.tensor_tensor(self.place(par, half, m, 1), self.turned[m][:], self.place(par, half, m, 0).bitcast(F32), ALU.subtract
                              ).then_inc(self.placed, 1)

    def tensor_step(self, pe, c, j):
        if j == 0 and isinstance(c, int) and c == 0:
            pe.sem_inc(self.placed, self.PIECES)
        if j % 4 == 2:
            m = j // 4
            n = self.PIECES * c + m
            pe.wait_ge(self.deq_ready, n + 1 + self.PIECES)
            pe.wait_ge(self.placed, n + 1)
            rows = self.deq[:, m].rearrange("p a b -> p (a b)")
            for k in range(KD):
                ins = pe.transpose(self.turned[m][:, k, :], rows[:, k * P:(k + 1) * P], self.ident[:])
            ins.then_inc(self.turned_full, 1)

    def scalar_step(self, act, c, par, half, j):
        if j % 4 == 2:
            m = j // 4
            n = self.PIECES * c + m
            if par:
                act.wait_ge(self.stored[m], 32 * half + 32)
            wait_alone(act, self.turned_full, n + 1 + self.PIECES, self.spacer)
            act.activation(self.place(par, half, m, 0), self.turned[m][:], ACT.Copy).then_inc(self.hi_done, 1)


def dequantize(nc, name, loops, pieces, ident):
    n = len(pieces)
    NQ = D // QB
    with Phase(nc, name) as ph:
        raw = ph.sb("raw", [P, n, NQ, QB])
        amax = ph.sb("amax", [P, n, NQ])
        scale = ph.sb("scale", [P, n, NQ])
        inv = ph.sb("inv", [P, n, NQ])
        whole = ph.sb("whole", [P, NQ, QB], I16)
        deq = ph.sb("deq", [P, n, NQ, QB])
        turned = [ph.ps(f"turned{i}", [P, KD, P]) for i in range(n)]
        raw_ready = [ph.sem(f"raw_ready{i}") for i in range(n)]
        steps_done, deq_ready, turned_full = ph.sem("steps"), ph.sem("deq_ready"), ph.sem("turned_full")
        hi_done, placed = ph.sem("hi_done"), ph.sem("placed")
        spacer = ph.sem("spacer")
        STEPS = 4
        with nc.Block() as block:
            @block.sync
            def _(sp):
                sp.sem_inc(deq_ready, n)
                with sp.Fori(0, loops) as it:
                    for i, (src, _) in enumerate(pieces):
                        sp.wait_ge(deq_ready, n * it + i + 1)
                        sp.dma_start(raw[:, i], src(it).rearrange("p (a b) -> p a b", b=QB)).then_inc(raw_ready[i], 16)

            @block.vector
            def _(dve):
                def integers(it, i):
                    c = Count(dve, steps_done, (n * STEPS) * it + i * STEPS)
                    dve.wait_ge(raw_ready[i], 16 * it + 16)
                    integers_times_scale(dve, c, raw[:, i], amax[:, i], scale[:, i], inv[:, i], whole[:], deq[:, i]).then_inc(deq_ready, 1)
                    assert c.n == STEPS

                def low_part(it, i):
                    dst = pieces[i][1]
                    dve.wait_ge(hi_done, n * it + i + 1)
                    dve.tensor_tensor(dst(it, 1), turned[i][:], dst(it, 0).bitcast(F32), ALU.subtract).then_inc(placed, 1)

                with dve.Fori(0, loops) as it:
                    for i in range(n):
                        integers(it, i)
                        if i:
                            low_part(it, i - 1)
                    low_part(it, n - 1)

            @block.tensor
            def _(pe):
                pe.sem_inc(placed, n)
                with pe.Fori(0, loops) as it:
                    for i in range(n):
                        pe.wait_ge(deq_ready, n * it + i + 1 + n)
                        pe.wait_ge(placed, n * it + i + 1)
                        rows = deq[:, i].rearrange("p a b -> p (a b)")
                        for k in range(KD):
                            ins = pe.transpose(turned[i][:, k, :], rows[:, k * P:(k + 1) * P], ident[:])
                        ins.then_inc(turned_full, 1)

            @block.scalar
            def _(act):
                with act.Fori(0, loops) as it:
                    for i, (_, dst) in enumerate(pieces):
                        wait_alone(act, turned_full, n * it + i + 1, spacer)
                        act.activation(dst(it, 0), turned[i][:], ACT.Copy).then_inc(hi_done, 1)


def quantized_ffn(nc, a, x1, x2, raw_up, raw_gate, ident, neghalf):
    xq = nc.dram_tensor("xq", (NCH, P, KD * CT), I16).ap()
    wd_parts = nc.dram_tensor("wd_parts", (P, 2, KF, D), F32R).ap()

    def pieces_of(w, parts, rows_per):
        return [(lambda it, r=r: w[bass.ds(it * (rows_per * P) + r * P, P), :],
                 lambda it, part, r=r: parts[:, part, :, bass.ds(it * (rows_per * P) + r * P, P)]) for r in range(rows_per)]

    with Phase(nc, "qf") as top:
        scal = top.sb("scal", [P, 16])
        big = top.sb("big", [P, 4])
        with ExitStack() as gates:
            with Phase(nc, "qu") as mid:
                wu = mid.sb("wu", [P, 2, KD, FF], F32R)
                with Phase(nc, "qg") as low:
                    wg = low.sb("wg", [P, 2, KD, FF], F32R)
                    dequantize(nc, "qwg", KF // 4, pieces_of(a["L0_ffn_w_gate"], wg, 4), ident)
                    normalize_all(nc, x1, xq, big, scal, ident, neghalf)
                    project(nc, "pg", xq, wg, raw_gate, big, S_G, I_G, scal, meanwhile=lambda ph: Meanwhile(
                        nc, ph, a["L0_ffn_w_up"], a["L0_ffn_w_down"], wu, wd_parts, ident))
                gate = gates.enter_context(nc.sbuf_tensor("qf_gate", [P, NCH * KF * CT], I16, side="right"))
                project(nc, "pu", xq, wu, raw_up, big, S_U, I_U, scal, raw_gate, gate)
            wd = top.sb("wd", [P, 2, KF, D], F32R)
            output_maximum(nc, raw_up, gate, big, scal, wd, wd_parts)
            down(nc, x1, x2, raw_up, gate, wd, scal)


def scale_of(dve, c, scal, big_col, scale, inverse, unit, raw):
    def col(i):
        return scal[:, i:i + 1]
    if unit is None:
        c.done(dve.tensor_scalar(col(scale), big_col, 1.0 / AMAX, TINY, ALU.mult, ALU.max))
        c.wait()
        c.done(dve.reciprocal(col(inverse), col(scale)))
        c.wait()
        return
    c.done(dve.tensor_scalar(col(scale), big_col, col(unit), raw / AMAX, ALU.mult, ALU.mult))
    c.wait()
    c.done(dve.tensor_scalar(col(scale), col(scale), TINY, None, ALU.max))
    c.wait()
    c.done(dve.reciprocal(col(inverse), col(scale)))
    c.wait()
    c.done(dve.tensor_scalar(col(inverse), col(inverse), col(unit), raw, ALU.mult, ALU.mult))
    c.wait()


def normalize_all(nc, x1, xq, big, scal, ident, neghalf):
    with Phase(nc, "na") as ph:
        xn = ph.sb("xn", [P, NCH, NT * D])
        with Phase(nc, "nr") as rows:
            normalized_rows(nc, rows, x1, xn, big, scal, neghalf)
        stage = ph.sb("stage", [P, 2, KD, CT], I16)
        bank = [ph.ps(f"bank{i}", [P, CT]) for i in range(2 * KD)]
        filled = ph.sem("filled")
        turned = [ph.sem("turned_act"), ph.sem("turned_dve")]
        stored = [ph.sem(f"stored{i}") for i in range(2)]
        with nc.Block() as block:
            def take(eng, it, half, e, op):
                for k in range(e, KD, 2):
                    eng.wait_ge(filled, 2 * KD * it + half * KD + k + 1)
                    if k == e:
                        eng.wait_ge(stored[half], 16 * it + 16)
                    op(stage[:, half, k, :], bank[half * KD + k][:]).then_inc(turned[e], 1)

            @block.tensor
            def _(pe):
                for e in range(2):
                    pe.sem_inc(turned[e], 4)
                for c in range(NCH):
                    for k in range(KD):
                        pe.wait_ge(turned[k % 2], 2 * c + k // 2 + 1)
                        for t in range(NT):
                            ins = pe.transpose(bank[c % 2 * KD + k][:, t * P:(t + 1) * P], xn[:, c, t * D + k * P:t * D + (k + 1) * P], ident[:])
                        ins.then_inc(filled, 1)

            @block.scalar
            def _(act):
                with act.Fori(0, NCH // 2) as it:
                    for half in range(2):
                        take(act, it, half, 0, lambda o, i: act.activation(o, i, ACT.Copy, scale=scal[:, I_X:I_X + 1]))

            @block.vector
            def _(dve):
                with dve.Fori(0, NCH // 2) as it:
                    for half in range(2):
                        take(dve, it, half, 1, lambda o, i: dve.tensor_scalar(o, i, scal[:, I_X:I_X + 1], None, ALU.mult))

            @block.sync
            def _(sp):
                for s in stored:
                    sp.sem_inc(s, 16)
                with sp.Fori(0, NCH // 2) as it:
                    for half in range(2):
                        for e in range(2):
                            sp.wait_ge(turned[e], 4 * it + 2 * half + 2 + 4)
                        sp.dma_start(xq[bass.ds(2 * it + half, 1)].rearrange("a p n -> p (a n)"),
                                     stage[:, half].rearrange("p k n -> p (k n)")).then_inc(stored[half], 16)
                for s in stored:
                    sp.wait_ge(s, 16 * (NCH // 2 + 1))


def normalized_rows(nc, ph, x1, xn, big, scal, neghalf):
    xin = ph.sb("xin", [P, 2, NT, D])
    st = ph.sb("st", [P, 2, NT, 6])
    mv = ph.sb("mv", [P, 2, NT, 2])
    var = ph.sb("var", [P, NT])
    rstd = ph.sb("rstd", [P, 2, NT])
    shift = ph.sb("shift", [P, 2, NT])
    mx = ph.sb("mx", [P, NCH])
    mx_row = ph.sb("mx_row", [P, 1])
    x_ready = [ph.sem(f"x_ready{i}") for i in range(2)]
    xn_ready, max_done, row_max, all_max, settled = (ph.sem(n) for n in ("xn_ready", "max_done", "row_max", "all_max", "settled"))
    steps_done, mv_ready, shift_ready, scale_steps = (ph.sem(n) for n in ("steps", "mv_ready", "shift_ready", "scale_steps"))
    spacer_d, spacer_p, spacer_a = ph.sem("spacer_d"), ph.sem("spacer_p"), ph.sem("spacer_a")
    block = ph.block()

    @block.sync
    def _(sp):
        sp.sem_inc(xn_ready, 2)
        with sp.Fori(0, NCH // 2) as it:
            for i in range(2):
                sp.wait_ge(xn_ready, 2 * it + i + 1)
                sp.dma_start(xin[:, i], tokens(x1, 2 * it + i)).then_inc(x_ready[i], 16)

    @block.gpsimd
    def _(pool):
        with pool.Fori(0, NCH // 2) as it:
            for i in range(2):
                c = 2 * it + i
                steps = Count(pool, scale_steps, 3 * c)
                wait_alone(pool, mv_ready, c + 1, spacer_p)
                steps.done(pool.tensor_scalar(var[:], mv[:, i, :, 1], EPS, None, ALU.add))
                steps.wait()
                pool.wait_ge(xn_ready, c + 1)
                steps.done(pool.tensor_tensor(rstd[:, i, :], var[:], neghalf[:], ALU.pow))
                steps.wait()
                steps.done(pool.tensor_tensor(shift[:, i, :], mv[:, i, :, 0], rstd[:, i, :], ALU.mult))
                wait_alone(pool, scale_steps, 3 * c + 3, spacer_p)
                pool.tensor_scalar(shift[:, i, :], shift[:, i, :], -1.0, None, ALU.mult).then_inc(shift_ready, 1)
        pool.wait_ge(row_max, 1)
        pool.partition_all_reduce(big[:, 0:1], mx_row[:], P, RMAX).then_inc(all_max, 1)

    @block.scalar
    def _(act):
        with act.Fori(0, NCH // 2) as it:
            for i in range(2):
                c = 2 * it + i
                act.wait_ge(x_ready[i], 16 * it + 16)
                wait_alone(act, shift_ready, c + 1, spacer_a)
                for t in range(NT):
                    ins = act.activation(xn[:, bass.ds(c, 1), t * D:(t + 1) * D].rearrange("p a n -> p (a n)"), xin[:, i, t, :], ACT.Identity,
                                         bias=shift[:, i, t:t + 1], scale=rstd[:, i, t:t + 1])
                ins.then_inc(xn_ready, 1)

    @block.vector
    def _(dve):
        def statistics(c, i, half):
            dve.wait_ge(x_ready[i], 16 * half + 16)
            if not (isinstance(c, int) and c < 2):
                dve.wait_ge(shift_ready, c - 1)
            norm_stats(dve, st[:, i], mv[:, i], Count(dve, steps_done, NT * c), mv_ready, spacer_d, xin[:, i])

        def largest(c):
            dve.wait_ge(xn_ready, c + 3)
            dve.tensor_reduce(mx[:, bass.ds(c, 1)], xn[:, bass.ds(c, 1), :].rearrange("p a n -> p (a n)"), AX_X, ALU.max,
                              apply_absolute_value=True).then_inc(max_done, 1)

        statistics(0, 0, 0)
        statistics(1, 1, 0)
        with dve.Fori(0, NCH // 2 - 1) as it:
            for i in range(2):
                largest(2 * it + i)
                statistics(2 * it + i + 2, i, it + 1)
        largest(NCH - 2)
        largest(NCH - 1)
        dve.wait_ge(max_done, NCH)
        dve.tensor_reduce(mx_row[:], mx[:], AX_X, ALU.max).then_inc(row_max, 1)
        dve.wait_ge(all_max, 1)
        scale_of(dve, Count(dve, settled), scal, big[:, 0:1], S_X, I_X, None, None)


def project(nc, name, xq, w, raw, big, scale, inverse, scal, raw_gate=None, gate=None, meanwhile=None):
    NBANK = 4
    NR = 3
    LAG = 1
    with Phase(nc, name) as ph:
        xi = ph.sb("xi", [P, 2, KD * CT], I16)
        xs = ph.sb("xs", [P, 2, 2, KD, CT], F32R)
        stage = ph.sb("stage", [P, NBANK, CT])
        mx = {0: ph.sb("mx", [P, NCH * KF])}
        mx_row = {0: ph.sb("mx_row", [P, 1])}
        if gate is not None:
            rg = ph.sb("rg", [P, NR, CT])
            sig = ph.sb("sig", [P, 2, CT])
            sq = ph.sb("sq", [P, CT], U16)
            prod = ph.sb("prod", [P, CT])
            mx[1] = ph.sb("mxg", [P, NCH * KF])
            mx_row[1] = ph.sb("mxg_row", [P, 1])
        bank = [ph.ps(f"bank{i}", [P, CT]) for i in range(NBANK)]
        xi_ready = [ph.sem(f"xi_ready{i}") for i in range(2)]
        x_hi, x_lo = ph.sem("x_hi"), ph.sem("x_lo")
        r_full, r_copied, max_done = ph.sem("r_full"), ph.sem("r_copied"), ph.sem("max_done")
        stored = [ph.sem(f"stored{i}") for i in range(NBANK)]
        rg_ready = [ph.sem(f"rg_ready{i}") for i in range(NR)]
        g_ready, sig_ready, sq_done, prod_done, prod_max = (ph.sem(n) for n in ("g_ready", "sig_ready", "sq_done", "prod_done", "prod_max"))
        row_max, all_max, settled, spacer, spacer_s = (ph.sem(n) for n in ("row_max", "all_max", "settled", "spacer", "spacer_s"))
        side = meanwhile(ph) if meanwhile else None
        SPLIT = 5

        with nc.Block() as block:
            def gate_place(c, j):
                return gate[:, bass.ds(c * (KF * CT) + j * CT, CT)]

            @block.sync
            def _(sp):
                sp.sem_inc(x_lo, 2)
                for s in stored:
                    sp.sem_inc(s, 16)

                def load_rows(c, par):
                    sp.wait_ge(x_lo, c + 1)
                    sp.dma_start(xi[:, par], xq[bass.ds(c, 1)].rearrange("a p n -> p (a n)")).then_inc(xi_ready[par], 16)

                def load_gate(c, j):
                    sp.wait_ge(g_ready, KF * c + j + 1)
                    sp.dma_start(rg[:, j % NR, :], raw_gate[bass.ds(c, 1), :, (j % KF) * CT:(j % KF + 1) * CT].rearrange("a p n -> p (a n)")
                                 ).then_inc(rg_ready[j % NR], 16)

                load_rows(0, 0)
                if side:
                    side.prefill(sp)
                if gate is not None:
                    sp.sem_inc(g_ready, NR)
                    load_gate(0, 0)
                    load_gate(0, 1)

                def body(c, par, first, last, half):
                    if not last:
                        load_rows(c + 1, 1 - par)
                    for j in range(KF):
                        if gate is not None and not (last and j + 2 >= KF):
                            nxt = j + 2 >= KF
                            load_gate(c + 1 if nxt else c, j + 2 - KF if nxt else j + 2)
                        wait_alone(sp, r_copied, KF * c + j + 1 + NBANK, spacer_s)
                        sp.dma_start(raw[bass.ds(c, 1), :, j * CT:(j + 1) * CT].rearrange("a p n -> p (a n)"), stage[:, j % NBANK, :]
                                     ).then_inc(stored[j % NBANK], 16)
                        if side:
                            side.sync_step(sp, c, par, last, half, j)
                chunk_loop(sp, body)
                for s in stored:
                    sp.wait_ge(s, 16 * (KF // NBANK * NCH + 1))
                if side:
                    side.finish(sp)

            @block.scalar
            def _(act):
                act.sem_inc(max_done, NBANK)
                if gate is not None:
                    act.sem_inc(sq_done, 2)

                def high_part(c, par, half):
                    act.wait_ge(xi_ready[par], 16 * half + 16)
                    if not (isinstance(c, int) and c < 2):
                        act.wait_ge(r_full, KF * (c - 1))
                    act.activation(xs[:, par, 0].rearrange("p k n -> p (k n)"), xi[:, par], ACT.Copy).then_inc(x_hi, 1)

                def gates(c, j):
                    wait_alone(act, rg_ready[j % NR], 16 * (KF // NR) * c + 16 * (j // NR) + 16, spacer)
                    act.activation(gate_place(c, j), rg[:, j % NR, :], ACT.Copy, scale=scal[:, I_G:I_G + 1]).then_inc(g_ready, 1)
                    act.wait_ge(sq_done, KF * c + j + 1)
                    wait_alone(act, g_ready, KF * c + j + 1 + NR, spacer)
                    act.activation(sig[:, j % 2, :], gate_place(c, j), ACT.Sigmoid, scale=scal[:, S_G:S_G + 1]).then_inc(sig_ready, 1)

                high_part(0, 0, 0)

                def body(c, par, first, last, half):
                    for j in range(KF):
                        i = j % NBANK
                        if gate is not None:
                            gates(c, j)
                        if side:
                            side.scalar_step(act, c, par, half, j)
                        if j == SPLIT and not last:
                            high_part(c + 1, 1 - par, half + (1 if par else 0))
                        act.wait_ge(r_full, KF * c + j + 1)
                        act.wait_ge(stored[i], 16 * (KF // NBANK) * c + 16 * (j // NBANK) + 16)
                        act.wait_ge(max_done, KF * c + j + 1)
                        act.activation(stage[:, i, :], bank[i][:], ACT.Copy).then_inc(r_copied, 1)
                chunk_loop(act, body)

            @block.vector
            def _(dve):
                def low_part(c, par):
                    dve.wait_ge(x_hi, c + 1)
                    dve.tensor_tensor(xs[:, par, 1].rearrange("p k n -> p (k n)"), xi[:, par],
                                      xs[:, par, 0].rearrange("p k n -> p (k n)").bitcast(F32), ALU.subtract).then_inc(x_lo, 1)

                def gates(c, j):
                    n = KF * c + j
                    dve.wait_ge(sig_ready, n + 1)
                    dve.tensor_scalar(sq[:], sig[:, j % 2, :], SIGQ, SIGQ - 1, ALU.mult, ALU.min).then_inc(sq_done, 1)
                    dve.wait_ge(sq_done, n + 3)
                    dve.tensor_tensor(prod[:], gate_place(c, j), sq[:], ALU.mult).then_inc(prod_done, 1)
                    dve.wait_ge(prod_done, n + 1)
                    dve.tensor_reduce(mx[1][:, bass.ds(n, 1)], prod[:], AX_X, ALU.max, apply_absolute_value=True).then_inc(prod_max, 1)

                low_part(0, 0)

                def body(c, par, first, last, half):
                    for j in range(KF):
                        if gate is not None:
                            gates(c, j)
                        if side:
                            side.vector_step(dve, c, par, half, j)
                        if j == SPLIT and not last:
                            low_part(c + 1, 1 - par)
                        dve.wait_ge(r_copied, KF * c + j + 1 + NBANK)
                        dve.tensor_reduce(mx[0][:, bass.ds(c * KF + j, 1)], stage[:, j % NBANK, :], AX_X, ALU.max,
                                          apply_absolute_value=True).then_inc(max_done, 1)
                chunk_loop(dve, body)
                dve.wait_ge(max_done, KF * NCH + NBANK)
                if gate is not None:
                    dve.wait_ge(prod_max, KF * NCH)
                for i in mx:
                    dve.tensor_reduce(mx_row[i][:], mx[i][:], AX_X, ALU.max).then_inc(row_max, 1)
                dve.wait_ge(all_max, len(mx))
                count = Count(dve, settled)
                scale_of(dve, count, scal, big[:, 0:1], scale, inverse, S_X, 1.0)
                if gate is not None:
                    scale_of(dve, count, scal, big[:, 1:2], S_A, I_A, S_G, 1.0 / SIGQ)

            @block.gpsimd
            def _(pool):
                pool.wait_ge(row_max, len(mx))
                for i in mx:
                    pool.partition_all_reduce(big[:, i:i + 1], mx_row[i][:], P, RMAX).then_inc(all_max, 1)

            @block.tensor
            def _(pe):
                pe.sem_inc(r_copied, NBANK)

                def body(c, par, first, last, half):
                    pe.wait_ge(x_lo, c + 3)
                    for j in range(KF):
                        if side:
                            side.tensor_step(pe, c, j)
                        pe.wait_ge(r_copied, KF * c + j + 1)
                        cols = slice(j * P, (j + 1) * P)
                        for k in range(KD):
                            ins = product(pe, bank[j % NBANK][:], (w[:, 0, k, cols], w[:, 1, k, cols]), (xs[:, par, 0, k, :], xs[:, par, 1, k, :]),
                                          k == 0, k == KD - 1)
                        ins.then_inc(r_full, 1)
                chunk_loop(pe, body)


def part(raw, it, s):
    return raw[bass.ds(it, 1), :, s * SC:(s + 1) * SC].rearrange("a p n -> p (a n)")


def output_maximum(nc, raw_up, gate, big, scal, wd, wd_parts):
    with Phase(nc, "om") as ph:
        raw = ph.sb("raw", [P, 2, SC])
        sig = ph.sb("sig", [P, 2, SC])
        up = ph.sb("up", [P, 2, SC], I16)
        sq = ph.sb("sq", [P, SC], U16)
        prod = ph.sb("prod", [P, 2, SC])
        outp = ph.sb("outp", [P, SC])
        mx = ph.sb("mx", [P, NCH * SUB])
        mx_row = ph.sb("mx_row", [P, 1])
        raw_ready = [ph.sem(f"raw_ready{i}") for i in range(2)]
        up_ready, sig_ready, sq_done, prod_done, gate_ready, out_done, max_done = (
            ph.sem(n) for n in ("up_ready", "sig_ready", "sq_done", "prod_done", "gate_ready", "out_done", "max_done"))
        row_max, all_max, settled, wd_ready = ph.sem("row_max"), ph.sem("all_max"), ph.sem("settled"), ph.sem("wd_ready")
        spacer = ph.sem("spacer")
        N = NCH * SUB
        with nc.Block() as block:
            def place(n):
                return gate[:, bass.ds(n * SC, SC)]

            @block.sync
            def _(sp):
                sp.sem_inc(up_ready, 2)
                with sp.Fori(0, NCH) as it:
                    for s in range(SUB):
                        sp.wait_ge(up_ready, SUB * it + s + 1)
                        sp.dma_start(raw[:, s % 2, :], part(raw_up, it, s)).then_inc(raw_ready[s % 2], 16)

            @block.scalar
            def _(act):
                act.sem_inc(sq_done, 2)
                act.sem_inc(out_done, 2)
                act.sem_inc(max_done, 1)

                def sigmoid(n, s):
                    wait_alone(act, sq_done, n + 1, spacer)
                    act.activation(sig[:, s, :], place(n), ACT.Sigmoid, scale=scal[:, S_G:S_G + 1]).then_inc(sig_ready, 1)

                def products(n, s, half):
                    act.wait_ge(raw_ready[s], 16 * half + 16)
                    act.wait_ge(out_done, n + 1)
                    act.activation(up[:, s, :], raw[:, s, :], ACT.Copy, scale=scal[:, I_U:I_U + 1]).then_inc(up_ready, 1)
                    wait_alone(act, prod_done, n + 1, spacer)
                    act.activation(place(n), prod[:, s, :], ACT.Copy, scale=scal[:, I_A:I_A + 1]).then_inc(gate_ready, 1)

                sigmoid(0, 0)
                with act.Fori(0, N // 2 - 1) as it:
                    for s in range(2):
                        sigmoid(2 * it + s + 1, 1 - s)
                        products(2 * it + s, s, it)
                sigmoid(N - 1, 1)
                products(N - 2, 0, N // 2 - 1)
                products(N - 1, 1, N // 2 - 1)

            @block.vector
            def _(dve):
                def sigmoids(n, s):
                    dve.wait_ge(sig_ready, n + 1)
                    if not (isinstance(n, int) and n == 0):
                        dve.wait_ge(prod_done, n)
                    dve.tensor_scalar(sq[:], sig[:, s, :], SIGQ, SIGQ - 1, ALU.mult, ALU.min).then_inc(sq_done, 1)

                def products(n, s):
                    dve.wait_ge(sq_done, n + 3)
                    if not (isinstance(n, int) and n < 2):
                        dve.wait_ge(gate_ready, n - 1)
                    dve.tensor_tensor(prod[:, s, :], place(n), sq[:], ALU.mult).then_inc(prod_done, 1)

                def outputs(n, s):
                    dve.wait_ge(gate_ready, n + 1)
                    dve.wait_ge(up_ready, n + 3)
                    dve.wait_ge(max_done, n + 1)
                    dve.tensor_tensor(outp[:], place(n), up[:, s, :], ALU.mult).then_inc(out_done, 1)

                def largest(n):
                    dve.wait_ge(out_done, n + 3)
                    dve.tensor_reduce(mx[:, bass.ds(n, 1)], outp[:], AX_X, ALU.max, apply_absolute_value=True).then_inc(max_done, 1)

                for s in range(2):
                    sigmoids(s, s)
                    products(s, s)
                with dve.Fori(0, N // 2 - 1) as it:
                    for s in range(2):
                        n = 2 * it + s
                        outputs(n, s)
                        sigmoids(n + 2, s)
                        largest(n)
                        products(n + 2, s)
                for s in range(2):
                    outputs(N - 2 + s, s)
                    largest(N - 2 + s)
                dve.wait_ge(max_done, N + 1)
                dve.tensor_reduce(mx_row[:], mx[:], AX_X, ALU.max).then_inc(row_max, 1)
                dve.wait_ge(all_max, 1)
                c = Count(dve, settled)
                c.done(dve.tensor_tensor(scal[:, S_AU:S_AU + 1], scal[:, S_A:S_A + 1], scal[:, S_U:S_U + 1], ALU.mult))
                c.wait()
                scale_of(dve, c, scal, big[:, 0:1], S_O, I_O, S_AU, 1.0)

            @block.gpsimd
            def _(pool):
                tiles = 2 * KF // NCH
                with pool.Fori(0, NCH) as it:
                    pool.wait_ge(up_ready, SUB * it + 3)
                    pool.dma_start(wd[:].rearrange("p a k n -> p (a k) n")[:, bass.ds(it * tiles, tiles), :],
                                   wd_parts.rearrange("p a k n -> p (a k) n")[:, bass.ds(it * tiles, tiles), :]).then_inc(wd_ready, 16)
                pool.wait_ge(wd_ready, 16 * NCH)
                pool.wait_ge(row_max, 1)
                pool.partition_all_reduce(big[:, 0:1], mx_row[:], P, RMAX).then_inc(all_max, 1)


def down(nc, x1, x2, raw_up, gate, wd, scal):
    NO = 3
    with Phase(nc, "dn") as ph:
        raw = ph.sb("raw", [P, 2, SC])
        up = ph.sb("up", [P, SC], I16)
        prod = ph.sb("prod", [P, SC])
        oq = ph.sb("oq", [P, SC], I16)
        om = ph.sb("om", [P, NO, 2, MS, CT], F32R)
        y = ph.sb("y", [P, 2, NT, D])
        py = [[ph.ps(f"py{i}_{t}", [P, D]) for t in range(NT)] for i in range(2)]
        raw_ready = [ph.sem(f"raw_ready{i}") for i in range(2)]
        up_ready, out_done, oq_ready, om_hi, om_lo, om_used = (ph.sem(n) for n in ("up_ready", "out_done", "oq_ready", "om_hi", "om_lo", "om_used"))
        y_full, y_done = ph.sem("y_full"), ph.sem("y_done")
        res_ready = [ph.sem(f"res_ready{i}") for i in range(2)]
        stored, y_free = ph.sem("stored"), ph.sem("y_free")
        with nc.Block() as block:
            @block.sync
            def _(sp):
                sp.sem_inc(up_ready, 2)
                sp.sem_inc(y_free, 2)
                with sp.Fori(0, NCH // 2) as it:
                    for par in range(2):
                        sp.wait_ge(y_free, 2 * it + par + 1)
                        sp.dma_start(y[:, par], tokens(x1, 2 * it + par)).then_inc(res_ready[par], 16)
                        for s in range(SUB):
                            sp.wait_ge(up_ready, 2 * SUB * it + SUB * par + s + 1)
                            sp.dma_start(raw[:, s % 2, :], part(raw_up, 2 * it + par, s)).then_inc(raw_ready[s % 2], 16)

            @block.gpsimd
            def _(pool):
                with pool.Fori(0, NCH // 2) as it:
                    for par in range(2):
                        pool.wait_ge(y_done, NT * (2 * it + par) + 2 * NT + NT)
                        pool.dma_start(tokens(x2, 2 * it + par), y[:, par]).then_inc(stored, 16)
                        pool.wait_ge(stored, 16 * (2 * it + par) + 16)
                        pool.sem_inc(y_free, 1)

            @block.scalar
            def _(act):
                act.sem_inc(out_done, 1)
                act.sem_inc(om_used, 2)
                act.sem_inc(y_full, NT)
                act.sem_inc(oq_ready, 1)
                with act.Fori(0, NCH) as it:
                    for s in range(SUB):
                        n = SUB * it + s
                        act.wait_ge(raw_ready[s % 2], 16 * (SUB // 2) * it + 16 * (s // 2) + 16)
                        act.wait_ge(out_done, n + 1)
                        act.activation(up[:], raw[:, s % 2, :], ACT.Copy, scale=scal[:, I_U:I_U + 1]).then_inc(up_ready, 1)
                        act.wait_ge(out_done, n + 2)
                        act.wait_ge(om_lo, n + 1)
                        act.activation(oq[:], prod[:], ACT.Copy, scale=scal[:, I_O:I_O + 1]).then_inc(oq_ready, 1)
                        act.wait_ge(oq_ready, n + 2)
                        if s == SUB - 1 - NO:
                            act.wait_ge(y_full, NT * it + NT)
                        else:
                            act.wait_ge(om_used, (SUB - 1) * it + s + (1 if s < NO else 0))
                        act.activation(om[:, s % NO, 0].rearrange("p m n -> p (m n)"), oq[:], ACT.Copy).then_inc(om_hi, 1)

            @block.vector
            def _(dve):
                dve.sem_inc(om_lo, 1)
                dve.sem_inc(y_done, 2 * NT)

                def outputs(c, s):
                    n = SUB * c + s
                    dve.wait_ge(up_ready, n + 3)
                    dve.wait_ge(oq_ready, n + 1)
                    dve.tensor_tensor(prod[:], gate[:, bass.ds(c * (KF * CT) + s * SC, SC)], up[:], ALU.mult).then_inc(out_done, 1)
                    dve.wait_ge(om_hi, n + 1)
                    dve.tensor_tensor(om[:, s % NO, 1].rearrange("p m n -> p (m n)"), oq[:],
                                      om[:, s % NO, 0].rearrange("p m n -> p (m n)").bitcast(F32), ALU.subtract).then_inc(om_lo, 1)

                def ends(c, par, half):
                    dve.wait_ge(res_ready[par], 16 * half + 16)
                    for t in range(NT):
                        dve.wait_ge(y_full, NT * c + NT + t + 1)
                        dve.scalar_tensor_tensor(y[:, par, t, :], py[par][t][:], scal[:, S_O:S_O + 1], y[:, par, t, :], ALU.mult, ALU.add
                                                 ).then_inc(y_done, 1)

                for s in range(SUB):
                    outputs(0, s)
                with dve.Fori(0, NCH // 2 - 1) as it:
                    for par in range(2):
                        for s in range(SUB):
                            if s == 3:
                                ends(2 * it + par, par, it)
                            outputs(2 * it + par + 1, s)
                for s in range(SUB):
                    if s == 3:
                        ends(NCH - 2, 0, NCH // 2 - 1)
                    outputs(NCH - 1, s)
                ends(NCH - 1, 1, NCH // 2 - 1)

            @block.tensor
            def _(pe):
                with pe.Fori(0, NCH // 2) as it:
                    for par in range(2):
                        c = 2 * it + par
                        for s in range(SUB):
                            pe.wait_ge(om_lo, SUB * c + s + 2)
                            for t in range(NT):
                                if s == 0:
                                    pe.wait_ge(y_done, NT * c + t + 1)
                                cols = slice(t * P, (t + 1) * P)
                                for m in range(MS):
                                    ins = product(pe, py[par][t][:], (om[:, s % NO, 0, m, cols], om[:, s % NO, 1, m, cols]),
                                                  (wd[:, 0, s * MS + m, :], wd[:, 1, s * MS + m, :]),
                                                  s == 0 and m == 0, s == SUB - 1 and m == MS - 1)
                                if s == SUB - 1:
                                    ins.then_inc(y_full, 1)
                            if s < SUB - 1:
                                ins.then_inc(om_used, 1)


def masked_attention(nc, a, x2, ctx_in, x3, ident, neghalf):
    SCALE = D ** -0.5
    NK = S // P
    with Phase(nc, "ma") as ph:
        gram = ph.sb("gram", [P, 2, KD, D], F32R)
        gcol = ph.sb("gcol", [P, KD])
        grow = ph.sb("grow", [P, D])
        bb = ph.sb("bb", [P, 1])
        fold_projections(nc, a, gram, gcol, grow, bb, ident, SCALE)
        mask = ph.sb("mask", [P, NK, S])
        xin = ph.sb("xin", [P, NT, D])
        cin = ph.sb("cin", [P, 2, NT, D])
        y = ph.sb("y", [P, 2, NT, D])
        junk = ph.sb("junk", [P, D])
        rowc = ph.sb("rowc", [P, 2, NT])
        st = ph.sb("st", [P, NT, 6])
        mv = ph.sb("mv", [P, NT, 2])
        var = ph.sb("var", [P, NT])
        rstd = ph.sb("rstd", [P, NT])
        xT = ph.sb("xT", [P, 2, KD, CT], F32R)
        cT = ph.sb("cT", [P, 2, 2, KD, CT], F32R)
        rT = ph.sb("rT", [P, 2, 2, KD, CT], F32R)
        val = ph.sb("val", [P, 2, 2, NT, D], F32R)
        pT = ph.sb("pT", [P, 2, 2, S], F32R)
        logit = ph.sb("logit", [P, 2, S])
        prob = ph.sb("prob", [P, 2, S])
        nm = ph.sb("nm", [P, 2])
        sums = ph.sb("sums", [P, NT])
        rec = ph.sb("rec", [P, NT])
        pj = [ph.ps(f"pj{i}", [P, CT]) for i in range(2)]
        sc = [ph.ps(f"sc{i}", [P, 512]) for i in range(2)]
        tp = [ph.ps(f"tp{i}", [P, 512]) for i in range(2)]
        po = [ph.ps(f"po{i}", [P, D]) for i in range(2)]
        loaded, x_ready, stored = ph.sem("loaded"), ph.sem("x_ready"), ph.sem("stored")
        c_ready = [ph.sem(f"c_ready{i}") for i in range(2)]
        res_ready = [ph.sem(f"res_ready{i}") for i in range(2)]
        steps_done, mv_ready, rstd_ready, var_done, xn_ready, rowc_ready = (
            ph.sem(n) for n in ("steps", "mv_ready", "rstd_ready", "var_done", "xn_ready", "rowc_ready"))
        spacer_d, spacer_p = ph.sem("spacer_d"), ph.sem("spacer_p")
        job_full, job_hi = ph.sem("job_full"), ph.sem("job_hi")
        job_done = [ph.sem(f"job_done{i}") for i in range(2)]
        val_hi, val_lo = ph.sem("val_hi"), ph.sem("val_lo")
        s_full, logit_done, max_done, exp_done, rec_done, t_full, pt_hi, pt_done, o_full, y_done = (
            ph.sem(n) for n in ("s_full", "logit_done", "max_done", "exp_done", "rec_done", "t_full", "pt_hi", "pt_done", "o_full", "y_done"))
        block = ph.block()

        STEPS = [([("c", 0), ("c", 1)], [("c", 2), ("c", 3)]),
                 ([("x", 0), ("x", 1)], [("x", 2), ("x", 3)]),
                 ([("r", 0)], [("r", 1)]),
                 ([("r", 2)], [("r", 3)])]
        ORDER = [job for step in STEPS for place in step for job in place]
        JOBS = len(ORDER)

        def chunks(eng, body):
            body(0, 0, False)
            with eng.Fori(0, (NCH - 2) // 2) as i:
                body(2 * i + 1, 1, False)
                body(2 * i + 2, 0, False)
            body(NCH - 1, 1, True)

        def prologue_and_chunks(eng, jobs, steps, unit, tail):
            for t in range(NT):
                steps(0, 0, t)
                for place in STEPS[t]:
                    jobs(0, 0, place)

            def body(c, par, last):
                for t in range(NT):
                    unit(c, par, t, 0)
                    if not last:
                        steps(c + 1, 1 - par, t)
                        jobs(c + 1, 1 - par, STEPS[t][0])
                    unit(c, par, t, 1)
                    if not last:
                        jobs(c + 1, 1 - par, STEPS[t][1])
            chunks(eng, body)
            tail()

        def before(c, t, lag):
            return not (isinstance(c, int) and c == 0 and t < lag)

        @block.sync
        def _(sp):
            sp.dma_start(mask[:], a["fside_1xSxS2_0"].rearrange("o (m p) s -> p (o m) s", p=P)).then_inc(loaded, 16)
            sp.dma_start(xin[:], tokens(x2, 0)).then_inc(x_ready, 16)
            sp.dma_start(cin[:, 0], tokens(ctx_in, 0)).then_inc(c_ready[0], 16)
            sp.sem_inc(stored, 16)

            def body(c, par, last):
                if not last:
                    sp.wait_ge(rowc_ready, NT * c + NT)
                    for g in (ORDER.index(("x", NT - 2)), ORDER.index(("x", NT - 1))):
                        sp.wait_ge(job_done[g % 2], (JOBS // 2) * c + g // 2 + 2)
                    sp.dma_start(xin[:], tokens(x2, c + 1)).then_inc(x_ready, 16)
                    if not (isinstance(c, int) and c == 0):
                        sp.wait_ge(val_lo, 2 * c)
                    sp.dma_start(cin[:, 1 - par], tokens(ctx_in, c + 1)).then_inc(c_ready[1 - par], 16)
                sp.wait_ge(stored, 16 * (c - 1) + 16 if not (isinstance(c, int) and c == 0) else 16)
                sp.dma_start(y[:, par], tokens(x2, c)).then_inc(res_ready[par], 16)
                if not (isinstance(c, int) and c == 0):
                    sp.wait_ge(y_done, NT * c + 2)
                    sp.dma_start(tokens(x3, c - 1), y[:, 1 - par]).then_inc(stored, 16)
            chunks(sp, body)
            sp.wait_ge(y_done, NT * NCH + 2)
            sp.dma_start(tokens(x3, NCH - 1), y[:, 1]).then_inc(stored, 16)
            sp.wait_ge(stored, 16 * NCH + 16)

        @block.gpsimd
        def _(pool):
            with pool.Fori(0, NCH) as n:
                norm_rstd(pool, mv, var, rstd, neghalf, mv_ready, rstd_ready, var_done, n, spacer_p)

        @block.vector
        def _(dve):
            dve.wait_ge(loaded, 16)

            def steps(c, par, t):
                if t == 0:
                    dve.wait_ge(x_ready, 16 * c + 16)
                    norm_stats(dve, st, mv, Count(dve, steps_done, NT * c), mv_ready, spacer_d, xin)
                if t == 1:
                    dve.wait_ge(rstd_ready, c + 1)
                    for u in range(NT):
                        dve.tensor_scalar(xin[:, u, :], xin[:, u, :], mv[:, u, 0:1], rstd[:, u:u + 1], ALU.subtract, ALU.mult).then_inc(xn_ready, 1)
                if t == 2:
                    dve.wait_ge(xn_ready, NT * c + NT)
                    for u in range(NT):
                        dve.tensor_tensor_reduce(junk[:], xin[:, u, :], grow[:], SCALE, bb[:, 0:1], ALU.mult, ALU.add, rowc[:, par, u:u + 1]
                                                 ).then_inc(rowc_ready, 1)
                        dve.wait_ge(rowc_ready, NT * c + u + 1)
                if t > 1:
                    tiles = slice(2 * (t - 2), 2 * (t - 2) + 2)
                    dve.wait_ge(val_hi, 2 * c + t - 1)
                    dve.tensor_tensor(val[:, par, 1, tiles, :], cin[:, par, tiles, :], val[:, par, 0, tiles, :].bitcast(F32), ALU.subtract).then_inc(val_lo, 1)

            def jobs(c, par, place):
                for job in place:
                    kind, i = job
                    g = ORDER.index(job)
                    bank = pj[g % 2][:]
                    dve.wait_ge(job_hi, JOBS * c + g + 1)
                    if kind == "r":
                        ins = dve.scalar_tensor_tensor(rT[:, par, 1, i, :], bank, gcol[:, i:i + 1], rT[:, par, 0, i, :].bitcast(F32), ALU.add, ALU.subtract)
                    else:
                        to = (xT if kind == "x" else cT[:, par])[:, :, :, i * P:(i + 1) * P]
                        ins = dve.tensor_tensor(to[:, 1], bank.rearrange("p (k n) -> p k n", k=KD), to[:, 0].bitcast(F32), ALU.subtract)
                    ins.then_inc(job_done[g % 2], 1)

            def turned_low(n, i):
                dve.wait_ge(pt_hi, n + 1)
                dve.tensor_tensor(pT[:, i, 1], tp[i][:, 0:S], pT[:, i, 0].bitcast(F32), ALU.subtract).then_inc(pt_done, 1)

            def reciprocal(n, t):
                dve.wait_ge(exp_done, n + 3)
                dve.reciprocal(rec[:, t:t + 1], sums[:, t:t + 1]).then_inc(rec_done, 1)

            def output(n, par, t, half):
                if t == 0:
                    dve.wait_ge(res_ready[par], half + 16)
                dve.wait_ge(o_full, n + 3)
                dve.wait_ge(rec_done, n + 1)
                dve.scalar_tensor_tensor(y[:, par, t, :], po[t % 2][:], rec[:, t:t + 1], y[:, par, t, :], ALU.mult, ALU.add).then_inc(y_done, 1)

            def unit(c, par, t, place):
                n, i = NT * c + t, t % 2
                if place == 0:
                    dve.wait_ge(s_full, n + 1)
                    dve.wait_ge(exp_done, n + 1)
                    dve.scalar_tensor_tensor(logit[:, i, :], sc[i][:, 0:S], rowc[:, par, t:t + 1], mask[:, t % NK, :], ALU.add, ALU.add).then_inc(logit_done, 1)
                    dve.wait_ge(logit_done, n + 3)
                    dve.tensor_reduce(nm[:, i:i + 1], logit[:, i, :], AX_X, ALU.max, negate=True).then_inc(max_done, 1)
                    return
                if before(c, t, 1):
                    reciprocal(n - 1, (t - 1) % NT)
                    turned_low(n - 1, 1 - i)
                if before(c, t, 2):
                    par_u = par if t > 1 else 1 - par
                    c_u = c if t > 1 else c - 1
                    output(n - 2, par_u, (t - 2) % NT, 8 * (c_u - par_u))

            def tail():
                n = NT * NCH
                reciprocal(n - 1, NT - 1)
                turned_low(n - 1, 1)
                output(n - 2, 1, NT - 2, 0)
                output(n - 1, 1, NT - 1, 0)
            prologue_and_chunks(dve, jobs, steps, unit, tail)

        @block.scalar
        def _(act):
            def steps(c, par, t):
                if t > 1:
                    tiles = slice(2 * (t - 2), 2 * (t - 2) + 2)
                    act.wait_ge(c_ready[par], 8 * (c - par) + 16)
                    act.activation(val[:, par, 0, tiles, :], cin[:, par, tiles, :], ACT.Copy).then_inc(val_hi, 1)

            def jobs(c, par, place):
                for job in place:
                    kind, i = job
                    g = ORDER.index(job)
                    bank = pj[g % 2][:]
                    act.wait_ge(job_full, JOBS * c + g + 1)
                    if kind == "r":
                        ins = act.activation(rT[:, par, 0, i, :], bank, ACT.Identity, bias=gcol[:, i:i + 1])
                    else:
                        to = (xT if kind == "x" else cT[:, par])[:, 0, :, i * P:(i + 1) * P]
                        ins = act.activation(to, bank.rearrange("p (k n) -> p k n", k=KD), ACT.Copy)
                    ins.then_inc(job_hi, 1)

            def turned_high(n, i):
                act.wait_ge(t_full, n + 3)
                act.wait_ge(o_full, n + 1)
                act.activation(pT[:, i, 0], tp[i][:, 0:S], ACT.Copy).then_inc(pt_hi, 1)

            def unit(c, par, t, place):
                n, i = NT * c + t, t % 2
                if place == 0:
                    act.wait_ge(max_done, n + 1)
                    act.wait_ge(t_full, n + 1)
                    act.activation(prob[:, i, :], logit[:, i, :], ACT.Exp, bias=nm[:, i:i + 1], accum_out=sums[:, t:t + 1]).then_inc(exp_done, 1)
                elif before(c, t, 1):
                    turned_high(n - 1, 1 - i)
            prologue_and_chunks(act, jobs, steps, unit, lambda: turned_high(NT * NCH - 1, 1))

        @block.tensor
        def _(pe):
            for s in job_done:
                pe.sem_inc(s, 1)
            for s in (exp_done, logit_done, pt_done, y_done, t_full, o_full):
                pe.sem_inc(s, 2)

            def jobs(c, par, place):
                for job in place:
                    kind, i = job
                    g = ORDER.index(job)
                    bank = pj[g % 2]
                    pe.wait_ge(job_done[g % 2], (JOBS // 2) * c + g // 2 + 1)
                    if kind == "x":
                        pe.wait_ge(xn_ready, NT * c + i + 1)
                    if kind == "c":
                        pe.wait_ge(c_ready[par], 8 * (c - par) + 16)
                    if kind == "r":
                        if i == 0:
                            pe.wait_ge(job_done[1 - g % 2], (JOBS // 2) * c + (g - 1) // 2 + 2)
                        cols = slice(i * P, (i + 1) * P)
                        for k in range(KD):
                            ins = product(pe, bank[:], (gram[:, 0, k, cols], gram[:, 1, k, cols]), (xT[:, 0, k, :], xT[:, 1, k, :]), k == 0, k == KD - 1)
                    else:
                        src = xin if kind == "x" else cin[:, par]
                        for k in range(KD):
                            ins = pe.transpose(bank[:, k * P:(k + 1) * P], src[:, i, k * P:(k + 1) * P], ident[:])
                    ins.then_inc(job_full, 1)

            def turn(n, i):
                pe.wait_ge(exp_done, n + 3)
                pe.wait_ge(pt_done, n + 1)
                for k in range(NK):
                    ins = pe.transpose(tp[i][:, k * P:(k + 1) * P], prob[:, i, k * P:(k + 1) * P], ident[:])
                ins.then_inc(t_full, 1)

            def values(n, par, t):
                i = t % 2
                pe.wait_ge(pt_done, n + 3)
                pe.wait_ge(y_done, n + 1)
                for k in range(NK):
                    cols, tile = slice(k * P, (k + 1) * P), (t // NK) * NK + k
                    ins = product(pe, po[i][:], (pT[:, i, 0, cols], pT[:, i, 1, cols]), (val[:, par, 0, tile, :], val[:, par, 1, tile, :]), k == 0, k == NK - 1)
                ins.then_inc(o_full, 1)

            def unit(c, par, t, place):
                n, i, b = NT * c + t, t % 2, t // NK
                if place == (0 if t == 0 else 1):
                    if before(c, t, 1):
                        turn(n - 1, 1 - i)
                    if before(c, t, 2):
                        values(n - 2, par if t > 1 else 1 - par, (t - 2) % NT)
                if place == 0:
                    if t == 0:
                        for s in job_done:
                            pe.wait_ge(s, (JOBS // 2) * c + JOBS // 2 + 1)
                        pe.wait_ge(val_lo, 2 * c + 2)
                    pe.wait_ge(logit_done, n + 1)
                    rows, keys = slice(t * P, (t + 1) * P), slice(b * S, (b + 1) * S)
                    for k in range(KD):
                        ins = product(pe, sc[i][:, 0:S], (rT[:, par, 0, k, rows], rT[:, par, 1, k, rows]), (cT[:, par, 0, k, keys], cT[:, par, 1, k, keys]),
                                      k == 0, k == KD - 1)
                    ins.then_inc(s_full, 1)

            def tail():
                n = NT * NCH
                values(n - 2, 1, NT - 2)
                turn(n - 1, 1)
                values(n - 1, 1, NT - 1)
            prologue_and_chunks(pe, jobs, lambda c, par, t: None, unit, tail)


def fold_projections(nc, a, gram, gcol, grow, bb, ident, scale):
    with Phase(nc, "fp") as ph:
        w1 = ph.sb("w1", [P, KD, D])
        w2 = ph.sb("w2", [P, KD, D])
        w2T = ph.sb("w2T", [P, KD, D])
        b12 = ph.sb("b12", [P, 2, KD])
        m = ph.sb("m", [P, KD, D])
        beta = ph.sb("beta", [P, KD])
        ones = ph.sb("ones", [P, P])
        betas = ph.sb("betas", [P, KD, P])
        pw = [ph.ps(f"pw{i}", [P, D]) for i in range(4)]
        pc = [ph.ps(f"pc{i}", [P, D]) for i in range(4)]
        loaded, turned, turned_out, m_full, m_out, beta_full, beta_out, betas_out, done = (
            ph.sem(n) for n in ("loaded", "turned", "turned_out", "m_full", "m_out", "beta_full", "beta_out", "betas_out", "done"))
        g_full, g_out = ph.sem("g_full"), ph.sem("g_out")
        ones_made = ph.sem("ones_made")
        with nc.Block() as block:
            @block.sync
            def _(sp):
                sp.dma_start(w1[:], a["L1_xattn_W1"].rearrange("(k p) n -> p k n", p=P)).then_inc(loaded, 16)
                sp.dma_start(w2[:], a["L1_xattn_W2"].rearrange("(k p) n -> p k n", p=P)).then_inc(loaded, 16)
                sp.dma_start(b12[:, 0, :], a["L1_xattn_b1"].rearrange("(k p) -> p k", p=P), allow_slow_non_contiguous=True).then_inc(loaded, 16)
                sp.dma_start(b12[:, 1, :], a["L1_xattn_b2"].rearrange("(k p) -> p k", p=P), allow_slow_non_contiguous=True).then_inc(loaded, 16)

            @block.gpsimd
            def _(pool):
                pool.memset(ones[:], 1.0).then_inc(ones_made, 1)

            @block.tensor
            def _(pe):
                pe.wait_ge(loaded, 64)
                for k in range(KD):
                    for t in range(KD):
                        ins = pe.transpose(pw[k][:, t * P:(t + 1) * P], w2[:, t, k * P:(k + 1) * P], ident[:])
                    ins.then_inc(turned, 1)
                pe.wait_ge(turned_out, KD)
                for o in range(KD):
                    for k in range(KD):
                        ins = pe.matmul(pw[o][:], w2T[:, k, o * P:(o + 1) * P], w1[:, k, :], start=k == 0, stop=k == KD - 1)
                    ins.then_inc(m_full, 1)
                for o in range(KD):
                    for k in range(KD):
                        ins = pe.matmul(pc[0][:, o:o + 1], w2T[:, k, o * P:(o + 1) * P], b12[:, 0, k:k + 1], start=k == 0, stop=k == KD - 1)
                ins.then_inc(beta_full, 1)
                pe.wait_ge(m_out, KD)
                for d in range(KD):
                    for o in range(KD):
                        ins = pe.matmul(pw[d][:], m[:, o, d * P:(d + 1) * P], m[:, o, :], start=o == 0, stop=o == KD - 1)
                    ins.then_inc(g_full, 1)
                pe.wait_ge(betas_out, KD)
                for d in range(KD):
                    for o in range(KD):
                        ins = pe.matmul(pc[1][:, d:d + 1], m[:, o, d * P:(d + 1) * P], beta[:, o:o + 1], start=o == 0, stop=o == KD - 1)
                for o in range(KD):
                    ins = pe.matmul(pc[2][:], betas[:, o, :], m[:, o, :], start=o == 0, stop=o == KD - 1)
                for o in range(KD):
                    ins = pe.matmul(pc[3][:, 0:1], betas[:, o, :], beta[:, o:o + 1], start=o == 0, stop=o == KD - 1)
                ins.then_inc(g_full, 1)

            @block.scalar
            def _(act):
                for k in range(KD):
                    act.wait_ge(turned, k + 1)
                    act.activation(w2T[:, k, :], pw[k][:], ACT.Copy).then_inc(turned_out, 1)
                for o in range(KD):
                    act.wait_ge(m_full, o + 1)
                    act.activation(m[:, o, :], pw[o][:], ACT.Copy).then_inc(m_out, 1)
                for d in range(KD):
                    act.wait_ge(g_full, d + 1)
                    act.activation(gram[:, 0, d, :], pw[d][:], ACT.Copy, scale=scale).then_inc(g_out, 1)

            @block.vector
            def _(dve):
                dve.wait_ge(beta_full, 1)
                dve.tensor_tensor(beta[:], pc[0][:, 0:KD], b12[:, 1, :], ALU.add).then_inc(beta_out, 1)
                dve.wait_ge(beta_out, 1)
                dve.wait_ge(ones_made, 1)
                for o in range(KD):
                    dve.tensor_scalar(betas[:, o, :], ones[:], beta[:, o:o + 1], None, ALU.mult).then_inc(betas_out, 1)
                for d in range(KD):
                    dve.wait_ge(g_out, d + 1)
                    dve.scalar_tensor_tensor(gram[:, 1, d, :], pw[d][:], scale, gram[:, 0, d, :].bitcast(F32), ALU.mult, ALU.subtract).then_inc(done, 1)
                dve.wait_ge(g_full, KD + 1)
                dve.tensor_scalar(gcol[:], pc[1][:, 0:KD], scale, None, ALU.mult).then_inc(done, 1)
                dve.tensor_copy(grow[:], pc[2][:]).then_inc(done, 1)
                dve.tensor_scalar(bb[:], pc[3][:, 0:1], scale, None, ALU.mult).then_inc(done, 1)
                dve.wait_ge(done, 3 + KD)


def lora_ffn(nc, a, x3, out, ident, neghalf):
    SCALING = 1.0 / R
    ZC = 2 * LZ + 2 * (LZ % 2)
    ROWH, ROWL = 0, 32
    LAG = 2
    HEAD = NT + 3
    TAIL = 2
    with Phase(nc, "lf") as ph:
        w1 = ph.sb("w1", [P, 2, KD, H2], F32R)
        w2 = ph.sb("w2", [P, 2, KH, D], F32R)
        ra1 = ph.sb("ra1", [P, KD * ZC + P], F32R)
        ra2 = ph.sb("ra2", [P, KH * ZC + P], F32R)
        lb1 = ph.sb("lb1", [P, H2], F32R)
        lb2 = ph.sb("lb2", [P, D], F32R)
        lora_weights(nc, a, w1, w2, ra1, ra2, lb1, lb2, ZC)
        xin = ph.sb("xin", [P, 2, D])
        y = ph.sb("y", [P, NT, D])
        st = ph.sb("st", [P, 2, 6])
        mv = ph.sb("mv", [P, 2, 2])
        var = ph.sb("var", [P, 2])
        rstd = ph.sb("rstd", [P, 2])
        xT = ph.sb("xT", [P, 2, 2, KD, CT], F32R)
        hT = ph.sb("hT", [P, 2, 2, CT], F32R)
        zT = ph.sb("zT", [P, CT])
        z2 = ph.sb("z2", [P, NT, ZC])
        z = ph.sb("z", [P, NT, LZ])
        zmax = ph.sb("zmax", [P, NT])
        zsum = ph.sb("zsum", [P, NT])
        zrec = ph.sb("zrec", [P, NT])
        gl = ph.sb("gl", [P, NT, E])
        ge = ph.sb("ge", [P, NT, E])
        zg = ph.sb("zg", [P, NT, P])
        zf = ph.sb("zf", [P, NT, ER])
        mixT = ph.sb("mixT", [P, 2, CT], F32R)
        pj = ph.ps("pj", [P, CT])
        pz = ph.ps("pz", [P, CT])
        hb = [ph.ps(f"hb{i}", [P, CT]) for i in range(2)]
        py = [ph.ps(f"py{i}", [P, D]) for i in range(NT)]
        x_ready = [ph.sem(f"x_ready{i}") for i in range(2)]
        res_ready, stored, cleared = ph.sem("res_ready"), ph.sem("stored"), ph.sem("cleared")
        stat_done, mv_ready, var_done, rstd_ready, xn_ready = (ph.sem(n) for n in ("stat_done", "mv_ready", "var_done", "rstd_ready", "xn_ready"))
        spacer_d, spacer_p = ph.sem("spacer_d"), ph.sem("spacer_p")
        pj_full, pj_hi, pj_done = ph.sem("pj_full"), ph.sem("pj_hi"), ph.sem("pj_done")
        h_full, h_hi, h_done, h_used = ph.sem("h_full"), ph.sem("h_hi"), ph.sem("h_done"), ph.sem("h_used")
        z_full, z_done = ph.sem("z_full"), ph.sem("z_done")
        y_full, y_done = ph.sem("y_full"), ph.sem("y_done")
        mix_steps, gl_ready, ge_ready, zg_ready = ([ph.sem(f"{n}{i}") for i in range(2)] for n in ("mix_steps", "gl_ready", "ge_ready", "zg_ready"))
        MIX = 9
        block = ph.block()

        def head_base(c):
            return 0 if isinstance(c, int) and c == 0 else (HEAD + TAIL) * c - TAIL

        def tail_base(c):
            return (HEAD + TAIL) * c + (HEAD if isinstance(c, int) and c == NCH - 1 else 2 * HEAD)

        def chunks(eng, body):
            body(0, 0, False, True)
            with eng.Fori(0, (NCH - 2) // 2) as i:
                body(2 * i + 1, 1, True, True)
                body(2 * i + 2, 0, True, True)
            body(NCH - 1, 1, True, False)

        @block.sync
        def _(sp):
            sp.sem_inc(pj_done, 1)
            sp.sem_inc(y_done, NT)

            def head(c, tiles):
                for t in tiles:
                    if t >= 2:
                        sp.wait_ge(pj_done, head_base(c) + t - 2 + 2)
                    elif not (isinstance(c, int) and c == 0):
                        sp.wait_ge(pj_done, head_base(c - 1) + t + 2 + 2)
                    sp.dma_start(xin[:, t % 2, :], x3[bass.ds(c * CT + t * P, P), :]).then_inc(x_ready[t % 2], 16)

            def end(c):
                sp.wait_ge(y_done, NT * c + 2 * NT)
                sp.dma_start(tokens(out, c), y[:]).then_inc(stored, 16)

            head(0, range(NT))

            def body(c, par, tail, nxt):
                if nxt:
                    head(c + 1, range(2))
                if tail:
                    end(c - 1)
                if nxt:
                    head(c + 1, range(2, NT))
                if tail:
                    sp.wait_ge(stored, 16 * c)
                sp.dma_start(y[:], tokens(x3, c)).then_inc(res_ready, 16)
            chunks(sp, body)
            end(NCH - 1)
            sp.wait_ge(stored, 16 * NCH)

        @block.gpsimd
        def _(pool):
            pool.memset(zg[:], 0.0).then_inc(cleared, 1)
            pool.wait_ge(cleared, 1)
            pool.memset(zg[:, :, ROWH + ER:ROWH + ER + 1], 1.0).then_inc(cleared, 1)
            pool.memset(zg[:, :, ROWL + ER:ROWL + ER + 1], 1.0).then_inc(cleared, 1)
            with pool.Fori(0, NCH) as c:
                for t in range(NT):
                    wait_alone(pool, mv_ready, NT * c + t + 1, spacer_p)
                    pool.tensor_scalar(var[:, t % 2:t % 2 + 1], mv[:, t % 2, 1:2], EPS, None, ALU.add).then_inc(var_done, 1)
                    pool.wait_ge(var_done, NT * c + t + 1)
                    pool.tensor_tensor(rstd[:, t % 2:t % 2 + 1], var[:, t % 2:t % 2 + 1], neghalf[:, 0:1], ALU.pow).then_inc(rstd_ready, 1)

        @block.vector
        def _(dve):
            dve.wait_ge(cleared, 3)

            def stats(c, t):
                i = t % 2
                dve.wait_ge(x_ready[i], 32 * c + 16 * (t // 2) + 16)
                dve.bn_stats(st[:, i, :], xin[:, i, :]).then_inc(stat_done, 1)
                wait_alone(dve, stat_done, NT * c + t + 1, spacer_d)
                dve.bn_aggr(mv[:, i, :], st[:, i, :]).then_inc(mv_ready, 1)

            def rows(c, t):
                i = t % 2
                dve.wait_ge(rstd_ready, NT * c + t + 1)
                dve.tensor_scalar(xin[:, i, :], xin[:, i, :], mv[:, i, 0:1], rstd[:, i:i + 1], ALU.subtract, ALU.mult).then_inc(xn_ready, 1)

            def turned_lo(c, t, par):
                cols = slice(t * P, (t + 1) * P)
                dve.wait_ge(pj_hi, NT * c + t + 1)
                dve.tensor_tensor(xT[:, par, 1, :, cols], pj[:].rearrange("p (k n) -> p k n", k=KD), xT[:, par, 0, :, cols].bitcast(F32),
                                  ALU.subtract).then_inc(pj_done, 1)

            def mixture(c, layer, job):
                s = Count(dve, mix_steps[layer], MIX * c)
                dve.wait_ge(pj_full, job + 1)
                dve.tensor_copy(z2[:], pj[:].rearrange("p (t n) -> p t n", t=NT)[:, :, 0:ZC]).then_inc(pj_done, 1)
                dve.wait_ge(pj_done, job + 2)
                s.done(dve.tensor_tensor(z[:], z2[:, :, 0:LZ], z2[:, :, ZC // 2:ZC // 2 + LZ], ALU.add))
                s.wait()
                s.done(dve.tensor_reduce(zmax[:], z[:, :, 0:E], AX_X, ALU.max))
                s.wait()
                dve.tensor_tensor(gl[:], z[:, :, 0:E], zmax[:].unsqueeze(2).broadcast_to([P, NT, E]), ALU.subtract).then_inc(gl_ready[layer], 1)
                dve.wait_ge(ge_ready[layer], c + 1)
                s.done(dve.tensor_reduce(zsum[:], ge[:], AX_X, ALU.add))
                s.wait()
                s.done(dve.reciprocal(zrec[:], zsum[:]))
                s.wait()
                s.done(dve.scalar_tensor_tensor(gl[:], ge[:], SCALING, zrec[:].unsqueeze(2).broadcast_to([P, NT, E]), ALU.mult, ALU.mult))
                s.wait()
                for e in range(E):
                    ins = dve.tensor_tensor(zf[:, :, e * R:(e + 1) * R], z[:, :, E + e * R:E + (e + 1) * R],
                                            gl[:, :, e:e + 1].broadcast_to([P, NT, R]), ALU.mult)
                s.done(ins)
                s.wait()
                s.done(dve.tensor_copy(zg[:, :, ROWH:ROWH + ER].bitcast(F32R), zf[:]))
                s.wait()
                s.done(dve.tensor_copy(zg[:, :, ROWL:ROWL + ER], zg[:, :, ROWH:ROWH + ER]))
                s.done(dve.tensor_tensor(zg[:, :, 64:64 + ER].bitcast(F32R), zf[:], zg[:, :, ROWH:ROWH + ER], ALU.subtract))
                s.wait()
                dve.sem_inc(zg_ready[layer], 1)
                assert s.n == MIX, s.n

            def hidden_lo(c, m):
                i = m % 2
                dve.wait_ge(h_hi, KH * c + m + 1)
                dve.scalar_tensor_tensor(hT[:, i, 1, :], hb[i][:], 0.0, hT[:, i, 0, :].bitcast(F32), ALU.max, ALU.subtract).then_inc(h_done, 1)

            def end(c):
                dve.wait_ge(res_ready, 16 * c + 16)
                for t in range(NT):
                    dve.wait_ge(y_full, NT * c + t + 1)
                    dve.tensor_tensor(y[:, t, :], py[t][:], y[:, t, :], ALU.add).then_inc(y_done, 1)

            for t in range(NT):
                stats(0, t)
                rows(0, t)
                turned_lo(0, t, 0)
            mixture(0, 0, head_base(0) + NT + 1)

            def body(c, par, tail, nxt):
                for m in range(KH + LAG):
                    if m < KH:
                        hidden_lo(c, m)
                    if tail and m == 0:
                        mixture(c - 1, 1, tail_base(c - 1))
                    if tail and m == 1:
                        end(c - 1)
                    if nxt:
                        if m in (1, 3, 5, 7):
                            stats(c + 1, m // 2)
                        if m in (2, 4, 6, 8):
                            rows(c + 1, m // 2 - 1)
                        if m in (3, 5, 7, 9):
                            turned_lo(c + 1, m // 2 - 1, 1 - par)
                        if m == 11:
                            mixture(c + 1, 0, head_base(c + 1) + NT + 1)
            chunks(dve, body)
            mixture(NCH - 1, 1, tail_base(NCH - 1))
            end(NCH - 1)

        @block.scalar
        def _(act):
            act.sem_inc(h_used, 2)

            def turned_hi(c, t, par):
                act.wait_ge(pj_full, head_base(c) + t + 1)
                act.activation(xT[:, par, 0, :, t * P:(t + 1) * P], pj[:].rearrange("p (k n) -> p k n", k=KD), ACT.Copy).then_inc(pj_hi, 1)

            def projected(job):
                act.wait_ge(pj_full, job + 1)
                act.activation(zT[:], pj[:], ACT.Copy).then_inc(pj_done, 1)

            def exps(c, layer):
                act.wait_ge(gl_ready[layer], c + 1)
                act.activation(ge[:], gl[:], ACT.Exp).then_inc(ge_ready[layer], 1)

            def mixed(job, layer):
                act.wait_ge(pj_full, job + 1)
                act.activation(mixT[:, layer, :], pj[:], ACT.Copy).then_inc(pj_done, 1)

            def hidden_hi(c, m):
                act.wait_ge(h_full, KH * c + m + 1)
                act.wait_ge(h_used, KH * c + m + 1)
                act.activation(hT[:, m % 2, 0, :], hb[m % 2][:], ACT.Relu).then_inc(h_hi, 1)

            def second_projected(c):
                act.wait_ge(z_full, c + 1)
                act.activation(zT[:], pz[:], ACT.Copy).then_inc(z_done, 1)

            for t in range(NT):
                turned_hi(0, t, 0)
            projected(head_base(0) + NT)
            exps(0, 0)
            mixed(head_base(0) + NT + 2, 0)

            def body(c, par, tail, nxt):
                for m in range(KH + LAG):
                    if m < KH:
                        hidden_hi(c, m)
                    if tail and m == 0:
                        exps(c - 1, 1)
                    if tail and m == 1:
                        mixed(tail_base(c - 1) + 1, 1)
                    if nxt:
                        if m in (3, 5, 7, 9):
                            turned_hi(c + 1, m // 2 - 1, 1 - par)
                        if m == 10:
                            projected(head_base(c + 1) + NT)
                        if m == 11:
                            exps(c + 1, 0)
                        if m == KH:
                            mixed(head_base(c + 1) + NT + 2, 0)
                second_projected(c)
            chunks(act, body)
            exps(NCH - 1, 1)
            mixed(tail_base(NCH - 1) + 1, 1)

        @block.tensor
        def _(pe):
            pe.sem_inc(z_done, 1)
            pe.sem_inc(h_done, 2)
            pe.wait_ge(cleared, 3)

            def pj_free(job):
                pe.wait_ge(pj_done, job + 1)

            def pj_taken(job):
                pe.wait_ge(pj_done, job + 2)

            def turn_tile(c, t):
                pe.wait_ge(xn_ready, NT * c + t + 1)
                pj_free(head_base(c) + t)
                for k in range(KD):
                    ins = pe.transpose(pj[:, k * P:(k + 1) * P], xin[:, t % 2, k * P:(k + 1) * P], ident[:])
                ins.then_inc(pj_full, 1)

            def first_projections(c, par):
                job = head_base(c) + NT
                pj_taken(job - 1)
                for k in range(KD):
                    for part in range(2):
                        ins = pe.matmul(pj[:], ra1[:, k * ZC:k * ZC + P], xT[:, par, part, k, :], start=k == 0 and part == 0,
                                        stop=k == KD - 1 and part == 1)
                ins.then_inc(pj_full, 1)

            def turn_projections(job):
                pj_free(job)
                for t in range(NT):
                    ins = pe.transpose(pj[:, t * P:(t + 1) * P], zT[:, t * P:(t + 1) * P], ident[:])
                ins.then_inc(pj_full, 1)

            def turn_mixture(c, layer, job):
                pe.wait_ge(zg_ready[layer], c + 1)
                pj_free(job)
                for t in range(NT):
                    ins = pe.transpose(pj[:, t * P:(t + 1) * P], zg[:, t, :], ident[:])
                ins.then_inc(pj_full, 1)

            def hidden(c, m, par):
                pe.wait_ge(h_done, KH * c + m + 1)
                cols = slice(m * P, (m + 1) * P)
                for k in range(KD):
                    product(pe, hb[m % 2][:], (w1[:, 0, k, cols], w1[:, 1, k, cols]), (xT[:, par, 0, k, :], xT[:, par, 1, k, :]), k == 0, False)
                if m == 0:
                    pj_taken(head_base(c) + NT + 2)
                pe.matmul(hb[m % 2][:], lb1[:, cols], mixT[:, 0, :], start=False, stop=True).then_inc(h_full, 1)

            def use_hidden(c, u):
                i = u % 2
                pe.wait_ge(h_done, KH * c + u + 3)
                if u == 0:
                    pe.wait_ge(z_done, c + 1)
                for part in range(2):
                    ins = pe.matmul(pz[:], ra2[:, u * ZC:u * ZC + P], hT[:, i, part, :], start=u == 0 and part == 0, stop=u == KH - 1 and part == 1)
                if u == KH - 1:
                    ins.then_inc(z_full, 1)
                for t in range(NT):
                    cols = slice(t * P, (t + 1) * P)
                    if u == 0:
                        pe.wait_ge(y_done, NT * c + t + 1)
                    ins = product(pe, py[t][:], (hT[:, i, 0, cols], hT[:, i, 1, cols]), (w2[:, 0, u, :], w2[:, 1, u, :]), u == 0, False)
                ins.then_inc(h_used, 1)

            def second_lora(c):
                pj_taken(tail_base(c) + 1)
                for t in range(NT):
                    pe.matmul(py[t][:], mixT[:, 1, t * P:(t + 1) * P], lb2[:], start=False, stop=True).then_inc(y_full, 1)

            for t in range(NT):
                turn_tile(0, t)
            first_projections(0, 0)
            pj_taken(head_base(0) + NT)
            turn_projections(head_base(0) + NT + 1)
            turn_mixture(0, 0, head_base(0) + NT + 2)

            def body(c, par, tail, nxt):
                for m in range(KH + LAG):
                    if m < KH:
                        if tail and m == 2:
                            turn_mixture(c - 1, 1, tail_base(c - 1) + 1)
                        hidden(c, m, par)
                    if tail and m == 0:
                        pe.wait_ge(z_done, c + 1)
                        turn_projections(tail_base(c - 1))
                    if tail and m == 2:
                        second_lora(c - 1)
                    if nxt:
                        if m in (3, 5, 7, 9):
                            turn_tile(c + 1, m // 2 - 1)
                        if m == 10:
                            first_projections(c + 1, 1 - par)
                        if m == 11:
                            pj_taken(head_base(c + 1) + NT)
                            turn_projections(head_base(c + 1) + NT + 1)
                        if m == KH:
                            turn_mixture(c + 1, 0, head_base(c + 1) + NT + 2)
                    if m >= LAG:
                        use_hidden(c, m - LAG)
            chunks(pe, body)
            pe.wait_ge(z_done, NCH + 1)
            turn_projections(tail_base(NCH - 1))
            turn_mixture(NCH - 1, 1, tail_base(NCH - 1) + 1)
            second_lora(NCH - 1)


def split_pieces(nc, name, pieces, cols, pool_part=None, first=None, scalar_last=None, vector_last=None):
    NB_ = 3
    with Phase(nc, name) as ph:
        raw = ph.sb("raw", [P, NB_, cols])
        raw_ready = [ph.sem(f"raw_ready{i}") for i in range(NB_)]
        hi_done, lo_done = ph.sem("hi_done"), ph.sem("lo_done")
        block = ph.block()

        def place(i, hi):
            n = 1
            for s in hi.shape[1:]:
                n *= s
            r = raw[:, i % NB_, 0:n]
            return r.rearrange("p (k n) -> p k n", k=hi.shape[1]) if len(hi.shape) == 3 else r

        @block.sync
        def _(sp):
            for i, (src, hi, lo) in enumerate(pieces):
                if i >= NB_:
                    sp.wait_ge(lo_done, i - NB_ + 1)
                sp.dma_start(place(i, hi), src).then_inc(raw_ready[i % NB_], 16)

        @block.scalar
        def _(act):
            if first:
                first(act)
            for i, (src, hi, lo) in enumerate(pieces):
                act.wait_ge(raw_ready[i % NB_], 16 * (i // NB_ + 1))
                act.activation(hi, place(i, hi), ACT.Copy).then_inc(hi_done, 1)
            if scalar_last:
                scalar_last(act)

        @block.vector
        def _(dve):
            for i, (src, hi, lo) in enumerate(pieces):
                dve.wait_ge(hi_done, i + 1)
                dve.tensor_tensor(lo, place(i, hi), hi.bitcast(F32), ALU.subtract).then_inc(lo_done, 1)
            dve.wait_ge(lo_done, len(pieces))
            if vector_last:
                vector_last(dve)

        if pool_part:
            block.gpsimd(pool_part)


def lora_weights(nc, a, w1, w2, ra1, ra2, lb1, lb2, ZC):
    W1, W2 = a["L1_ffn_W1"], a["L1_ffn_W2"]
    pieces = [(W1[k * P:(k + 1) * P, :], w1[:, 0, k, :], w1[:, 1, k, :]) for k in range(KD)]
    KP = H2 // D
    for g in range(KH // KP):
        rows = slice(g * KP, (g + 1) * KP)
        pieces.append((W2[g * KP * P:(g + 1) * KP * P, :].rearrange("(k p) n -> p k n", p=P), w2[:, 0, rows, :], w2[:, 1, rows, :]))
    with Phase(nc, "ls") as ph:
        s1 = ph.sb("s1", [P, KD, LZ])
        s2 = ph.sb("s2", [P, KH, LZ])
        t1 = ph.sb("t1", [P, H2])
        t2 = ph.sb("t2", [P, D])
        cleared, loaded, hi_done, lo_done = (ph.sem(n) for n in ("cleared", "loaded", "hi_done", "lo_done"))
        NL = 2 * (1 + E) + 2 * 5

        def side(ra, kn, part):
            lo = part * (ZC // 2)
            return ra[:, 0:kn * ZC].rearrange("p (k z) -> p k z", z=ZC)[:, :, lo:lo + LZ]

        def clear(pool):
            pool.memset(t1[:], 0.0).then_inc(cleared, 1)
            pool.memset(t2[:], 0.0).then_inc(cleared, 1)
            pool.memset(ra1[:].bitcast(F32), 0.0).then_inc(cleared, 1)
            pool.memset(ra2[:].bitcast(F32), 0.0).then_inc(cleared, 1)

        def load(act):
            for s, r, low in ((s1, "L1_ffn_R1", "L1_ffn_A1"), (s2, "L1_ffn_R2", "L1_ffn_A2")):
                act.dma_start(s[:, :, 0:E], a[r].rearrange("(k p) e -> p k e", p=P)).then_inc(loaded, 16)
                for e in range(E):
                    act.dma_start(s[:, :, E + e * R:E + (e + 1) * R], a[low][e].rearrange("(k p) r -> p k r", p=P)).then_inc(loaded, 16)
            act.wait_ge(cleared, 4)
            for t, w, bias in ((t1, "L1_ffn_B1", "L1_ffn_b1"), (t2, "L1_ffn_B2", "L1_ffn_b2")):
                for row in (0, 32, 64):
                    act.dma_start(t[row:row + ER, :], a[w].rearrange("e r n -> (e r) n")).then_inc(loaded, 16)
                for row in (0, 32):
                    act.dma_start(t[row + ER:row + ER + 1, :], a[bias].rearrange("(o n) -> o n", o=1)).then_inc(loaded, 16)

        def high_parts(act):
            act.wait_ge(loaded, 16 * NL)
            for hi, src in ((side(ra1, KD, 0), s1[:]), (side(ra2, KH, 0), s2[:]), (lb1[:], t1[:]), (lb2[:], t2[:])):
                act.activation(hi, src, ACT.Copy).then_inc(hi_done, 1)

        def low_parts(dve):
            dve.wait_ge(hi_done, 4)
            for ra, kn, src in ((ra1, KD, s1), (ra2, KH, s2)):
                dve.tensor_tensor(side(ra, kn, 1), src[:], side(ra, kn, 0).bitcast(F32), ALU.subtract).then_inc(lo_done, 1)
            for t, lb in ((t1, lb1), (t2, lb2)):
                dve.tensor_tensor(lb[32:64, :], t[32:64, :], lb[32:64, :].bitcast(F32), ALU.subtract).then_inc(lo_done, 1)
            dve.wait_ge(lo_done, 4)

        split_pieces(nc, "lw", pieces, H2, clear, load, high_parts, low_parts)


_INS = ['x', 'ctx_1024', 'fside_1xSxS2_0', 'L0_xattn_Wq', 'L0_xattn_Wk', 'L0_xattn_Wv', 'L0_xattn_Wk_ip', 'L0_xattn_Wv_ip',
        'L0_xattn_Wo', 'L0_xattn_bo', 'L0_ffn_w_gate', 'L0_ffn_w_up', 'L0_ffn_w_down', 'L1_xattn_W1', 'L1_xattn_b1',
        'L1_xattn_W2', 'L1_xattn_b2', 'L1_ffn_W1', 'L1_ffn_b1', 'L1_ffn_A1', 'L1_ffn_B1', 'L1_ffn_R1', 'L1_ffn_W2',
        'L1_ffn_b2', 'L1_ffn_A2', 'L1_ffn_B2', 'L1_ffn_R2']
_OUTS = [((B, S, D), 'float32')]


def kernel(**inputs):
    import numpy as _np
    import concourse.bacc as _bacc
    from concourse import mybir as _mybir
    from concourse.bass_utils import run_bass_kernel_spmd as _run

    nc = _bacc.Bacc("TRN2", target_bir_lowering=False, num_devices=1)
    arrays, args = {}, {}
    for name in _INS:
        a = _np.ascontiguousarray(inputs[name])
        arrays[f"in_{name}_dram"] = a
        args[name] = nc.dram_tensor(f"in_{name}_dram", a.shape, _mybir.dt.from_np(a.dtype), kind="ExternalInput").ap()
    outs = []
    for i, (shape, dtype) in enumerate(_OUTS):
        outs.append(nc.dram_tensor(f"out_{i}_dram", shape, _mybir.dt.from_np(_np.dtype(dtype)), kind="ExternalOutput").ap())
    kernel_program(nc, args, outs[0])
    r = _run(nc, [arrays], core_ids=[0])
    return r.results[0]["out_0_dram"]
```
